# Optimizing a Trainium2 kernel written in Bass

```python
import numpy as np
import jax
import jax.numpy as jnp

def _softmax(x, axis=-1):
    return jax.nn.softmax(x, axis=axis)

def _gelu(x):
    return jax.nn.gelu(x, approximate=True)

def _silu(x):
    return jax.nn.silu(x)

def _sigmoid(x):
    return jax.nn.sigmoid(x)

def _layernorm(x, axis=-1, eps=1e-05):
    m = jnp.mean(x, axis=axis, keepdims=True)
    v = jnp.var(x, axis=axis, keepdims=True)
    return (x - m) / jnp.sqrt(v + eps)

def _scatter_add(tgt, idx, src, axis=0):
    return tgt.at[idx].add(src)

def _segment_sum(src, seg, n):
    return jax.ops.segment_sum(src, seg, n)
kernel_name = 'mk_xattn_seq_d2_seqx_r8_a9d9ee'

def setup_inputs(seed: int=0):
    np.random.seed(seed)
    _w = jnp.asarray

    def _rec_inputs():
        import jax
        import jax.numpy as jnp
        _rk = jax.random.key(seed)
        x = 7.22e-05 + 1 * jax.random.normal(jax.random.fold_in(_rk, 1), (8, 256, 256), jnp.float32)
        _lenS = 256 - jax.random.randint(jax.random.fold_in(_rk, 7), (8,), 0, max(1, 256 // 4) + 1, jnp.int32)
        _lenS2 = 1601 - jax.random.randint(jax.random.fold_in(_rk, 8), (8,), 0, max(1, 1601 // 4) + 1, jnp.int32)
        _ctx_1024P = jax.random.normal(jax.random.fold_in(_rk, 11), (8, 16, 128), jnp.float32)
        _ctx_1024c = jax.random.dirichlet(jax.random.fold_in(_rk, 511), 0.3 * jnp.ones((16,), jnp.float32), (8, 1601))
        _ctx_1024t = jnp.einsum('bsk,bkd->bsd', _ctx_1024c, _ctx_1024P)
        _ctx_1024t = _ctx_1024t * jax.lax.rsqrt(jnp.mean(jnp.square(_ctx_1024t)) + 1e-12) * 0.953939
        ctx_1024 = -0.000514642 + 1.00011 * (_ctx_1024t + 0.3 * jax.random.normal(jax.random.fold_in(_rk, 611), (8, 1601, 128), jnp.float32))
        pos_1xS = jnp.broadcast_to(jnp.arange(256, dtype=jnp.int32), (1, 256))
        _validS = jnp.arange(256)[None, :] < _lenS[:, None]
        _validS2 = jnp.arange(1601)[None, :] < _lenS2[:, None]
        _causal = jnp.tril(jnp.ones((256, 256), dtype=bool))
        mask_BxS_ik0 = jnp.where(jnp.broadcast_to(_validS[:, :], (8, 256)), 0, 1).astype(jnp.int32)
        return (x, ctx_1024, pos_1xS, mask_BxS_ik0)
    x, ctx_1024, pos_1xS, mask_BxS_ik0 = _rec_inputs()

    def _L0_xattn_setup():
        import jax, jax.numpy as jnp
        import numpy as np
        H = 256
        NH = 16
        HD = H // NH
        CH = 128
        CC = 128
        CHD = CC // NH
        I = 688
        B = 2
        L = 256
        LE = 128
        EPS = 1e-06

        def rms_norm(x, w):
            xf = x.astype(jnp.float32)
            var = jnp.mean(xf * xf, axis=-1, keepdims=True)
            return (w * (xf * jax.lax.rsqrt(var + EPS))).astype(x.dtype)

        def expert_mask(tt):
            vm = jnp.zeros(tt.shape, dtype=bool)
            vm = vm.at[:, :-1].set((tt[:, :-1] == 1) & (tt[:, 1:] == 1))
            return vm

        def rotate_half(x):
            d = x.shape[-1] // 2
            return jnp.concatenate([-x[..., d:], x[..., :d]], axis=-1)

        def apply_rotary(q, k, position_ids, seq_len):
            inv = 1.0 / 10000.0 ** (jnp.arange(0, HD, 2, dtype=jnp.float32) / HD)
            t = jnp.arange(seq_len, dtype=jnp.float32)
            freqs = jnp.outer(t, inv)
            emb = jnp.concatenate([freqs, freqs], axis=-1)
            cos = jnp.cos(emb)[position_ids][:, None].astype(q.dtype)
            sin = jnp.sin(emb)[position_ids][:, None].astype(q.dtype)
            return (q * cos + rotate_half(q) * sin, k * cos + rotate_half(k) * sin)

        def sdpa(q, k, v, causal):
            scale = 1.0 / np.sqrt(q.shape[-1])
            scores = jnp.einsum('bhqd,bhkd->bhqk', q * scale, k)
            if causal:
                mask = jnp.tril(jnp.ones((q.shape[-2], k.shape[-2]), dtype=bool))
                scores = jnp.where(mask, scores, jnp.finfo(jnp.float32).min)
            p = jax.nn.softmax(scores.astype(jnp.float32), axis=-1).astype(q.dtype)
            return jnp.einsum('bhqk,bhkd->bhqd', p, v)

        def heads(x, nh, hd):
            b, l, _ = x.shape
            return x.reshape(b, l, nh, hd).transpose(0, 2, 1, 3)
        key = jax.random.key(seed)
        ks = jax.random.split(key, 20)
        s = 0.02
        f32 = jnp.float32
        return {'hidden_states': jax.random.normal(ks[0], (B, L, H), f32), 'encoder_outputs': jax.random.normal(ks[1], (B, LE, CH), f32), 'token_type_ids': jax.random.randint(ks[2], (B, L), 0, 2, jnp.int32), 'position_ids': jnp.arange(L, dtype=jnp.int32)[None, :], 'ln_in_w': jnp.ones((H,), f32), 'ln_post_attn_w': jnp.ones((H,), f32), 'ln_post_cross_w': jnp.ones((H,), f32), 'v_qkv': jax.random.normal(ks[3], (H, 3 * H), f32) * s, 'l_qkv': jax.random.normal(ks[4], (H, 3 * H), f32) * s, 'v_dense': jax.random.normal(ks[5], (H, H), f32) * s, 'l_dense': jax.random.normal(ks[6], (H, H), f32) * s, 'cq_w': jax.random.normal(ks[7], (H, CC), f32) * s, 'ckv_w': jax.random.normal(ks[8], (CH, 2 * CC), f32) * s, 'cdense_w': jax.random.normal(ks[9], (CC, H), f32) * s, 'v_gate': jax.random.normal(ks[10], (H, I), f32) * s, 'v_up': jax.random.normal(ks[11], (H, I), f32) * s, 'v_down': jax.random.normal(ks[12], (I, H), f32) * s, 'l_gate': jax.random.normal(ks[13], (H, I), f32) * s, 'l_up': jax.random.normal(ks[14], (H, I), f32) * s, 'l_down': jax.random.normal(ks[15], (I, H), f32) * s}
    _L0_xattn_all = _L0_xattn_setup()
    _L0_xattn_in = {k: v for k, v in _L0_xattn_all.items() if k in ('ln_in_w', 'ln_post_attn_w', 'ln_post_cross_w', 'v_qkv', 'l_qkv', 'v_dense', 'l_dense', 'cq_w', 'ckv_w', 'cdense_w', 'v_gate', 'v_up', 'v_down', 'l_gate', 'l_up', 'l_down')}
    del _L0_xattn_all

    def _L1_xattn_setup():
        import jax, jax.numpy as jnp
        import numpy as np
        EPS = 1e-06

        def _rmsnorm(x, w):
            var = jnp.mean(jnp.square(x), axis=-1, keepdims=True)
            return x * jax.lax.rsqrt(var + EPS) * w
        key = jax.random.key(seed)
        ks = jax.random.split(key, 6)
        B, N, M = (4, 512, 256)
        d_model, memory_dim = (256, 128)
        hidden_states = jax.random.normal(ks[0], (B, N, d_model), dtype=jnp.float32)
        memory = jax.random.normal(ks[1], (B, M, memory_dim), dtype=jnp.float32)
        W_mem = jax.random.normal(ks[2], (d_model, memory_dim), dtype=jnp.float32) / np.sqrt(memory_dim)
        W_gate = jax.random.normal(ks[3], (d_model, 2 * d_model), dtype=jnp.float32) / np.sqrt(2 * d_model)
        b_gate = jax.random.normal(ks[4], (d_model,), dtype=jnp.float32) * 0.01
        norm_w = jnp.ones((d_model,), dtype=jnp.float32)
        return {'hidden_states': hidden_states, 'memory': memory, 'W_mem': W_mem, 'W_gate': W_gate, 'b_gate': b_gate, 'norm_w': norm_w}
    _L1_xattn_all = _L1_xattn_setup()
    _L1_xattn_in = {k: v for k, v in _L1_xattn_all.items() if k in ('W_mem', 'W_gate', 'b_gate', 'norm_w')}
    del _L1_xattn_all
    return {'x': x, 'ctx_1024': ctx_1024, 'pos_1xS': pos_1xS, 'mask_BxS_ik0': mask_BxS_ik0, 'L0_xattn_ln_in_w': _L0_xattn_in['ln_in_w'], 'L0_xattn_ln_post_attn_w': _L0_xattn_in['ln_post_attn_w'], 'L0_xattn_ln_post_cross_w': _L0_xattn_in['ln_post_cross_w'], 'L0_xattn_v_qkv': _L0_xattn_in['v_qkv'], 'L0_xattn_l_qkv': _L0_xattn_in['l_qkv'], 'L0_xattn_v_dense': _L0_xattn_in['v_dense'], 'L0_xattn_l_dense': _L0_xattn_in['l_dense'], 'L0_xattn_cq_w': _L0_xattn_in['cq_w'], 'L0_xattn_ckv_w': _L0_xattn_in['ckv_w'], 'L0_xattn_cdense_w': _L0_xattn_in['cdense_w'], 'L0_xattn_v_gate': _L0_xattn_in['v_gate'], 'L0_xattn_v_up': _L0_xattn_in['v_up'], 'L0_xattn_v_down': _L0_xattn_in['v_down'], 'L0_xattn_l_gate': _L0_xattn_in['l_gate'], 'L0_xattn_l_up': _L0_xattn_in['l_up'], 'L0_xattn_l_down': _L0_xattn_in['l_down'], 'L1_xattn_W_mem': _L1_xattn_in['W_mem'], 'L1_xattn_W_gate': _L1_xattn_in['W_gate'], 'L1_xattn_b_gate': _L1_xattn_in['b_gate'], 'L1_xattn_norm_w': _L1_xattn_in['norm_w']}

def reference(x, ctx_1024, pos_1xS, mask_BxS_ik0, L0_xattn_ln_in_w, L0_xattn_ln_post_attn_w, L0_xattn_ln_post_cross_w, L0_xattn_v_qkv, L0_xattn_l_qkv, L0_xattn_v_dense, L0_xattn_l_dense, L0_xattn_cq_w, L0_xattn_ckv_w, L0_xattn_cdense_w, L0_xattn_v_gate, L0_xattn_v_up, L0_xattn_v_down, L0_xattn_l_gate, L0_xattn_l_up, L0_xattn_l_down, L1_xattn_W_mem, L1_xattn_W_gate, L1_xattn_b_gate, L1_xattn_norm_w):
    import jax
    import jax.numpy as jnp

    def _L0_xattn_ref(hidden_states, encoder_outputs, token_type_ids, position_ids, ln_in_w, ln_post_attn_w, ln_post_cross_w, v_qkv, l_qkv, v_dense, l_dense, cq_w, ckv_w, cdense_w, v_gate, v_up, v_down, l_gate, l_up, l_down):
        import jax, jax.numpy as jnp
        import numpy as np
        H = 256
        NH = 16
        HD = H // NH
        CH = 128
        CC = 128
        CHD = CC // NH
        I = 688
        B = 2
        L = 256
        LE = 128
        EPS = 1e-06

        def rms_norm(x, w):
            xf = x.astype(jnp.float32)
            var = jnp.mean(xf * xf, axis=-1, keepdims=True)
            return (w * (xf * jax.lax.rsqrt(var + EPS))).astype(x.dtype)

        def expert_mask(tt):
            vm = jnp.zeros(tt.shape, dtype=bool)
            vm = vm.at[:, :-1].set((tt[:, :-1] == 1) & (tt[:, 1:] == 1))
            return vm

        def rotate_half(x):
            d = x.shape[-1] // 2
            return jnp.concatenate([-x[..., d:], x[..., :d]], axis=-1)

        def apply_rotary(q, k, position_ids, seq_len):
            inv = 1.0 / 10000.0 ** (jnp.arange(0, HD, 2, dtype=jnp.float32) / HD)
            t = jnp.arange(seq_len, dtype=jnp.float32)
            freqs = jnp.outer(t, inv)
            emb = jnp.concatenate([freqs, freqs], axis=-1)
            cos = jnp.cos(emb)[position_ids][:, None].astype(q.dtype)
            sin = jnp.sin(emb)[position_ids][:, None].astype(q.dtype)
            return (q * cos + rotate_half(q) * sin, k * cos + rotate_half(k) * sin)

        def sdpa(q, k, v, causal):
            scale = 1.0 / np.sqrt(q.shape[-1])
            scores = jnp.einsum('bhqd,bhkd->bhqk', q * scale, k)
            if causal:
                mask = jnp.tril(jnp.ones((q.shape[-2], k.shape[-2]), dtype=bool))
                scores = jnp.where(mask, scores, jnp.finfo(jnp.float32).min)
            p = jax.nn.softmax(scores.astype(jnp.float32), axis=-1).astype(q.dtype)
            return jnp.einsum('bhqk,bhkd->bhqd', p, v)

        def heads(x, nh, hd):
            b, l, _ = x.shape
            return x.reshape(b, l, nh, hd).transpose(0, 2, 1, 3)
        b, l, _ = hidden_states.shape
        vm = expert_mask(token_type_ids)[..., None]
        residual = hidden_states
        x = rms_norm(hidden_states, ln_in_w)
        mixed = jnp.where(vm, x @ v_qkv, x @ l_qkv)
        q, k, v = jnp.split(mixed, 3, axis=-1)
        q, k, v = (heads(q, NH, HD), heads(k, NH, HD), heads(v, NH, HD))
        q, k = apply_rotary(q, k, position_ids, l)
        ctx = sdpa(q, k, v, causal=True)
        ctx = ctx.transpose(0, 2, 1, 3).reshape(b, l, H)
        attn_out = jnp.where(vm, ctx @ v_dense, ctx @ l_dense)
        hidden_states = residual + attn_out
        ci = rms_norm(hidden_states, ln_post_cross_w)
        cq = heads(ci @ cq_w, NH, CHD)
        ckv = encoder_outputs @ ckv_w
        ck, cv = jnp.split(ckv, 2, axis=-1)
        ck, cv = (heads(ck, NH, CHD), heads(cv, NH, CHD))
        cctx = sdpa(cq, ck, cv, causal=False)
        cctx = cctx.transpose(0, 2, 1, 3).reshape(b, l, CC)
        hidden_states = hidden_states + cctx @ cdense_w
        mi = rms_norm(hidden_states, ln_post_attn_w)
        v_out = jax.nn.silu(mi @ v_gate) * (mi @ v_up) @ v_down
        l_out = jax.nn.silu(mi @ l_gate) * (mi @ l_up) @ l_down
        hidden_states = hidden_states + jnp.where(vm, v_out, l_out)
        return hidden_states

    def _L1_xattn_ref(hidden_states, memory, W_mem, W_gate, b_gate, norm_w):
        import jax, jax.numpy as jnp
        import numpy as np
        EPS = 1e-06

        def _rmsnorm(x, w):
            var = jnp.mean(jnp.square(x), axis=-1, keepdims=True)
            return x * jax.lax.rsqrt(var + EPS) * w
        D = hidden_states.shape[-1]
        memory_proj = jnp.einsum('bme,de->bmd', memory, W_mem)
        scores = jnp.einsum('bnd,bmd->bnm', hidden_states, memory_proj) / jnp.sqrt(jnp.float32(D))
        attn = jax.nn.softmax(scores, axis=-1)
        memory_context = jnp.einsum('bnm,bmd->bnd', attn, memory_proj)
        gate_input = jnp.concatenate([hidden_states, memory_context], axis=-1)
        gate = jax.nn.sigmoid(jnp.einsum('bnf,df->bnd', gate_input, W_gate) + b_gate)
        fused = hidden_states + gate * memory_context
        return _rmsnorm(fused, norm_w)
    x = _L0_xattn_ref(x, ctx_1024, mask_BxS_ik0, pos_1xS, L0_xattn_ln_in_w, L0_xattn_ln_post_attn_w, L0_xattn_ln_post_cross_w, L0_xattn_v_qkv, L0_xattn_l_qkv, L0_xattn_v_dense, L0_xattn_l_dense, L0_xattn_cq_w, L0_xattn_ckv_w, L0_xattn_cdense_w, L0_xattn_v_gate, L0_xattn_v_up, L0_xattn_v_down, L0_xattn_l_gate, L0_xattn_l_up, L0_xattn_l_down)
    x = _L1_xattn_ref(x, ctx_1024, L1_xattn_W_mem, L1_xattn_W_gate, L1_xattn_b_gate, L1_xattn_norm_w)
    return x

_drawn_inputs = setup_inputs


def setup_inputs(seed=0):
    import zlib

    import numpy as np

    out = dict(_drawn_inputs(seed))
    spreads = {'L0_xattn_ln_in_w': (1.0, 0.6),
     'L0_xattn_ln_post_attn_w': (1.0, 0.6),
     'L0_xattn_ln_post_cross_w': (1.0, 0.6),
     'L1_xattn_norm_w': (1.0, 0.2)}
    factors = {'L0_xattn_v_qkv': 8.0,
     'L0_xattn_l_qkv': 3.588,
     'L0_xattn_v_dense': 8.0,
     'L0_xattn_l_dense': 3.66,
     'L0_xattn_cq_w': 64.0,
     'L0_xattn_v_gate': 5.334,
     'L0_xattn_v_up': 5.25,
     'L0_xattn_v_down': 5.265,
     'L1_xattn_b_gate': 64.0,
     'L0_xattn_ckv_w': 3.067,
     'L0_xattn_cdense_w': 3.096}
    for name, (base, spread) in spreads.items():
        noise = np.random.default_rng([zlib.crc32(name.encode()), seed]).standard_normal(out[name].shape)
        drawn = base * np.exp(spread * noise) if base else spread * noise
        out[name] = jnp.asarray(drawn.astype(out[name].dtype))
    for name, factor in factors.items():
        out[name] = (out[name] * factor).astype(out[name].dtype)
    return out
```

```python
from collections import namedtuple
from contextlib import ExitStack

import numpy as np

import concourse.bass as bass
from concourse import mybir

ALU = mybir.AluOpType
ACT = mybir.ActivationFunctionType
F32 = mybir.dt.float32
F32R = mybir.dt.float32r
BF16 = mybir.dt.bfloat16
I32 = mybir.dt.int32
AX_X = mybir.AxisListType.X

P = 128
B, L, H = 8, 256, 256
LE, CH = 1601, 128
NH = 16
HD, CHD = H // NH, CH // NH
FF = 688
EPS = 1e-6
T = L // P
C = H // P
KT = (LE + P - 1) // P
LAST = LE - (KT - 1) * P
NJ = (KT + 3) // 4
EVEN = LAST + LAST % 2
MASKED = -(2.0 ** 120)

ID0 = 0
MS0 = ID0 + P
CS0 = MS0 + NH
PO0 = CS0 + T * 2 * HD
EC0 = PO0 + T
MC0 = EC0 + 4 * 32
CM0 = MC0 + 4
NCONST = CM0 + 2 * P


def chunk_tiles(j):
    return range(4 * j, min(4 * j + 4, KT))


def tile_rows(kt):
    return P if kt < KT - 1 else LAST


def chunk_cols(j):
    return sum(tile_rows(kt) for kt in chunk_tiles(j))


def constants():
    c = np.zeros((P, NCONST), np.float32)
    c[:, ID0:ID0 + P] = np.eye(P, dtype=np.float32)
    for h in range(NH):
        c[96 + h, MS0 + h] = c[112 + h, MS0 + h] = 1.0
    inv = np.float32(1.0) / np.power(np.float32(10000.0), np.arange(0, HD, 2, dtype=np.float32) / np.float32(HD))
    ang = np.arange(L, dtype=np.float32)[:, None] * inv.astype(np.float32)[None, :]
    cos, sin = np.cos(ang).astype(np.float32), np.sin(ang).astype(np.float32)
    tab = np.concatenate([cos, cos, -sin, sin], axis=1)
    for t in range(T):
        c[:, CS0 + t * 32:CS0 + t * 32 + 32] = tab[t * P:(t + 1) * P]
        c[:, PO0 + t] = np.arange(t * P, (t + 1) * P)
    for parity in range(2):
        for kg in range(4):
            for e in range(2):
                for d in range(CHD):
                    col = 16 * parity + CHD * e + d
                    c[32 * kg + 9 * e + d, EC0 + 32 * parity + col] = 1.0
                    c[32 * kg + 9 * e + 8, EC0 + 64 + 32 * parity + col] = 1.0
    for j in range(4):
        c[:, MC0 + j] = (np.arange(P) % 32) // CHD == j
    k = np.arange(P)
    c[:, CM0:CM0 + P] = np.where(k[None, :] > k[:, None], MASKED, 0.0)
    c[:, CM0 + P:CM0 + 2 * P] = np.where(k[:, None] > k[None, :], MASKED, 0.0)
    return c


def allocator(nc, ctx):
    def sb(name, shape, dt=F32):
        return ctx.enter_context(nc.sbuf_tensor(name, shape, dt))

    def ps(name, shape, dt=F32):
        return ctx.enter_context(nc.psum_tensor(name, shape, dt))

    return sb, ps


def semaphores(nc, ctx, *names):
    return namedtuple("Semaphores", names)(*[ctx.enter_context(nc.semaphore(name)) for name in names])


def split_hi(nc, hi, src):
    return nc.vector.tensor_copy(hi, src)


def split_lo(nc, lo, src, hi):
    return nc.vector.tensor_tensor(lo, src, hi.bitcast(F32), ALU.subtract)


def three(hi_lo_pairs):
    (sh, sl), (mh, ml) = hi_lo_pairs
    return [(sh, mh), (sh, ml), (sl, mh)]



SLOTS1 = 24
S1_ITEMS = [(0, 4 * i, 4) for i in range(4)] + [(1, 2 * i, 2) for i in range(8)]


def self_attention(nc, g, io):
    with ExitStack() as ctx:
        sb, ps = allocator(nc, ctx)
        ident16 = sb("ident16", [P, P], BF16)
        causal = sb("causal", [P, 2 * P], BF16)
        work = ps("work1", [P, 3, 512])
        st = ps("st1", [P, 2, 2, 512])
        nd = ps("nd1", [P, 2, 256])
        stage = sb("stage1", [P, C, 3 * H])
        wq_hi = sb("wqkv_hi", [P, 2, C, 3 * H], F32R)
        wq_lo = sb("wqkv_lo", [P, 2, C, 3 * H], F32R)
        wd_hi = sb("wdense_hi", [P, C, 2 * H], F32R)
        wd_lo = sb("wdense_lo", [P, C, 2 * H], F32R)
        lnw = sb("ln_in_w", [P, C])
        posr = sb("positions", [P, L], I32)
        posf = sb("positions_f", [P, L])
        pick = sb("position_picks", [P, T, L])
        cs = sb("cos_sin", [P, T, 2 * HD])
        vones = sb("ones_by_parity", [P, 2, 32])
        sq = sb("squares1", [P, T, H])
        ssq = sb("sum_squares1", [P, T])
        var = sb("variance1", [P, T])
        rstd = sb("rstd1", [P, T])
        rex = sb("rstd_by_expert1", [P, 2, T])
        xe = sb("x_by_expert1", [P, 2, T, H])
        xh = sb("xt_hi1", [P, 2, C, L], F32R)
        xl = sb("xt_lo1", [P, 2, C, L], F32R)
        rc = sb("rot_cos", [P, 2 * H])
        rs = sb("rot_sin", [P, 2 * H])
        qk = sb("qk_rotated", [P, T, 2 * H])
        qkh = sb("qkt_hi", [P, 4, L], F32R)
        qkl = sb("qkt_lo", [P, 4, L], F32R)
        vs = sb("v_self", [P, T, NH // 2, 64])
        qm = sb("q_rows1", [P, NH, L], F32R)
        ks = sb("k_rows1", [P, NH // 2, L], F32R)
        mx = sb("max1", [P, T, NH])
        mn = sb("neg_max1", [P, T, P], F32R)
        pr = sb("probs1", [P, 2, 8, 384])
        rden = sb("rden1", [P, 256])
        cx = sb("ctx1", [P, C, L])
        cxh = sb("ctx_hi1", [P, C, L], F32R)
        cxl = sb("ctx_lo1", [P, C, L], F32R)
        m = semaphores(nc, ctx, "w1_loaded", "w1_staged", "w1_hi", "w1_lo", "in_loaded", "table_ready", "pos_f", "picks", "cs_psum",
              "v_zero", "v_ones", "rows_init", "x_loaded0", "x_loaded1", "work_ready", "work_free", "ssq_ready", "var_ready", "rstd_ready",
              "rex_ready", "xe_ready", "xh_ready", "xl_ready", "rot_parts", "rot_ready", "qkh_ready", "qkl_ready",
              "v_ready", "rows_ready", "mx_ready", "mh_ready", "ml_ready", "qm_max", "st_ready", "exp_done",
              "nd_ready", "rden_ready", "ctx_ready", "cxh_ready", "cxl_ready", "res_v", "res_done", "vm_a", "vm_b",
              "rows_free")
        ident = g.const[:, ID0:ID0 + P]
        block = ctx.enter_context(nc.Block())

        @block.sync
        def _(sp):
            sp.dma_start(g.const[:, :], io["const"]).then_inc(m.in_loaded, 16)
            sp.dma_start(posr[:, :], io["pos_1xS"].broadcast_to([P, L])).then_inc(m.in_loaded, 16)
            sp.dma_start(lnw[:, :], io["L0_xattn_ln_in_w"].rearrange("(c p) -> p c", p=P), allow_slow_non_contiguous=True).then_inc(m.in_loaded, 16)
            tt = io["mask_BxS_ik0"].rearrange("b (t p) -> p b t", p=P)
            sp.dma_start(g.tok[:, :].rearrange("p (b t) -> p b t", t=T), tt, allow_slow_non_contiguous=True).then_inc(m.in_loaded, 16)
            sp.wait_ge(m.vm_a, 1)
            nxt = io["mask_BxS_ik0"][:, 1:L]
            dst = g.tok_next[:, :].rearrange("p (b t) -> p b t", t=T)
            sp.dma_start(dst[:, :, 0], nxt[:, 0:P].rearrange("b p -> p b"), allow_slow_non_contiguous=True).then_inc(m.in_loaded, 16)
            sp.dma_start(dst[0:P - 1, :, 1], nxt[:, P:L - 1].rearrange("b p -> p b"), allow_slow_non_contiguous=True).then_inc(m.in_loaded, 16)
            for i, (name, cols) in enumerate((("L0_xattn_v_qkv", 3 * H), ("L0_xattn_l_qkv", 3 * H))):
                if i:
                    sp.wait_ge(m.w1_lo, i)
                sp.dma_start(stage[:, :, :], io[name].rearrange("(c p) n -> p c n", p=P)).then_inc(m.w1_loaded, 16)
            sp.wait_ge(m.w1_lo, 2)
            sp.dma_start(stage[:, :, 0:H], io["L0_xattn_v_dense"].rearrange("(c p) n -> p c n", p=P)).then_inc(m.w1_loaded, 16)
            sp.dma_start(stage[:, :, H:2 * H], io["L0_xattn_l_dense"].rearrange("(c p) n -> p c n", p=P)).then_inc(m.w1_loaded, 16)
            with sp.Fori(0, B) as b:
                sp.wait_ge(m.qkl_ready, 2 * b + 2)
                sp.wait_ge(m.rows_free, 2 * b + 2)
                qv = qm[:, :, :].rearrange("p (a r e) n -> p a r e n", a=2, e=2).bitcast(F32)
                kv = ks[:, :, :].rearrange("p (a r) n -> p a r n", a=2).bitcast(F32)
                qh32, ql32 = qkh[:, :, :].bitcast(F32), qkl[:, :, :].bitcast(F32)
                for blk, part in enumerate((qh32, qh32, ql32)):
                    for r in range(4):
                        for e in range(2):
                            lo = 32 * blk + 16 * e
                            src = 32 * r + 16 * e
                            sp.dma_start(qv[lo:lo + 16, :, r, e, :], part[src:src + 16, 0:2, :]).then_inc(m.rows_ready, 16)
                for blk, part in enumerate((qh32, ql32, qh32)):
                    for r in range(4):
                        sp.dma_start(kv[32 * blk:32 * blk + 32, :, r, :], part[32 * r:32 * r + 32, 2:4, :]).then_inc(m.rows_ready, 16)

        @block.gpsimd
        def _(pool):
            pool.dma_start(g.x[:, :, :], io["x"].rearrange("b (t p) n -> p (b t) n", p=P)).then_inc(m.x_loaded0, 16)
            nc.gpsimd.memset(vs[:, :, :, :], 0.0).then_inc(m.v_zero, 1)
            nc.gpsimd.memset(vones[:, :, :], 0.0).then_inc(m.v_zero, 1)
            pool.wait_ge(m.v_zero, 2)
            nc.gpsimd.memset(vones[:, 0, 0:16], 1.0).then_inc(m.v_ones, 1)
            nc.gpsimd.memset(vones[:, 1, 16:32], 1.0).then_inc(m.v_ones, 1)
            pool.wait_ge(m.vm_a, 5)
            with pool.Fori(0, B) as b:
                pool.wait_ge(m.ssq_ready, 2 * b + 2)
                nc.gpsimd.tensor_tensor(var[:, :], ssq[:, :], g.eps[:, :], ALU.add).then_inc(m.var_ready, 1)
                pool.wait_ge(m.var_ready, b + 1)
                nc.gpsimd.tensor_tensor(rstd[:, :], var[:, :], g.minus_half[:, :], ALU.pow).then_inc(m.rstd_ready, 1)

        @block.scalar
        def _(act):
            act.wait_ge(m.x_loaded0, 16)
            with act.Fori(0, B) as b:
                for t in range(T):
                    nc.scalar.activation(sq[:, t, :], g.x[:, 2 * b + t, :], ACT.Square, scale=H ** -0.5,
                                         accum_out=ssq[:, t:t + 1]).then_inc(m.ssq_ready, 1)
                for e in range(2):
                    act.wait_ge(m.work_ready, SLOTS1 * b + e + 1)
                    for c in range(C):
                        nc.scalar.activation(xh[:, e, c, :], work[:, e, c * L:(c + 1) * L], ACT.Copy,
                                             scale=lnw[:, c:c + 1]).then_inc(m.xh_ready, 1)
                for i in range(2):
                    act.wait_ge(m.work_ready, SLOTS1 * b + 7 + i)
                    nc.scalar.activation(qkh[:, 2 * i:2 * i + 2, :], work[:, i, :].rearrange("p (c n) -> p c n", c=2),
                                         ACT.Copy).then_inc(m.qkh_ready, 1)
                for i in range(NH // 2):
                    act.wait_ge(m.st_ready, 8 * b + i + 1)
                    if i % 4 == 0:
                        act.wait_ge(m.nd_ready, 2 * b + i // 4 + 1)
                    nc.scalar.activation(pr[:, i // 4, 2 * (i % 4):2 * (i % 4) + 2, :], st[:, i % 2, :, 0:384],
                                         ACT.Exp, scale=HD ** -0.5).then_inc(m.exp_done, 1)
                    if i == 5:
                        act.wait_ge(m.ctx_ready, 2 * b + 1)
                        nc.scalar.activation(cxh[:, 0, :], cx[:, 0, :], ACT.Copy).then_inc(m.cxh_ready, 1)
                act.wait_ge(m.ctx_ready, 2 * b + 2)
                nc.scalar.activation(cxh[:, 1, :], cx[:, 1, :], ACT.Copy).then_inc(m.cxh_ready, 1)

        @block.vector
        def _(dve):
            nc.vector.memset(g.tok_next[:, :], 0).then_inc(m.vm_a, 1)
            nc.vector.memset(g.minus_half[:, :], -0.5).then_inc(m.vm_a, 1)
            nc.vector.memset(g.eps[:, :], EPS).then_inc(m.vm_a, 1)
            nc.vector.memset(g.zero[:, :], 0.0).then_inc(m.vm_a, 1)
            nc.vector.memset(g.one[:, :], 1.0).then_inc(m.vm_a, 1)
            dve.wait_ge(m.vm_a, 5)
            nc.vector.tensor_copy(qm[:, :, :], g.zero[:, 0:1].unsqueeze(2).broadcast_to([P, NH, L])).then_inc(m.rows_init, 1)
            nc.vector.tensor_copy(ks[96:128, :, :], g.one[96:128, 0:1].unsqueeze(2).broadcast_to([32, NH // 2, L])).then_inc(m.rows_init, 1)
            nc.vector.tensor_copy(mn[:, :, :], g.zero[:, 0:1].unsqueeze(2).broadcast_to([P, T, P])).then_inc(m.rows_init, 1)
            dve.wait_ge(m.in_loaded, 96)
            nc.vector.tensor_copy(causal[:, :], g.const[:, CM0:CM0 + 2 * P]).then_inc(m.table_ready, 1)
            nc.vector.tensor_copy(ident16[:, :], ident).then_inc(m.table_ready, 1)
            nc.vector.tensor_scalar(g.nvm[:, :], g.tok[:, :], 1.0, None, ALU.is_equal).then_inc(m.vm_b, 1)
            dve.wait_ge(m.vm_b, 1)
            nc.vector.scalar_tensor_tensor(g.vm[:, :], g.tok_next[:, :], 1.0, g.nvm[:, :], ALU.is_equal,
                                           ALU.mult).then_inc(m.vm_b, 1)
            dve.wait_ge(m.vm_b, 2)
            nc.vector.tensor_scalar(g.nvm[:, :], g.vm[:, :], -1.0, 1.0, ALU.mult, ALU.add).then_inc(m.vm_b, 1)
            nc.vector.tensor_copy(posf[:, :], posr[:, :]).then_inc(m.pos_f, 1)
            dve.wait_ge(m.pos_f, 1)
            for t in range(T):
                nc.vector.tensor_scalar(pick[:, t, :], posf[:, :], g.const[:, PO0 + t:PO0 + t + 1], None,
                                        ALU.is_equal).then_inc(m.picks, 1)
            dve.wait_ge(m.cs_psum, 1)
            nc.vector.tensor_copy(cs[:, :, :], nd[:, 0, 0:64].rearrange("p (t n) -> p t n", t=T)).then_inc(m.table_ready, 1)
            for i in range(2):
                dve.wait_ge(m.w1_loaded, 16 * i + 16)
                split_hi(nc, wq_hi[:, i, :, :], stage[:, :, :]).then_inc(m.w1_hi, 1)
                dve.wait_ge(m.w1_hi, i + 1)
                split_lo(nc, wq_lo[:, i, :, :], stage[:, :, :], wq_hi[:, i, :, :]).then_inc(m.w1_lo, 1)
            dve.wait_ge(m.w1_loaded, 64)
            split_hi(nc, wd_hi[:, :, :], stage[:, :, 0:2 * H]).then_inc(m.w1_hi, 1)
            dve.wait_ge(m.w1_hi, 3)
            split_lo(nc, wd_lo[:, :, :], stage[:, :, 0:2 * H], wd_hi[:, :, :]).then_inc(m.w1_lo, 1)
            dve.wait_ge(m.table_ready, 3)
            dve.wait_ge(m.vm_b, 3)
            dve.wait_ge(m.v_zero, 2)
            dve.wait_ge(m.rows_init, 3)
            dve.sem_inc(m.work_free, 3)
            with dve.Fori(0, B) as b:
                dve.wait_ge(m.rstd_ready, b + 1)
                nc.vector.tensor_tensor(rex[:, 0, :], rstd[:, :], g.vm[:, bass.ds(2 * b, 2)], ALU.mult).then_inc(m.rex_ready, 1)
                nc.vector.tensor_tensor(rex[:, 1, :], rstd[:, :], g.nvm[:, bass.ds(2 * b, 2)], ALU.mult).then_inc(m.rex_ready, 1)
                dve.wait_ge(m.rex_ready, 2 * b + 2)
                for e in range(2):
                    for t in range(T):
                        nc.vector.tensor_scalar(xe[:, e, t, :], g.x[:, 2 * b + t, :], rex[:, e, t:t + 1], None,
                                                ALU.mult).then_inc(m.xe_ready, 1)
                for e in range(2):
                    dve.wait_ge(m.xh_ready, 4 * b + 2 * e + 2)
                    for c in range(C):
                        ins = nc.vector.scalar_tensor_tensor(xl[:, e, c, :], work[:, e, c * L:(c + 1) * L], lnw[:, c:c + 1],
                                                             xh[:, e, c, :].bitcast(F32), ALU.mult, ALU.subtract)
                        ins.then_inc(m.xl_ready if c == 0 else m.work_free, 1)
                for t in range(T):
                    dve.wait_ge(m.work_ready, SLOTS1 * b + 3 + t)
                    src = work[:, (2 + t) % 3, :].rearrange("p (h d) -> p h d", d=HD)
                    if t:
                        dve.wait_ge(m.rot_ready, 2 * b + t)
                    half = HD // 2
                    rcv = rc[:, :].rearrange("p (h d) -> p h d", d=HD)
                    rsv = rs[:, :].rearrange("p (h d) -> p h d", d=HD)
                    cosb = cs[:, t:t + 1, 0:HD].broadcast_to([P, 2 * NH, HD])
                    sina = cs[:, t:t + 1, HD:HD + half].broadcast_to([P, 2 * NH, half])
                    sinb = cs[:, t:t + 1, HD + half:2 * HD].broadcast_to([P, 2 * NH, half])
                    nc.vector.tensor_tensor(rcv, src, cosb, ALU.mult).then_inc(m.rot_parts, 1)
                    nc.vector.tensor_tensor(rsv[:, :, 0:half], src[:, :, half:HD], sina, ALU.mult).then_inc(m.rot_parts, 1)
                    nc.vector.tensor_tensor(rsv[:, :, half:HD], src[:, :, 0:half], sinb, ALU.mult).then_inc(m.work_free, 1)
                    dve.wait_ge(m.rot_parts, 4 * b + 2 * t + 2)
                    dve.wait_ge(m.work_free, SLOTS1 * b + 3 + t + 3)
                    nc.vector.tensor_tensor(qk[:, t, :], rc[:, :], rs[:, :], ALU.add).then_inc(m.rot_ready, 1)
                for t in range(T):
                    dve.wait_ge(m.work_ready, SLOTS1 * b + 5 + t)
                    src = work[:, (4 + t) % 3, 0:H].rearrange("p (q e d) -> p q e d", e=2, d=HD)
                    for e in range(2):
                        ins = nc.vector.tensor_copy(vs[:, t, :, 48 * e:48 * e + HD], src[:, :, e, :])
                        ins.then_inc(m.v_ready if e == 0 else m.work_free, 1)
                for i in range(2):
                    dve.wait_ge(m.qkh_ready, 2 * b + i + 1)
                    nc.vector.tensor_tensor(qkl[:, 2 * i:2 * i + 2, :], work[:, i, :].rearrange("p (c n) -> p c n", c=2),
                                            qkh[:, 2 * i:2 * i + 2, :].bitcast(F32), ALU.subtract).then_inc(m.qkl_ready, 1)
                    dve.wait_ge(m.qkl_ready, 2 * b + i + 1)
                    dve.sem_inc(m.work_free, 1)
                for i, (t, h0, n) in enumerate(S1_ITEMS):
                    dve.wait_ge(m.work_ready, SLOTS1 * b + 9 + i)
                    nc.vector.reduce_max(mx[:, t, h0:h0 + n], work[:, (8 + i) % 3, :].rearrange("p (h k) -> p h k", h=n),
                                         AX_X).then_inc(m.work_free, 1)
                dve.wait_ge(m.work_free, SLOTS1 * b + 20 + 3)
                nc.vector.tensor_scalar(mn[:, :, 96:112], mx[:, :, :], -1.0, None, ALU.mult).then_inc(m.mh_ready, 1)
                dve.wait_ge(m.mh_ready, b + 1)
                nc.vector.scalar_tensor_tensor(mn[:, :, 112:128], mx[:, :, :], -1.0, mn[:, :, 96:112].bitcast(F32),
                                               ALU.mult, ALU.subtract).then_inc(m.ml_ready, 1)
                for t in range(T):
                    dve.wait_ge(m.work_ready, SLOTS1 * b + 21 + t)
                    nc.vector.tensor_tensor(qm[96:128, :, t * P:(t + 1) * P],
                                            work[96:128, (20 + t) % 3:(20 + t) % 3 + 1, 0:P].broadcast_to([32, NH, P]),
                                            g.const[96:128, MS0:MS0 + NH].unsqueeze(2).broadcast_to([32, NH, P]),
                                            ALU.mult).then_inc(m.work_free, 1)
                for c in range(C):
                    dve.wait_ge(m.nd_ready, 2 * b + c + 1 + 2)
                    nc.vector.reciprocal(rden[:, :], nd[:, 1, :]).then_inc(m.rden_ready, 1)
                    dve.wait_ge(m.rden_ready, 2 * b + c + 1)
                    nc.vector.tensor_tensor(cx[:, c, :], nd[:, 0, :], rden[:, :], ALU.mult).then_inc(m.ctx_ready, 1)
                    dve.wait_ge(m.cxh_ready, 2 * b + c + 1)
                    split_lo(nc, cxl[:, c, :], cx[:, c, :], cxh[:, c, :]).then_inc(m.cxl_ready, 1)
                for t in range(T):
                    dve.wait_ge(m.work_ready, SLOTS1 * b + 23 + t)
                    src = work[:, (22 + t) % 3, :]
                    xt = g.x[:, 2 * b + t, :]
                    nc.vector.scalar_tensor_tensor(xt, src[:, 0:H], g.vm[:, bass.ds(2 * b + t, 1)], xt, ALU.mult,
                                                   ALU.add).then_inc(m.res_v, 1)
                    dve.wait_ge(m.res_v, 2 * b + t + 1)
                    nc.vector.scalar_tensor_tensor(xt, src[:, H:2 * H], g.nvm[:, bass.ds(2 * b + t, 1)], xt, ALU.mult,
                                                   ALU.add).then_inc(m.work_free, 1)

        @block.tensor
        def _(pe):
            pe.sem_inc(m.nd_ready, 2)
            pe.sem_inc(m.rows_free, 2)
            pe.wait_ge(m.picks, 2)
            for t in range(T):
                for u in range(T):
                    last = nc.tensor.matmul(nd[:, 0, 32 * t:32 * t + 32], pick[:, u, t * P:(t + 1) * P],
                                            g.const[:, CS0 + 32 * u:CS0 + 32 * u + 32], start=(u == 0), stop=(u == T - 1))
            last.then_inc(m.cs_psum, 1)
            pe.wait_ge(m.w1_lo, 3)
            pe.wait_ge(m.table_ready, 3)
            pe.wait_ge(m.v_ones, 2)
            pe.wait_ge(m.rows_init, 3)
            with pe.Fori(0, B) as b:
                def take(n):
                    pe.wait_ge(m.work_free, SLOTS1 * b + n + 1)
                    return work[:, n % 3, :]

                for e in range(2):
                    pe.wait_ge(m.xe_ready, 4 * b + 2 * e + 2)
                    dst = take(e)
                    for t in range(T):
                        for c in range(C):
                            last = nc.tensor.transpose(dst[:, c * L + t * P:c * L + t * P + P],
                                                       xe[:, e, t, c * P:(c + 1) * P], ident)
                    last.then_inc(m.work_ready, 1)
                pe.wait_ge(m.xl_ready, 2 * b + 2)
                pe.wait_ge(m.work_free, SLOTS1 * b + 5)

                def project(n, t, a, w):
                    dst = take(n)
                    terms = []
                    for e in range(2):
                        for c in range(C):
                            terms += three(((xh[:, e, c, t * P:(t + 1) * P], xl[:, e, c, t * P:(t + 1) * P]),
                                            (wq_hi[:, e, c, a:a + w], wq_lo[:, e, c, a:a + w])))
                    for i, (s, mv) in enumerate(terms):
                        last = nc.tensor.matmul(dst[:, 0:w], s, mv, start=(i == 0), stop=(i == len(terms) - 1))
                    last.then_inc(m.work_ready, 1)

                for t in range(T):
                    project(2 + t, t, 0, 2 * H)
                for t in range(T):
                    project(4 + t, t, 2 * H, H)
                pe.wait_ge(m.rot_ready, 2 * b + 2)
                for i in range(2):
                    dst = take(6 + i)
                    for t in range(T):
                        for c in range(2):
                            last = nc.tensor.transpose(dst[:, c * L + t * P:c * L + t * P + P],
                                                       qk[:, t, (2 * i + c) * P:(2 * i + c + 1) * P], ident)
                    last.then_inc(m.work_ready, 1)
                pe.wait_ge(m.rows_ready, 36 * 16 * b + 36 * 16)
                for i, (t, h0, n) in enumerate(S1_ITEMS):
                    dst = take(8 + i)
                    w = (t + 1) * P
                    for k in range(n):
                        h = h0 + k
                        nc.tensor.matmul(dst[:, k * w:(k + 1) * w], qm[0:96, h, t * P:(t + 1) * P],
                                         ks[0:96, h // 2, 0:w], start=True, stop=False, skip_group_check=True)
                        last = nc.tensor.matmul(dst[:, (k + 1) * w - P:(k + 1) * w], ident16[:, :], causal[:, 0:P],
                                                start=False, stop=True, skip_group_check=True)
                    last.then_inc(m.work_ready, 1)
                pe.wait_ge(m.ml_ready, b + 1)
                for t in range(T):
                    dst = take(20 + t)
                    nc.tensor.transpose(dst[:, 0:P], mn[:, t, :].bitcast(F32), ident).then_inc(m.work_ready, 1)
                pe.wait_ge(m.work_free, SLOTS1 * b + 22 + 3)
                pe.wait_ge(m.v_ready, 2 * b + 2)

                def scores(i):
                    if i >= 2:
                        pe.wait_ge(m.exp_done, 8 * b + i - 1)
                    for k in range(2):
                        h = 2 * i + k
                        for kt in range(2):
                            a = 256 * kt
                            nc.tensor.matmul(st[:, i % 2, k, a:a + 256 - 128 * kt], ks[:, h // 2, kt * P:(kt + 1) * P],
                                             qm[:, h, kt * P:L], start=True, stop=False, skip_group_check=True)
                            last = nc.tensor.matmul(st[:, i % 2, k, a:a + P], ident16[:, :], causal[:, P:2 * P],
                                                    start=False, stop=True, skip_group_check=True)
                    last.then_inc(m.st_ready, 1)

                def values(c):
                    pe.wait_ge(m.exp_done, 8 * b + 4 * c + 4)
                    if c:
                        pe.wait_ge(m.ctx_ready, 2 * b + c)
                    for what in range(2):
                        for kt in range(2):
                            for e in range(2):
                                for q in range(4):
                                    lhs = vs[:, kt, 4 * c + q, 32 * e:32 * e + 32] if what == 0 else vones[:, e, :]
                                    rhs = pr[:, c, 2 * q + e, 256 * kt:384 if kt else 256]
                                    last = nc.tensor.matmul(nd[32 * q:32 * q + 32, what, kt * P:L], lhs, rhs,
                                                            start=(kt == 0 and e == 0), stop=(kt == 1 and e == 1),
                                                            tile_position=(0, 32 * q), skip_group_check=True)
                    last.then_inc(m.nd_ready, 1)

                for i in range(5):
                    scores(i)
                values(0)
                for i in range(5, 8):
                    scores(i)
                pe.wait_ge(m.st_ready, 8 * b + 8)
                pe.sem_inc(m.rows_free, 2)
                values(1)
                pe.wait_ge(m.cxl_ready, 2 * b + 2)
                for t in range(T):
                    dst = take(22 + t)
                    terms = []
                    for c in range(C):
                        terms += three(((cxh[:, c, t * P:(t + 1) * P], cxl[:, c, t * P:(t + 1) * P]),
                                        (wd_hi[:, c, :], wd_lo[:, c, :])))
                    for i, (s, mv) in enumerate(terms):
                        last = nc.tensor.matmul(dst[:, :], s, mv, start=(i == 0), stop=(i == len(terms) - 1))
                    last.then_inc(m.work_ready, 1)



QUADS = NH // 4
ITEMS = 26
CHUNKS = 13
FRONT = 14
QC = NJ - 1


def plan(front, maxima, probs):
    out, slots = [], 0

    def put(what, k, slot=True):
        nonlocal slots
        out.append((what, k, slots if slot else None))
        slots += slot

    steps = QUADS * CHUNKS
    items = QUADS * ITEMS
    hold = 8 if probs else 0
    done = fronts = 0
    for s in range(steps):
        if probs:
            put("scores", s, False)
        if maxima:
            while done < (s + 1) * (items - hold) // steps:
                put("max", done)
                done += 1
                if done % ITEMS == 0 and done < items:
                    put("maxrow", done // ITEMS - 1, False)
                if done % ITEMS == 6 and done > ITEMS:
                    put("maxcol", done // ITEMS - 1)
        if front:
            while fronts < FRONT and s >= 3 * fronts + 3:
                put("front", fronts)
                fronts += 1
        if probs and s >= 2:
            put("values", s - 2, False)
    if probs:
        put("values", steps - 2, False)
        put("values", steps - 1, False)
    rest = items - done if maxima else 0

    def some(n):
        nonlocal done, rest
        for _ in range(min(n, rest)):
            put("max", done)
            done += 1
            rest -= 1

    some(2)
    if probs:
        put("sums", 0)
        put("sums", 1)
    some(3)
    if probs:
        put("out", 0)
        put("out", 1)
    some(rest)
    if maxima:
        put("maxrow", QUADS - 1, False)
        put("maxcol", QUADS - 1)
    return out, slots


PLAN = {k: plan(*k) for k in ((1, 0, 0), (1, 1, 0), (1, 1, 1), (0, 1, 1), (0, 0, 1))}


Batch = namedtuple("Batch", "number parity before")


def iterations(eng, one):
    first = 0
    per = PLAN[1, 1, 1][1]
    assert per % 3 == 0

    def run(pair, s, parts, slot0, bank0):
        one(Batch(2 * pair + (s + 2), s, pair + 1), Batch(2 * pair + (s + 1), 1 - s, pair + s), Batch(2 * pair + s, s, pair),
            parts, slot0, bank0)

    for s, parts in enumerate(((1, 0, 0), (1, 1, 0))):
        run(-1, s, parts, first, first % 3)
        first += PLAN[parts][1]
    with eng.Fori(0, B // 2 - 1) as pair:
        for s in range(2):
            run(pair, s, (1, 1, 1), (2 * per) * pair + (first + per * s), first % 3)
    first += per * (B - 2)
    for s, parts in enumerate(((0, 1, 1), (0, 0, 1))):
        run(B // 2 - 1, s, parts, first, first % 3)
        first += PLAN[parts][1]


def cross_attention(nc, g, io):
    with ExitStack() as ctx:
        sb, ps = allocator(nc, ctx)
        work = ps("work2", [P, 3, 512])
        st = ps("st2", [P, 2, 4, 256])
        acc = ps("acc2", [P, 2, 256])
        wq_hi = sb("wcq_hi", [P, C, CH], F32R)
        wq_lo = sb("wcq_lo", [P, C, CH], F32R)
        wkv_hi = sb("wckv_hi", [P, 2 * CH], F32R)
        wkv_lo = sb("wckv_lo", [P, 2 * CH], F32R)
        wd_hi = sb("wcdense_hi", [P, H], F32R)
        wd_lo = sb("wcdense_lo", [P, H], F32R)
        lnw = sb("ln_cross_w", [P, C])
        ssq = sb("mean_squares2", [P, T])
        var = sb("variance2", [P, T])
        rstd = sb("rstd2", [P, T])
        xs = sb("x_scaled2", [P, T, H])
        xh = sb("xt_hi2", [P, C, L], F32R)
        xl = sb("xt_lo2", [P, C, L], F32R)
        qh = sb("cqt_hi", [P, L], F32R)
        ql = sb("cqt_lo", [P, L], F32R)
        qb = sb("q_quads", [96, QUADS, L], F32R)
        qm = [sb(f"q_rows2_{s}", [P, NH, L], F32R) for s in range(2)]
        ks = [sb(f"k_rows2_{s}", [P, QUADS, LE], F32R) for s in range(2)]
        enc = sb("enc2", [P, KT, CH])
        eh = sb("enct_hi2", [P, 2, 512], F32R)
        el = sb("enct_lo2", [P, 2, 512], F32R)
        kh = sb("ckt_hi", [P, LE], F32R)
        kl = sb("ckt_lo", [P, LE], F32R)
        vraw = enc
        va = [sb(f"v_cross_{s}", [P, KT, NH // 2, 2, 18]) for s in range(2)]
        mp = sb("max_parts2", [P, T, NH, NJ])
        mx = sb("max2", [P, T, NH])
        mn = sb("neg_max2", [P, T, P], F32R)
        mt = sb("neg_max_rows2", [P, L])
        pr = sb("probs2", [P, 4, 4, 256])
        stage = pr[:, 0:2, 0, :]
        accs = sb("acc_sb2", [P, QUADS, 2, 256])
        rden = sb("rden2", [P, L])
        cx = sb("ctx2", [P, L])
        cxh = sb("ctx_hi2", [P, L], F32R)
        cxl = sb("ctx_lo2", [P, L], F32R)
        m = semaphores(nc, ctx, "w2_loaded", "w2_hi", "w2_lo", "v_zeroed", "v_one", "rows_zero", "acc_zero", "work_ready", "work_free",
              "ssq_ready", "eps_added", "rstd_ready", "xs_ready", "xh_ready", "xl_ready", "qh_ready", "qb_ready",
              "qm_ready", "enc_loaded", "eh_ready", "kh_ready", "ks_ready00", "ks_ready01", "ks_ready02", "ks_ready03",
              "ks_ready10", "ks_ready11", "ks_ready12", "ks_ready13", "va_ready", "mx_ready", "mh_ready", "ml_ready",
              "mrow_ready", "st_ready", "exp_done", "pv_done", "acc_copied", "acc_used", "rden_ready", "cxh_ready",
              "cxl_ready")
        ks_ready = [[m.ks_ready00, m.ks_ready01, m.ks_ready02, m.ks_ready03],
                    [m.ks_ready10, m.ks_ready11, m.ks_ready12, m.ks_ready13]]
        ident = g.const[:, ID0:ID0 + P]
        NS = QUADS * CHUNKS
        DMA = 16

        def chunk(k):
            quad, r = divmod(k, CHUNKS)
            return quad, (4 * quad + r // QC if r < CHUNKS - 1 else None), r % QC

        def item(k):
            pair, r = divmod(k, ITEMS // 2)
            if r == ITEMS // 2 - 1:
                return pair // 2, 2 * pair, None, NJ - 1
            return pair // 2, 2 * pair + r // (T * QC), (r // QC) % T, r % QC

        def front_part(k):
            return ("x", 0) if k == 0 else ("q", 0) if k == 1 else (("t", "k", "v")[(k - 2) % 3], (k - 2) // 3)

        def slot_of(parts, what, k):
            return next(s for w, n, s in PLAN[parts][0] if (w, n) == (what, k))

        block = ctx.enter_context(nc.Block())

        @block.sync
        def _(sp):
            sp.dma_start(lnw[:, :], io["L0_xattn_ln_post_cross_w"].rearrange("(c p) -> p c", p=P),
                         allow_slow_non_contiguous=True).then_inc(m.w2_loaded, DMA)
            sp.dma_start(stage[:, :, 0:CH], io["L0_xattn_cq_w"].rearrange("(c p) n -> p c n", p=P)).then_inc(m.w2_loaded, DMA)
            sp.dma_start(stage[:, 0, CH:2 * CH], io["L0_xattn_ckv_w"][:, 0:CH]).then_inc(m.w2_loaded, DMA)
            sp.dma_start(stage[:, 1, CH:2 * CH], io["L0_xattn_ckv_w"][:, CH:2 * CH]).then_inc(m.w2_loaded, DMA)
            sp.dma_start(cx[:, :], io["L0_xattn_cdense_w"]).then_inc(m.w2_loaded, DMA)

            def one(f, n, b, parts, slot0, bank0):
                if not parts[0]:
                    return
                i, s = f.number, f.parity
                if parts != (1, 0, 0):
                    sp.wait_ge(m.va_ready, 4 * i)
                load_encoder(i)
                sp.wait_ge(m.work_free, slot0 + (slot_of(parts, "front", 1) + 4))
                if parts != (1, 0, 0):
                    sp.wait_ge(m.qm_ready, 4 * i)
                for blk, part in enumerate((qh, qh, ql)):
                    for quad in range(QUADS):
                        sp.dma_start(qb[32 * blk:32 * blk + 32, quad, :].bitcast(F32),
                                     part[32 * quad:32 * quad + 32, :].bitcast(F32)).then_inc(m.qb_ready, DMA)
                sp.wait_ge(m.work_free, slot0 + (slot_of(parts, "front", FRONT - 2) + 4))
                for quad in range(QUADS):
                    if parts[2]:
                        sp.wait_ge(m.exp_done, NS * b.number + (CHUNKS * (quad + 1) + 2))
                    for blk, part in enumerate((kh, kl, kh)):
                        sp.dma_start(ks[s][32 * blk:32 * blk + 32, quad, :].bitcast(F32),
                                     part[32 * quad:32 * quad + 32, :].bitcast(F32)).then_inc(ks_ready[s][quad], DMA)

            def load_encoder(i):
                src = io["ctx_1024"]
                if isinstance(i, int):
                    rows = src[i]
                else:
                    rows = src[bass.ds(i, 1)].rearrange("a l c -> (a l) c")
                sp.dma_start(enc[:, 0:KT - 1, :], rows[0:(KT - 1) * P, :].rearrange("(k p) c -> p k c", p=P)).then_inc(m.enc_loaded, DMA)
                sp.dma_start(enc[0:LAST, KT - 1, :], rows[(KT - 1) * P:LE, :]).then_inc(m.enc_loaded, DMA)

            iterations(sp, one)

        @block.gpsimd
        def _(pool):
            for s in range(2):
                nc.gpsimd.memset(va[s][:, :, :, :, :], 0.0).then_inc(m.v_zeroed, 1)
            pool.wait_ge(m.v_zeroed, 2)
            for s in range(2):
                for e in range(2):
                    nc.gpsimd.memset(va[s][:, :, :, e, 9 * e + 8], 1.0).then_inc(m.v_one, 1)
            pool.wait_ge(m.v_one, 4)
            pool.wait_ge(m.rows_zero, 5)

            def one(f, n, b, parts, slot0, bank0):
                if parts[0]:
                    pool.wait_ge(m.ssq_ready, 2 * f.number + 2)
                    nc.gpsimd.tensor_tensor(var[:, :], ssq[:, :], g.eps[:, :], ALU.add).then_inc(m.eps_added, 1)
                    pool.wait_ge(m.eps_added, f.number + 1)
                    nc.gpsimd.tensor_tensor(rstd[:, :], var[:, :], g.minus_half[:, :], ALU.pow).then_inc(m.rstd_ready, 1)
                masked = 0
                for what, k, slot in PLAN[parts][0]:
                    if what == "max" and k == 0:
                        pool.wait_ge(m.work_ready, slot0 + (slot + 1))
                        pool.wait_ge(m.work_free, slot0 + (slot + 3))
                        for e in range(2):
                            for k0, k1, rows in ((0, KT - 1, P), (KT - 1, KT, LAST)):
                                src = vraw[0:rows, k0:k1, :].rearrange("p k (q e d) -> p k q e d", e=2, d=CHD)[:, :, :, e, :]
                                nc.gpsimd.tensor_tensor(
                                    va[n.parity][0:rows, k0:k1, :, e, 9 * e:9 * e + CHD], src,
                                    g.zero[0:rows, 0:1].unsqueeze(2).unsqueeze(3).broadcast_to([rows, k1 - k0, NH // 2, CHD]),
                                    ALU.add).then_inc(m.va_ready, 1)
                    elif what == "maxcol":
                        pool.wait_ge(m.va_ready, 4 * n.number + 4)
                        pool.wait_ge(m.rstd_ready, f.number + 1 if parts[0] else B)
                        pool.wait_ge(m.qm_ready, 4 * f.number + masked if parts[0] else 4 * B)
                        pool.wait_ge(m.work_free, slot0 + (slot + 4))
                        nc.gpsimd.tensor_tensor(qm[n.parity][96:128, 4 * k:4 * k + 4, :],
                                                mt[96:128, :].unsqueeze(1).broadcast_to([32, 4, L]),
                                                g.const[96:128, MS0 + 4 * k:MS0 + 4 * k + 4].unsqueeze(2).broadcast_to([32, 4, L]),
                                                ALU.mult).then_inc(m.mrow_ready, 1)
                        pool.wait_ge(m.mrow_ready, 4 * n.number + (k + 1))
                    elif what == "front" and k == FRONT - 1 and not parts[2]:
                        for quad in range(QUADS):
                            mask_quad(f, b, parts, quad)
                        masked = QUADS
                    elif what == "scores" and parts[0] and k >= CHUNKS and k % CHUNKS == 2:
                        mask_quad(f, b, parts, k // CHUNKS - 1)
                        masked += 1
                if parts[0] and parts[2]:
                    mask_quad(f, b, parts, QUADS - 1)

            def mask_quad(f, b, parts, quad):
                pool.wait_ge(m.qb_ready, 12 * DMA * f.number + 12 * DMA)
                if parts[2]:
                    pool.wait_ge(m.exp_done, NS * b.number + (CHUNKS * (quad + 1) + 2))
                nc.gpsimd.tensor_tensor(qm[f.parity][0:96, 4 * quad:4 * quad + 4, :],
                                        qb[:, quad:quad + 1, :].bitcast(F32).broadcast_to([96, 4, L]),
                                        g.const[0:96, MC0:MC0 + 4].unsqueeze(2).broadcast_to([96, 4, L]),
                                        ALU.mult).then_inc(m.qm_ready, 1)

            iterations(pool, one)

        @block.scalar
        def _(act):
            act.wait_ge(m.w2_loaded, 5 * DMA)
            act.sem_inc(m.acc_copied, 1)
            act.sem_inc(m.exp_done, 2)

            def one(f, n, b, parts, slot0, bank0):
                if parts[0]:
                    for t in range(T):
                        nc.scalar.activation(xs[:, t, :], g.x[:, 2 * f.number + t, :], ACT.Square, scale=H ** -0.5,
                                             accum_out=ssq[:, t:t + 1]).then_inc(m.ssq_ready, 1)
                for what, k, slot in PLAN[parts][0]:
                    if what == "scores":
                        act.wait_ge(m.st_ready, NS * b.number + (k + 1))
                        act.wait_ge(m.pv_done, NS * b.number + (k + 1))
                        rows = P if chunk(k)[1] is not None else LAST
                        nc.scalar.activation(pr[0:rows, k % 4], st[0:rows, k % 2], ACT.Exp,
                                             scale=CHD ** -0.5).then_inc(m.exp_done, 1)
                    elif what == "values" and k % CHUNKS == CHUNKS - 1:
                        if k == CHUNKS - 1:
                            act.wait_ge(m.acc_used, b.number + 1)
                        act.wait_ge(m.pv_done, NS * b.number + (k + 5))
                        nc.scalar.activation(accs[:, k // CHUNKS, :, :], acc[:, :, :], ACT.Copy).then_inc(m.acc_copied, 1)
                    elif what == "front":
                        front(f, parts, *front_part(k), work[:, (bank0 + slot) % 3, :], slot0 + (slot + 1))
                    elif what == "sums" and k == 1:
                        act.wait_ge(m.work_free, slot0 + (slot + 4))
                        nc.scalar.activation(cxh[:, :], cx[:, :], ACT.Copy).then_inc(m.cxh_ready, 1)

            def front(f, parts, kind, j, src, ready):
                if kind == "v":
                    return
                act.wait_ge(m.work_ready, ready)
                w = chunk_cols(j)
                if kind == "x":
                    for c in range(C):
                        nc.scalar.activation(xh[:, c, :], src[:, c * L:(c + 1) * L], ACT.Copy,
                                             scale=lnw[:, c:c + 1]).then_inc(m.xh_ready, 1)
                elif kind == "q":
                    nc.scalar.activation(qh[:, :], src[:, 0:L], ACT.Copy).then_inc(m.qh_ready, 2)
                elif kind == "t":
                    nc.scalar.activation(eh[:, j % 2, 0:w], src[:, 0:w], ACT.Copy).then_inc(m.eh_ready, 1)
                else:
                    if j == 0 and parts != (1, 0, 0):
                        for quad in range(QUADS):
                            before = f.before if f.parity else f.before - 1
                            act.wait_ge(ks_ready[1 - f.parity][quad], 3 * DMA * (before + 1))
                    nc.scalar.activation(kh[:, 512 * j:512 * j + w], src[:, 0:w], ACT.Copy).then_inc(m.kh_ready, 1)

            iterations(act, one)

        @block.vector
        def _(dve):
            for s in range(2):
                nc.vector.tensor_copy(qm[s][96:128, :, :], g.zero[96:128, 0:1].unsqueeze(2).broadcast_to([32, NH, L])).then_inc(m.rows_zero, 1)
                nc.vector.tensor_copy(ks[s][96:128, :, :], g.one[96:128, 0:1].unsqueeze(2).broadcast_to([32, QUADS, LE])).then_inc(m.rows_zero, 1)
            nc.vector.tensor_copy(mn[:, :, :], g.zero[:, 0:1].unsqueeze(2).broadcast_to([P, T, P])).then_inc(m.rows_zero, 1)
            nc.vector.memset(acc[:, :, :], 0.0).then_inc(m.acc_zero, 1)
            dve.wait_ge(m.w2_loaded, 5 * DMA)
            pieces = ((wq_hi[:, :, :], wq_lo[:, :, :], stage[:, :, 0:CH]), (wkv_hi[:, 0:CH], wkv_lo[:, 0:CH], stage[:, 0, CH:2 * CH]),
                      (wkv_hi[:, CH:2 * CH], wkv_lo[:, CH:2 * CH], stage[:, 1, CH:2 * CH]), (wd_hi[:, :], wd_lo[:, :], cx[:, :]))
            for hi, lo, src in pieces:
                split_hi(nc, hi, src).then_inc(m.w2_hi, 1)
            dve.wait_ge(m.w2_hi, 4)
            for hi, lo, src in pieces:
                split_lo(nc, lo, src, hi).then_inc(m.w2_lo, 1)
            dve.wait_ge(m.rows_zero, 5)
            dve.wait_ge(m.w2_lo, 4)
            dve.sem_inc(m.work_free, 3)

            def one(f, n, b, parts, slot0, bank0):
                if parts[0]:
                    dve.wait_ge(m.rstd_ready, f.number + 1)
                    for t in range(T):
                        nc.vector.tensor_scalar(xs[:, t, :], g.x[:, 2 * f.number + t, :], rstd[:, t:t + 1], None,
                                                ALU.mult).then_inc(m.xs_ready, 1)
                for what, k, slot in PLAN[parts][0]:
                    if slot is not None:
                        src = work[:, (bank0 + slot) % 3, :]
                    if what == "max":
                        quad, h, t, j = item(k)
                        dve.wait_ge(m.work_ready, slot0 + (slot + 1))
                        if t is None:
                            nc.vector.reduce_max(mp[:, :, h:h + 2, j].rearrange("p t h -> p h t"),
                                                 src[:, 0:2 * T * EVEN].rearrange("p (h t k) -> p h t k", h=2, t=T),
                                                 AX_X).then_inc(m.work_free, 1)
                        else:
                            nc.vector.reduce_max(mp[:, t, h, j:j + 1], src[:, :], AX_X).then_inc(m.work_free, 1)
                    elif what == "maxrow":
                        row_maxima(n, k, slot0, last_slot)
                    elif what == "maxcol":
                        dve.wait_ge(m.work_ready, slot0 + (slot + 1))
                        if not (parts == (1, 1, 0) and k == 0):
                            dve.wait_ge(m.mrow_ready, 4 * n.number + k)
                        nc.vector.tensor_copy(mt[96:128, :], src[96:128, 0:L]).then_inc(m.work_free, 1)
                    elif what == "front":
                        front(f, n, parts, *front_part(k), src, slot0 + (slot + 1))
                    elif what == "sums" and k == 0:
                        dve.wait_ge(m.work_ready, slot0 + (slot + 1))
                        nc.vector.reciprocal(rden[:, :], src[:, 0:L]).then_inc(m.work_free, 1)
                    elif what == "sums":
                        dve.wait_ge(m.work_ready, slot0 + (slot + 1))
                        dve.wait_ge(m.work_free, slot0 + (slot + 3))
                        nc.vector.tensor_tensor(cx[:, :], src[:, 0:L], rden[:, :], ALU.mult).then_inc(m.work_free, 1)
                    elif what == "out":
                        if k == 0:
                            dve.wait_ge(m.cxh_ready, b.number + 1)
                            split_lo(nc, cxl[:, :], cx[:, :], cxh[:, :]).then_inc(m.cxl_ready, 1)
                        dve.wait_ge(m.work_ready, slot0 + (slot + 1))
                        xt = g.x[:, 2 * b.number + k, :]
                        nc.vector.tensor_tensor(xt, src[:, 0:H], xt, ALU.add).then_inc(m.work_free, 1)
                    if slot is not None:
                        last_slot = slot

            def row_maxima(n, quad, slot0, last_slot):
                hs = slice(4 * quad, 4 * quad + 4)
                dve.wait_ge(m.work_free, slot0 + (last_slot + 4))
                nc.vector.reduce_max(mx[:, :, hs], mp[:, :, hs, :], AX_X).then_inc(m.mx_ready, 1)
                dve.wait_ge(m.mx_ready, 4 * n.number + (quad + 1))
                nc.vector.tensor_scalar(mn[:, :, 96 + 4 * quad:100 + 4 * quad], mx[:, :, hs], -1.0, None,
                                        ALU.mult).then_inc(m.mh_ready, 1)
                dve.wait_ge(m.mh_ready, 4 * n.number + (quad + 1))
                nc.vector.scalar_tensor_tensor(mn[:, :, 112 + 4 * quad:116 + 4 * quad], mx[:, :, hs], -1.0,
                                               mn[:, :, 96 + 4 * quad:100 + 4 * quad].bitcast(F32), ALU.mult,
                                               ALU.subtract).then_inc(m.ml_ready, 1)

            def front(f, n, parts, kind, j, src, ready):
                w = chunk_cols(j)
                if kind == "x":
                    dve.wait_ge(m.xh_ready, 2 * f.number + 2)
                    for c in range(C):
                        ins = nc.vector.scalar_tensor_tensor(xl[:, c, :], src[:, c * L:(c + 1) * L], lnw[:, c:c + 1],
                                                             xh[:, c, :].bitcast(F32), ALU.mult, ALU.subtract)
                        ins.then_inc(m.xl_ready if c == 0 else m.work_free, 1)
                elif kind == "q":
                    dve.wait_ge(m.qh_ready, 2 * f.number + 2)
                    nc.vector.tensor_tensor(ql[:, :], src[:, 0:L], qh[:, :].bitcast(F32), ALU.subtract).then_inc(m.work_free, 1)
                elif kind == "t":
                    dve.wait_ge(m.eh_ready, 4 * f.number + (j + 1))
                    nc.vector.tensor_tensor(el[:, j % 2, 0:w], src[:, 0:w], eh[:, j % 2, 0:w].bitcast(F32),
                                            ALU.subtract).then_inc(m.work_free, 1)
                elif kind == "k":
                    dve.wait_ge(m.kh_ready, 4 * f.number + (j + 1))
                    nc.vector.tensor_tensor(kl[:, 512 * j:512 * j + w], src[:, 0:w], kh[:, 512 * j:512 * j + w].bitcast(F32),
                                            ALU.subtract).then_inc(m.work_free, 1)
                else:
                    dve.wait_ge(m.work_ready, ready)
                    tiles = chunk_tiles(j)
                    rows = tile_rows(tiles[-1])
                    nc.vector.tensor_copy(vraw[0:rows, tiles[0]:tiles[-1] + 1, :],
                                          src[0:rows, 0:len(tiles) * CH].rearrange("p (k c) -> p k c", c=CH)).then_inc(m.work_free, 1)

            iterations(dve, one)

        @block.tensor
        def _(pe):
            pe.sem_inc(m.pv_done, 4)
            pe.sem_inc(m.acc_used, 1)
            pe.wait_ge(m.w2_lo, 4)
            pe.wait_ge(m.rows_zero, 5)
            pe.wait_ge(m.acc_zero, 1)
            pe.wait_ge(m.v_one, 4)

            def one(f, n, b, parts, slot0, bank0):
                for what, k, slot in PLAN[parts][0]:
                    if slot is not None:
                        dst = work[:, (bank0 + slot) % 3, :]
                        if what not in ("sums", "out", "maxcol") and what != "front":
                            pe.wait_ge(m.work_free, slot0 + (slot + 1))
                    if what == "max":
                        maxima(n, k, dst)
                    elif what == "maxcol":
                        pe.wait_ge(m.ml_ready, 4 * n.number + (k + 1))
                        pe.wait_ge(m.work_free, slot0 + (slot + 1))
                        for t in range(T):
                            last = nc.tensor.transpose(dst[:, t * P:(t + 1) * P], mn[:, t, :].bitcast(F32), ident)
                        last.then_inc(m.work_ready, 1)
                    elif what == "front":
                        front(f, *front_part(k), dst, slot0 + (slot + 1))
                    elif what == "scores":
                        scores(b, k)
                    elif what == "values":
                        values(b, k)
                    elif what == "sums":
                        if k == 0:
                            pe.wait_ge(m.acc_copied, 4 * b.number + 5)
                        pe.wait_ge(m.work_free, slot0 + (slot + 1))
                        for par in range(2):
                            for quad in range(QUADS):
                                e0 = EC0 + 64 * (1 - k) + 32 * par
                                last = nc.tensor.matmul(dst[32 * quad:32 * quad + 32, 0:L], g.const[:, e0:e0 + 32],
                                                        accs[:, quad, par, :], start=(par == 0), stop=(par == 1),
                                                        tile_position=(0, 32 * quad), skip_group_check=True)
                        last.then_inc(m.work_ready, 1)
                        if k == 1:
                            pe.wait_ge(m.work_ready, slot0 + (slot + 1))
                            pe.sem_inc(m.acc_used, 1)
                    elif what == "out":
                        if k == 0:
                            pe.wait_ge(m.cxl_ready, b.number + 1)
                        pe.wait_ge(m.work_free, slot0 + (slot + 1))
                        terms = three(((cxh[:, k * P:(k + 1) * P], cxl[:, k * P:(k + 1) * P]), (wd_hi[:, :], wd_lo[:, :])))
                        for i, (stat, mv) in enumerate(terms):
                            last = nc.tensor.matmul(dst[:, 0:H], stat, mv, start=(i == 0), stop=(i == 2))
                        last.then_inc(m.work_ready, 1)

            def maxima(n, k, dst):
                quad, h, t, j = item(k)
                if k % ITEMS == 0:
                    pe.wait_ge(m.qm_ready, 4 * n.number + (quad + 1))
                    pe.wait_ge(ks_ready[n.parity][quad], 3 * DMA * n.before + 3 * DMA)
                if t is None:
                    for i in range(2):
                        for t in range(T):
                            a = (i * T + t) * EVEN
                            last = nc.tensor.matmul(dst[:, a:a + EVEN], qm[n.parity][0:96, h + i, t * P:(t + 1) * P],
                                                    ks[n.parity][0:96, quad, LE - EVEN:LE], start=True, stop=True)
                else:
                    last = nc.tensor.matmul(dst[:, :], qm[n.parity][0:96, h, t * P:(t + 1) * P],
                                            ks[n.parity][0:96, quad, 512 * j:512 * j + 512], start=True, stop=True)
                last.then_inc(m.work_ready, 1)

            def scores(b, k):
                quad, h, j = chunk(k)
                if k % CHUNKS == 0:
                    pe.wait_ge(m.mrow_ready, 4 * b.number + (quad + 1))
                pe.wait_ge(m.exp_done, NS * b.number + (k + 1))
                for i in range(4):
                    kt, head, rows = (4 * j + i, h, P) if h is not None else (KT - 1, 4 * quad + i, LAST)
                    last = nc.tensor.matmul(st[0:rows, k % 2, i, :], ks[b.parity][:, quad, kt * P:kt * P + rows],
                                            qm[b.parity][:, head, :], start=True, stop=True)
                last.then_inc(m.st_ready, 1)

            def values(b, k):
                quad, h, j = chunk(k)
                if k == 0:
                    pe.wait_ge(m.va_ready, 4 * b.number + 4)
                if k % CHUNKS == 0:
                    pe.wait_ge(m.acc_copied, 4 * b.number + (quad + 1))
                pe.wait_ge(m.exp_done, NS * b.number + (k + 3))
                for i in range(4):
                    kt, head, rows = (4 * j + i, h, P) if h is not None else (KT - 1, 4 * quad + i, LAST)
                    local = head - 4 * quad
                    last = nc.tensor.matmul(acc[32 * i:32 * i + 18, local // 2, :],
                                            va[b.parity][0:rows, kt, head // 2, local % 2, :], pr[0:rows, k % 4, i, :],
                                            start=(k % CHUNKS == 0), stop=(h is None), tile_position=(0, 32 * i),
                                            skip_group_check=True)
                last.then_inc(m.pv_done, 1)

            def front(f, kind, j, dst, free):
                i = f.number
                tiles = chunk_tiles(j)
                w = chunk_cols(j)
                if kind == "x":
                    pe.wait_ge(m.xs_ready, 2 * i + 2)
                    pe.wait_ge(m.work_free, free)
                    for t in range(T):
                        for c in range(C):
                            last = nc.tensor.transpose(dst[:, c * L + t * P:c * L + t * P + P], xs[:, t, c * P:(c + 1) * P], ident)
                elif kind == "t":
                    if j == 0:
                        pe.wait_ge(m.enc_loaded, 2 * DMA * i + 2 * DMA)
                    pe.wait_ge(m.work_free, free)
                    for a, kt in enumerate(tiles):
                        rows = tile_rows(kt)
                        last = nc.tensor.transpose(dst[:, a * P:a * P + rows], enc[0:rows, kt, :], ident[0:rows, 0:rows])
                elif kind == "q":
                    pe.wait_ge(m.work_free, free + 2)
                    terms = []
                    for c in range(C):
                        terms += three(((wq_hi[:, c, :], wq_lo[:, c, :]), (xh[:, c, :], xl[:, c, :])))
                    for a, (stat, mv) in enumerate(terms):
                        last = nc.tensor.matmul(dst[:, 0:L], stat, mv, start=(a == 0), stop=(a == len(terms) - 1))
                elif kind == "k":
                    pe.wait_ge(m.work_free, free + 2)
                    w += w % 2
                    terms = three(((wkv_hi[:, 0:CH], wkv_lo[:, 0:CH]), (eh[:, j % 2, 0:w], el[:, j % 2, 0:w])))
                    for a, (stat, mv) in enumerate(terms):
                        last = nc.tensor.matmul(dst[:, 0:w], stat, mv, start=(a == 0), stop=(a == 2))
                else:
                    pe.wait_ge(m.work_free, free)
                    for a, kt in enumerate(tiles):
                        rows = tile_rows(kt)
                        terms = three(((eh[:, j % 2, a * P:a * P + rows], el[:, j % 2, a * P:a * P + rows]),
                                       (wkv_hi[:, CH:2 * CH], wkv_lo[:, CH:2 * CH])))
                        for c, (stat, mv) in enumerate(terms):
                            last = nc.tensor.matmul(dst[0:rows, a * CH:(a + 1) * CH], stat, mv, start=(c == 0), stop=(c == 2))
                last.then_inc(m.work_ready, 1)

            iterations(pe, one)



FT = 6
FW = (FF + FT - 1) // FT
RING3 = 5
SLOTS3 = FT + 2 + T


def mlp(nc, g, io):
    with ExitStack() as ctx:
        sb, ps = allocator(nc, ctx)
        work = ps("work3", [P, RING3, 512])
        raw_gu = sb("w_gate_up", [P, 2, 2, C, FF])
        raw_d = sb("w_down", [P, FT, 2 * H])
        gu_hi = sb("w_gate_up_hi", [P, 2, 2, C, FF], F32R)
        gu_lo = sb("w_gate_up_lo", [P, 2, 2, C, FF], F32R)
        d_hi = sb("w_down_hi", [P, FT, 2 * H], F32R)
        d_lo = sb("w_down_lo", [P, FT, 2 * H], F32R)
        lnw = sb("ln_mlp_w", [P, C])
        sq = sb("squares3", [P, T, H])
        ssq = sb("mean_squares3", [P, T])
        var = sb("variance3", [P, T])
        rstd = sb("rstd3", [P, T])
        rex = sb("rstd_by_expert3", [P, 2, T])
        xe = sb("x_by_expert3", [P, 2, T, H])
        xh = sb("xt_hi3", [P, 2, C, L], F32R)
        xl = sb("xt_lo3", [P, 2, C, L], F32R)
        th = sb("tanh3", [P, 2, L])
        sg = sb("gated3", [P, 2, L])
        pa = sb("act3", [P, FT, L])
        ah = sb("act_hi3", [P, FT, L], F32R)
        al = sb("act_lo3", [P, FT, L], F32R)
        m = semaphores(nc, ctx, "gu_loaded", "d_loaded", "ln_loaded", "gu_hi_ready", "gu_lo_ready", "d_hi_ready", "d_lo_ready", "ssq_ready",
              "eps_added", "rstd_ready", "rex_ready", "xe_ready", "xh_ready", "xl_ready", "work_ready", "work_free",
              "th_ready", "sg_ready", "ah_ready", "al_ready", "res_v")
        ident = g.const[:, ID0:ID0 + P]
        FIRST = 2
        block = ctx.enter_context(nc.Block())

        def width(i):
            return min(FW, FF - FW * i)

        def iterations(eng, one):
            with eng.Fori(0, B - 1) as b:
                one(b, True)
            one(B - 1, False)

        def slot(b, n):
            return SLOTS3 * b + (FIRST + n)

        def out_slot(t, ahead):
            return FT + (2 if ahead else 0) + t

        @block.sync
        def _(sp):
            sp.dma_start(lnw[:, :], io["L0_xattn_ln_post_attn_w"].rearrange("(c p) -> p c", p=P),
                         allow_slow_non_contiguous=True).then_inc(m.ln_loaded, 16)
            for e, x in enumerate("vl"):
                for u, name in enumerate(("gate", "up")):
                    sp.dma_start(raw_gu[:, e, u], io[f"L0_xattn_{x}_{name}"].rearrange("(c p) n -> p c n", p=P)).then_inc(m.gu_loaded, 16)
            for e, x in enumerate("vl"):
                wd = io[f"L0_xattn_{x}_down"]
                sp.dma_start(raw_d[0:FW, 0:FT - 1, e * H:(e + 1) * H],
                             wd[0:FW * (FT - 1), :].rearrange("(k p) n -> p k n", p=FW)).then_inc(m.d_loaded, 16)
                sp.dma_start(raw_d[0:width(FT - 1), FT - 1, e * H:(e + 1) * H], wd[FW * (FT - 1):FF, :]).then_inc(m.d_loaded, 16)

        @block.gpsimd
        def _(pool):
            def norm(b):
                pool.wait_ge(m.ssq_ready, 2 * b + 2)
                nc.gpsimd.tensor_tensor(var[:, :], ssq[:, :], g.eps[:, :], ALU.add).then_inc(m.eps_added, 1)
                pool.wait_ge(m.eps_added, b + 1)
                nc.gpsimd.tensor_tensor(rstd[:, :], var[:, :], g.minus_half[:, :], ALU.pow).then_inc(m.rstd_ready, 1)

            norm(0)
            with pool.Fori(1, B) as b:
                norm(b)

        @block.scalar
        def _(act):
            def norm(b):
                for t in range(T):
                    nc.scalar.activation(sq[:, t, :], g.x[:, 2 * b + t, :], ACT.Square, scale=H ** -0.5,
                                         accum_out=ssq[:, t:t + 1]).then_inc(m.ssq_ready, 1)

            def inputs(b, slot0, bank0):
                for e in range(2):
                    act.wait_ge(m.work_ready, slot0 + (e + 1))
                    for c in range(C):
                        nc.scalar.activation(xh[:, e, c, :], work[:, (bank0 + e) % RING3, c * L:(c + 1) * L], ACT.Copy,
                                             scale=lnw[:, c:c + 1]).then_inc(m.xh_ready, 1)

            def hi(b, i):
                act.wait_ge(m.work_free, slot(b, i) + (1 + RING3))
                w = width(i)
                nc.scalar.activation(ah[0:w, i, :], pa[0:w, i, :], ACT.Copy, scale=0.5).then_inc(m.ah_ready, 1)

            def one(b, ahead):
                if ahead:
                    norm(b + 1)
                for i in range(FT):
                    w = width(i)
                    act.wait_ge(m.work_ready, slot(b, i) + 1)
                    if i >= 2:
                        act.wait_ge(m.sg_ready, FT * b + (i - 1))
                    nc.scalar.activation(th[0:w, i % 2, :], work[0:w, (FIRST + i) % RING3, 0:L], ACT.Tanh,
                                         scale=0.5).then_inc(m.th_ready, 1)
                    if i:
                        hi(b, i - 1)
                hi(b, FT - 1)
                if ahead:
                    inputs(b + 1, slot(b, FT), FIRST + FT)

            act.wait_ge(m.ln_loaded, 16)
            norm(0)
            inputs(0, 0, 0)
            iterations(act, one)

        @block.vector
        def _(dve):
            def scaled(b):
                dve.wait_ge(m.rstd_ready, b + 1)
                nc.vector.tensor_tensor(rex[:, 0, :], rstd[:, :], g.vm[:, bass.ds(2 * b, 2)], ALU.mult).then_inc(m.rex_ready, 1)
                nc.vector.tensor_tensor(rex[:, 1, :], rstd[:, :], g.nvm[:, bass.ds(2 * b, 2)], ALU.mult).then_inc(m.rex_ready, 1)
                dve.wait_ge(m.rex_ready, 2 * b + 2)
                for e in range(2):
                    for t in range(T):
                        nc.vector.tensor_scalar(xe[:, e, t, :], g.x[:, 2 * b + t, :], rex[:, e, t:t + 1], None,
                                                ALU.mult).then_inc(m.xe_ready, 1)

            def inputs(b, bank0):
                for e in range(2):
                    dve.wait_ge(m.xh_ready, 4 * b + (2 * e + 2))
                    for c in range(C):
                        ins = nc.vector.scalar_tensor_tensor(xl[:, e, c, :], work[:, (bank0 + e) % RING3, c * L:(c + 1) * L],
                                                             lnw[:, c:c + 1], xh[:, e, c, :].bitcast(F32), ALU.mult, ALU.subtract)
                        ins.then_inc(m.xl_ready if c == 0 else m.work_free, 1)

            def lo(b, i):
                dve.wait_ge(m.ah_ready, FT * b + (i + 1))
                w = width(i)
                nc.vector.scalar_tensor_tensor(al[0:w, i, :], pa[0:w, i, :], 0.5, ah[0:w, i, :].bitcast(F32), ALU.mult,
                                               ALU.subtract).then_inc(m.al_ready, 1)

            def one(b, ahead):
                if ahead:
                    scaled(b + 1)
                for i in range(FT):
                    w = width(i)
                    src = work[0:w, (FIRST + i) % RING3, :]
                    dve.wait_ge(m.th_ready, FT * b + (i + 1))
                    nc.vector.scalar_tensor_tensor(sg[0:w, i % 2, :], th[0:w, i % 2, :], 1.0, src[:, 0:L], ALU.add,
                                                   ALU.mult).then_inc(m.sg_ready, 1)
                    dve.wait_ge(m.sg_ready, FT * b + (i + 1))
                    nc.vector.tensor_tensor(pa[0:w, i, :], src[:, L:2 * L], sg[0:w, i % 2, :], ALU.mult).then_inc(m.work_free, 1)
                    if i:
                        lo(b, i - 1)
                lo(b, FT - 1)
                if ahead:
                    inputs(b + 1, FIRST + FT)
                for t in range(T):
                    n = out_slot(t, ahead)
                    src = work[:, (FIRST + n) % RING3, :]
                    xt = g.x[:, 2 * b + t, :]
                    dve.wait_ge(m.work_ready, slot(b, n) + 1)
                    nc.vector.scalar_tensor_tensor(xt, src[:, 0:H], g.vm[:, bass.ds(2 * b + t, 1)], xt, ALU.mult,
                                                   ALU.add).then_inc(m.res_v, 1)
                    dve.wait_ge(m.res_v, 2 * b + (t + 1))
                    nc.vector.scalar_tensor_tensor(xt, src[:, H:2 * H], g.nvm[:, bass.ds(2 * b + t, 1)], xt, ALU.mult,
                                                   ALU.add).then_inc(m.work_free, 1)

            dve.sem_inc(m.work_free, RING3)
            dve.wait_ge(m.ln_loaded, 16)
            scaled(0)
            dve.wait_ge(m.gu_loaded, 64)
            for e in range(2):
                split_hi(nc, gu_hi[:, e], raw_gu[:, e]).then_inc(m.gu_hi_ready, 1)
            dve.wait_ge(m.gu_hi_ready, 2)
            for e in range(2):
                split_lo(nc, gu_lo[:, e], raw_gu[:, e], gu_hi[:, e]).then_inc(m.gu_lo_ready, 1)
            inputs(0, 0)
            dve.wait_ge(m.d_loaded, 64)
            pieces = [(slice(0, FW), slice(0, FT - 1)), (slice(0, width(FT - 1)), slice(FT - 1, FT))]
            for r, k in pieces:
                split_hi(nc, d_hi[r, k], raw_d[r, k]).then_inc(m.d_hi_ready, 1)
            dve.wait_ge(m.d_hi_ready, 2)
            for r, k in pieces:
                split_lo(nc, d_lo[r, k], raw_d[r, k], d_hi[r, k]).then_inc(m.d_lo_ready, 1)
            iterations(dve, one)

        @block.tensor
        def _(pe):
            def inputs(b, slot0, bank0):
                for e in range(2):
                    pe.wait_ge(m.xe_ready, 4 * b + (2 * e + 2))
                    pe.wait_ge(m.work_free, slot0 + (e + 1))
                    for t in range(T):
                        for c in range(C):
                            a = c * L + t * P
                            last = nc.tensor.transpose(work[:, (bank0 + e) % RING3, a:a + P], xe[:, e, t, c * P:(c + 1) * P], ident)
                    last.then_inc(m.work_ready, 1)

            def one(b, ahead):
                pe.wait_ge(m.xl_ready, 2 * b + 2)
                for i in range(FT):
                    w = width(i)
                    pe.wait_ge(m.work_free, slot(b, i) + 1)
                    if i == 0:
                        pe.wait_ge(m.work_free, SLOTS3 * b + RING3)
                    for u in range(2):
                        terms = []
                        for e in range(2):
                            for c in range(C):
                                terms += three(((gu_hi[:, e, u, c, FW * i:FW * i + w], gu_lo[:, e, u, c, FW * i:FW * i + w]),
                                                (xh[:, e, c, :], xl[:, e, c, :])))
                        for k, (stat, mv) in enumerate(terms):
                            last = nc.tensor.matmul(work[0:w, (FIRST + i) % RING3, u * L:(u + 1) * L], stat, mv,
                                                    start=(k == 0), stop=(k == len(terms) - 1))
                    last.then_inc(m.work_ready, 1)
                if ahead:
                    inputs(b + 1, slot(b, FT), FIRST + FT)
                pe.wait_ge(m.al_ready, FT * b + FT)
                for t in range(T):
                    n = out_slot(t, ahead)
                    pe.wait_ge(m.work_free, slot(b, n) + 1)
                    terms = []
                    for i in range(FT):
                        w = width(i)
                        for stat, mv in three(((ah[0:w, i, t * P:(t + 1) * P], al[0:w, i, t * P:(t + 1) * P]),
                                               (d_hi[0:w, i, :], d_lo[0:w, i, :]))):
                            terms.append((stat, mv))
                    for k, (stat, mv) in enumerate(terms):
                        last = nc.tensor.matmul(work[:, (FIRST + n) % RING3, :], stat, mv, start=(k == 0), stop=(k == len(terms) - 1))
                    last.then_inc(m.work_ready, 1)

            pe.wait_ge(m.xe_ready, 4)
            inputs(0, 0, 0)
            pe.wait_ge(m.gu_lo_ready, 2)
            pe.wait_ge(m.d_lo_ready, 2)
            iterations(pe, one)



RING4 = 4


def plan4(front, attend, close):
    out, slots = [], 0

    def put(what, k=0, slot=True):
        nonlocal slots
        out.append((what, k, slots if slot else None))
        slots += slot

    if attend:
        put("scores", 0, False)
    if close:
        put("fuse", 0, False)
    if front:
        for c in range(C):
            put("x", c)
        put("query", 0)
    if attend:
        put("scores", 1, False)
        for j in range(NJ):
            put("turn", j)
    if close:
        put("finish", 0, False)
    if front:
        for j in range(NJ):
            put("memory", j)
    if attend:
        for j in range(NJ, 2 * NJ):
            put("turn", j)
        put("context", 0)
        for t in range(T):
            put("out", t)
            put("gate", t)
    return out, slots


PLAN4 = {k: plan4(*k) for k in ((1, 0, 0), (1, 1, 0), (1, 1, 1), (0, 1, 1), (0, 0, 1))}


def iterations4(eng, one):
    first = 0

    def run(i, s, before, parts, slot0, bank0):
        one(Batch(i + 1, 1 - s, before + s), Batch(i, s, before), Batch(i - 1, 1 - s, before + s - 1), parts, slot0, bank0)

    run(-1, 1, -1, (1, 0, 0), 0, 0)
    first += PLAN4[1, 0, 0][1]
    run(0, 0, 0, (1, 1, 0), first, first % RING4)
    first += PLAN4[1, 1, 0][1]
    per = PLAN4[1, 1, 1][1]
    assert per % RING4 == 0
    with eng.Fori(0, B // 2 - 1) as pair:
        for s in range(2):
            run(2 * pair + (1 + s), 1 - s, pair + s, (1, 1, 1), (2 * per) * pair + (first + per * s), first % RING4)
    first += per * (B - 2)
    run(B - 1, 1, B // 2 - 1, (0, 1, 1), first, first % RING4)
    first += PLAN4[0, 1, 1][1]
    run(B, 0, B // 2, (0, 0, 1), first, first % RING4)


def fusion(nc, g, io):
    with ExitStack() as ctx:
        sb, ps = allocator(nc, ctx)
        work = ps("work4", [P, RING4, 512])
        st = ps("scores4", [P, NJ * 512])
        raw_m = sb("w_mem", [P, C, CH])
        m_hi = sb("w_mem_hi", [P, C, CH], F32R)
        m_lo = sb("w_mem_lo", [P, C, CH], F32R)
        raw_g = sb("w_gate", [P, C, 2 * H])
        gt = sb("w_gate_t", [P, 4, H])
        g_hi = sb("w_gate_t_hi", [P, C, H], F32R)
        g_lo = sb("w_gate_t_lo", [P, C, H], F32R)
        mc = sb("w_context", [P, 2 * H])
        mc_hi = sb("w_context_hi", [P, 2 * H], F32R)
        mc_lo = sb("w_context_lo", [P, 2 * H], F32R)
        bg = sb("b_gate", [P, H])
        nw = sb("norm_w", [P, H])
        xc = sb("x_of_batch", [P, T, H])
        enc = [sb(f"memory_{s}", [P, KT, CH]) for s in range(2)]
        xh = [sb(f"xt_hi4_{s}", [P, C, L], F32R) for s in range(2)]
        xl = [sb(f"xt_lo4_{s}", [P, C, L], F32R) for s in range(2)]
        qh = [sb(f"queries_hi_{s}", [P, L], F32R) for s in range(2)]
        ql = [sb(f"queries_lo_{s}", [P, L], F32R) for s in range(2)]
        eh = sb("memory_t_hi", [P, LE + 1], F32R)
        el = sb("memory_t_lo", [P, LE + 1], F32R)
        mx = sb("max4", [P, T])
        nm = sb("neg_max4", [P, T])
        pr = sb("probs4", [P, T, LE])
        total = sb("prob_sums4", [P, T])
        rt = sb("reciprocal_sums4", [P, T])
        pt = sb("probs_t4", [P, KT, L])
        tt = sb("memory_mix", [P, L])
        tth = sb("memory_mix_hi", [P, L], F32R)
        ttl = sb("memory_mix_lo", [P, L], F32R)
        cv = [sb(f"context_{s}", [P, T, H]) for s in range(2)]
        gp = sb("gate_part", [P, T, H])
        gs = [sb(f"gate_in_{s}", [P, T, H]) for s in range(2)]
        th = sb("tanh4", [P, T, H])
        fz = sb("gated_context", [P, T, H])
        fu = sb("fused", [P, T, H])
        sq = sb("squares4", [P, T, H])
        ssq = sb("mean_squares4", [P, T])
        var = sb("variance4", [P, T])
        rstd = sb("rstd4", [P, T])
        y = [sb(f"y_{s}", [P, T, H]) for s in range(2)]
        m = semaphores(nc, ctx, "w4_loaded", "pad_ready", "xc_ready", "gt_psum", "gt_ready", "m_psum", "mt_ready", "fold_ready", "w4_hi", "w4_lo", "enc_loaded0",
              "enc_loaded1", "enc_free", "xh_ready", "qh_ready", "eh_ready", "work_ready", "work_free", "st_ready",
              "mx_ready", "nm_ready", "exp_done", "rt_ready", "tth_ready", "cv_ready", "gp_ready", "th_ready",
              "fz_ready", "fu_ready", "ssq_ready", "eps_added", "rstd_ready", "y_ready", "y_free", "stored")
        enc_loaded = [m.enc_loaded0, m.enc_loaded1]
        ident = g.const[:, ID0:ID0 + P]
        block = ctx.enter_context(nc.Block())

        def slot_of(parts, what, k):
            return next(s for w, n, s in PLAN4[parts][0] if (w, n) == (what, k))

        @block.sync
        def _(sp):
            sp.dma_start(raw_m[:, :, :], io["L1_xattn_W_mem"].rearrange("(c p) n -> p c n", p=P)).then_inc(m.w4_loaded, 16)
            sp.dma_start(raw_g[:, :, :], io["L1_xattn_W_gate"].rearrange("(c p) n -> p c n", p=P)).then_inc(m.w4_loaded, 16)
            sp.dma_start(bg[:, :], io["L1_xattn_b_gate"].rearrange("(a n) -> a n", a=1).broadcast_to([P, H])).then_inc(m.w4_loaded, 16)
            sp.dma_start(nw[:, :], io["L1_xattn_norm_w"].rearrange("(a n) -> a n", a=1).broadcast_to([P, H])).then_inc(m.w4_loaded, 16)

            def one(f, n, b, parts, slot0, bank0):
                if parts[0]:
                    if parts[2]:
                        sp.wait_ge(m.enc_free, 2 * f.number - 2)
                    src = io["ctx_1024"]
                    rows = src[f.number] if isinstance(f.number, int) else src[bass.ds(f.number, 1)].rearrange("a l c -> (a l) c")
                    dst, sem = enc[f.parity], enc_loaded[f.parity]
                    sp.dma_start(dst[:, 0:KT - 1, :], rows[0:(KT - 1) * P, :].rearrange("(k p) c -> p k c", p=P)).then_inc(sem, 16)
                    sp.dma_start(dst[0:LAST, KT - 1, :], rows[(KT - 1) * P:LE, :]).then_inc(sem, 16)
                if parts[2]:
                    sp.wait_ge(m.y_ready, 2 * b.number + 2)
                    out = io["out"]
                    dst = out[b.number] if isinstance(b.number, int) else out[bass.ds(b.number, 1)].rearrange("a l c -> (a l) c")
                    sp.dma_start(dst.rearrange("(t p) n -> p t n", p=P), y[b.parity][:, :, :]).then_inc(m.stored, 16)
                    sp.wait_ge(m.stored, 16 * b.number + 16)
                    sp.sem_inc(m.y_free, 1)

            sp.sem_inc(m.y_free, 2)
            iterations4(sp, one)

        @block.gpsimd
        def _(pool):
            def one(f, n, b, parts, slot0, bank0):
                for what, k, slot in PLAN4[parts][0]:
                    if what == "x" and k == 0:
                        if parts[1]:
                            pool.wait_ge(m.xh_ready, 2 * f.number)
                        nc.gpsimd.tensor_copy(xc[:, :, :], g.x[:, bass.ds(2 * f.number, 2), :]).then_inc(m.xc_ready, 1)
                    elif what == "finish":
                        pool.wait_ge(m.ssq_ready, 2 * b.number + 2)
                        nc.gpsimd.tensor_tensor(var[:, :], ssq[:, :], g.eps[:, :], ALU.add).then_inc(m.eps_added, 1)
                        pool.wait_ge(m.eps_added, b.number + 1)
                        nc.gpsimd.tensor_tensor(rstd[:, :], var[:, :], g.minus_half[:, :], ALU.pow).then_inc(m.rstd_ready, 1)

            iterations4(pool, one)

        @block.scalar
        def _(act):
            def one(f, n, b, parts, slot0, bank0):
                for what, k, slot in PLAN4[parts][0]:
                    if slot is not None:
                        src = work[:, (bank0 + slot) % RING4, :]
                    if what == "scores":
                        act.wait_ge(m.nm_ready, 2 * n.number + (k + 1))
                        nc.scalar.activation(pr[:, k, :], st[:, 0:LE], ACT.Exp, bias=nm[:, k:k + 1], scale=H ** -0.5,
                                             accum_out=total[:, k:k + 1]).then_inc(m.exp_done, 1)
                    elif what == "x":
                        act.wait_ge(m.work_ready, slot0 + (slot + 1))
                        nc.scalar.activation(xh[f.parity][:, k, :], src[:, 0:L], ACT.Copy).then_inc(m.xh_ready, 1)
                    elif what == "query":
                        act.wait_ge(m.work_ready, slot0 + (slot + 1))
                        nc.scalar.activation(qh[f.parity][:, :], src[:, 0:L], ACT.Copy).then_inc(m.qh_ready, 1)
                    elif what == "memory":
                        act.wait_ge(m.work_ready, slot0 + (slot + 1))
                        w = chunk_cols(k)
                        nc.scalar.activation(eh[:, 512 * k:512 * k + w], src[:, 0:w], ACT.Copy).then_inc(m.eh_ready, 1)
                    elif what == "context":
                        act.wait_ge(m.work_ready, slot0 + (slot + 1))
                        nc.scalar.activation(tth[:, :], src[:, 0:L], ACT.Copy).then_inc(m.tth_ready, 1)
                    elif what == "fuse":
                        act.wait_ge(m.work_free, slot0 + RING4)
                        for t in range(T):
                            nc.scalar.activation(th[:, t, :], gs[b.parity][:, t, :], ACT.Tanh, scale=0.5).then_inc(m.th_ready, 1)
                    elif what == "finish":
                        act.wait_ge(m.fu_ready, 2 * b.number + 2)
                        for t in range(T):
                            nc.scalar.activation(sq[:, t, :], fu[:, t, :], ACT.Square, scale=H ** -0.5,
                                                 accum_out=ssq[:, t:t + 1]).then_inc(m.ssq_ready, 1)

            iterations4(act, one)

        @block.vector
        def _(dve):
            dve.sem_inc(m.work_free, RING4)
            for x in (eh, el):
                nc.vector.tensor_copy(x[:, LE:LE + 1], g.zero[:, :]).then_inc(m.pad_ready, 1)
            dve.wait_ge(m.gt_psum, 4)
            nc.vector.tensor_copy(gt[:, :, :], st[:, 0:4 * H].rearrange("p (k n) -> p k n", k=4)).then_inc(m.gt_ready, 1)
            dve.wait_ge(m.m_psum, 1)
            nc.vector.tensor_copy(mc[:, 0:H], st[:, 2 * 512:2 * 512 + H]).then_inc(m.mt_ready, 1)
            dve.wait_ge(m.m_psum, 2)
            nc.vector.tensor_copy(mc[:, H:2 * H], st[:, 3 * 512:3 * 512 + H]).then_inc(m.mt_ready, 1)
            dve.wait_ge(m.mt_ready, 2)
            pieces = ((m_hi[:, :, :], m_lo[:, :, :], raw_m[:, :, :]), (g_hi[:, :, :], g_lo[:, :, :], gt[:, 0:C, :]),
                      (mc_hi[:, :], mc_lo[:, :], mc[:, :]))
            for hi, lo, src in pieces:
                split_hi(nc, hi, src).then_inc(m.w4_hi, 1)
            dve.wait_ge(m.w4_hi, 3)
            for hi, lo, src in pieces:
                split_lo(nc, lo, src, hi).then_inc(m.w4_lo, 1)

            def one(f, n, b, parts, slot0, bank0):
                for what, k, slot in PLAN4[parts][0]:
                    if slot is not None:
                        src = work[:, (bank0 + slot) % RING4, :]
                        if what not in ("x", "query", "memory", "context"):
                            dve.wait_ge(m.work_ready, slot0 + (slot + 1))
                    if what == "scores":
                        dve.wait_ge(m.st_ready, 2 * n.number + (k + 1))
                        nc.vector.reduce_max(mx[:, k:k + 1], st[:, 0:LE], AX_X).then_inc(m.mx_ready, 1)
                        dve.wait_ge(m.mx_ready, 2 * n.number + (k + 1))
                        nc.vector.tensor_scalar(nm[:, k:k + 1], mx[:, k:k + 1], -(H ** -0.5), None, ALU.mult).then_inc(m.nm_ready, 1)
                    elif what == "x":
                        dve.wait_ge(m.xh_ready, 2 * f.number + (k + 1))
                        nc.vector.tensor_tensor(xl[f.parity][:, k, :], src[:, 0:L], xh[f.parity][:, k, :].bitcast(F32),
                                                ALU.subtract).then_inc(m.work_free, 1)
                    elif what == "query":
                        dve.wait_ge(m.qh_ready, f.number + 1)
                        nc.vector.tensor_tensor(ql[f.parity][:, :], src[:, 0:L], qh[f.parity][:, :].bitcast(F32),
                                                ALU.subtract).then_inc(m.work_free, 1)
                    elif what == "memory":
                        w = chunk_cols(k)
                        dve.wait_ge(m.eh_ready, NJ * f.number + (k + 1))
                        nc.vector.tensor_tensor(el[:, 512 * k:512 * k + w], src[:, 0:w], eh[:, 512 * k:512 * k + w].bitcast(F32),
                                                ALU.subtract).then_inc(m.work_free, 1)
                    elif what == "turn":
                        t, j = divmod(k, NJ)
                        tiles = chunk_tiles(j)
                        rows = tile_rows(tiles[-1])
                        nc.vector.tensor_copy(pt[0:rows, tiles[0]:tiles[-1] + 1, t * P:(t + 1) * P],
                                              src[0:rows, 0:len(tiles) * P].rearrange("p (k q) -> p k q", q=P)).then_inc(m.work_free, 1)
                    elif what == "context":
                        dve.wait_ge(m.exp_done, 2 * n.number + 2)
                        nc.vector.reciprocal(rt[:, :], total[:, :]).then_inc(m.rt_ready, 1)
                        dve.wait_ge(m.tth_ready, n.number + 1)
                        nc.vector.tensor_tensor(ttl[:, :], src[:, 0:L], tth[:, :].bitcast(F32), ALU.subtract).then_inc(m.work_free, 1)
                    elif what == "out":
                        dve.wait_ge(m.rt_ready, n.number + 1)
                        nc.vector.tensor_scalar(cv[n.parity][:, k, :], src[:, 0:H], rt[:, k:k + 1], None, ALU.mult).then_inc(m.cv_ready, 1)
                        nc.vector.scalar_tensor_tensor(gp[:, k, :], src[:, H:2 * H], rt[:, k:k + 1], bg[:, :], ALU.mult,
                                                       ALU.add).then_inc(m.work_free, 1)
                    elif what == "gate":
                        dve.wait_ge(m.work_free, slot0 + (slot + RING4))
                        nc.vector.tensor_tensor(gs[n.parity][:, k, :], src[:, 0:H], gp[:, k, :], ALU.add).then_inc(m.work_free, 1)
                    elif what == "fuse":
                        dve.wait_ge(m.th_ready, 2 * b.number + 2)
                        for t in range(T):
                            nc.vector.scalar_tensor_tensor(fz[:, t, :], th[:, t, :], 1.0, cv[b.parity][:, t, :], ALU.add,
                                                           ALU.mult).then_inc(m.fz_ready, 1)
                        dve.wait_ge(m.fz_ready, 2 * b.number + 2)
                        for t in range(T):
                            nc.vector.scalar_tensor_tensor(fu[:, t, :], fz[:, t, :], 0.5, g.x[:, 2 * b.number + t, :], ALU.mult,
                                                           ALU.add).then_inc(m.fu_ready, 1)
                    elif what == "finish":
                        dve.wait_ge(m.rstd_ready, b.number + 1)
                        dve.wait_ge(m.y_free, b.number + 1)
                        for t in range(T):
                            nc.vector.scalar_tensor_tensor(y[b.parity][:, t, :], fu[:, t, :], rstd[:, t:t + 1], nw[:, :], ALU.mult,
                                                           ALU.mult).then_inc(m.y_ready, 1)

            iterations4(dve, one)

        @block.tensor
        def _(pe):
            pe.wait_ge(m.w4_loaded, 64)
            for f in range(4):
                for o in range(C):
                    last = nc.tensor.transpose(st[:, f * H + o * P:f * H + o * P + P], raw_g[:, o, f * P:(f + 1) * P], ident)
                last.then_inc(m.gt_psum, 1)
            for c in range(C):
                last = nc.tensor.transpose(st[:, 2 * 512 + c * P:2 * 512 + c * P + P], raw_m[:, c, :], ident)
            last.then_inc(m.m_psum, 1)
            pe.wait_ge(m.gt_ready, 1)
            for c in range(C):
                last = nc.tensor.matmul(st[:, 3 * 512:3 * 512 + H], raw_m[:, c, :], gt[:, C + c, :], start=(c == 0), stop=(c == C - 1))
            last.then_inc(m.m_psum, 1)
            pe.wait_ge(m.w4_lo, 3)
            pe.wait_ge(m.pad_ready, 2)

            def product(dst, terms):
                for i, (stat, mv) in enumerate(terms):
                    last = nc.tensor.matmul(dst, stat, mv, start=(i == 0), stop=(i == len(terms) - 1))
                return last

            def one(f, n, b, parts, slot0, bank0):
                for what, k, slot in PLAN4[parts][0]:
                    if slot is not None:
                        dst = work[:, (bank0 + slot) % RING4, :]
                    if what == "scores":
                        if k == 0:
                            pe.wait_ge(m.work_free, slot0 + before_attend(parts))
                        if not (parts == (1, 1, 0) and k == 0):
                            pe.wait_ge(m.exp_done, 2 * n.number + k)
                        q = slice(k * P, (k + 1) * P)
                        for j in range(NJ):
                            w = chunk_cols(j) + chunk_cols(j) % 2
                            last = product(st[:, 512 * j:512 * j + w],
                                           three(((qh[n.parity][:, q], ql[n.parity][:, q]),
                                                  (eh[:, 512 * j:512 * j + w], el[:, 512 * j:512 * j + w]))))
                        last.then_inc(m.st_ready, 1)
                    elif what == "x":
                        pe.wait_ge(m.xc_ready, f.number + 1)
                        pe.wait_ge(m.work_free, slot0 + (slot + 1))
                        for t in range(T):
                            last = nc.tensor.transpose(dst[:, t * P:(t + 1) * P], xc[:, t, k * P:(k + 1) * P], ident)
                        last.then_inc(m.work_ready, 1)
                    elif what == "query":
                        pe.wait_ge(m.work_free, slot0 + (slot + RING4))
                        terms = []
                        for c in range(C):
                            terms += three(((m_hi[:, c, :], m_lo[:, c, :]), (xh[f.parity][:, c, :], xl[f.parity][:, c, :])))
                        product(dst[:, 0:L], terms).then_inc(m.work_ready, 1)
                    elif what == "memory":
                        if k == 0:
                            pe.wait_ge(enc_loaded[f.parity], 32 * f.before + 32)
                        pe.wait_ge(m.work_free, slot0 + (slot + 1))
                        for a, kt in enumerate(chunk_tiles(k)):
                            rows = tile_rows(kt)
                            last = nc.tensor.transpose(dst[:, a * P:a * P + rows], enc[f.parity][0:rows, kt, :], ident[0:rows, 0:rows])
                        last.then_inc(m.work_ready, 1)
                    elif what == "turn":
                        t, j = divmod(k, NJ)
                        pe.wait_ge(m.exp_done, 2 * n.number + (t + 1))
                        pe.wait_ge(m.work_free, slot0 + (slot + 1))
                        for a, kt in enumerate(chunk_tiles(j)):
                            rows = tile_rows(kt)
                            last = nc.tensor.transpose(dst[0:rows, a * P:(a + 1) * P], pr[:, t, kt * P:kt * P + rows], ident)
                        last.then_inc(m.work_ready, 1)
                    elif what == "context":
                        pe.wait_ge(m.work_free, slot0 + (slot + RING4))
                        for kt in range(KT):
                            rows = tile_rows(kt)
                            last = nc.tensor.matmul(dst[:, 0:L], enc[n.parity][0:rows, kt, :], pt[0:rows, kt, :],
                                                    start=(kt == 0), stop=(kt == KT - 1))
                        last.then_inc(m.work_ready, 1)
                        pe.wait_ge(m.work_ready, slot0 + (slot + 1))
                        pe.sem_inc(m.enc_free, 2)
                    elif what == "out":
                        q = slice(k * P, (k + 1) * P)
                        pe.wait_ge(m.work_free, slot0 + (slot + (RING4 if k == 0 else 1)))
                        product(dst, three(((tth[:, q], ttl[:, q]), (mc_hi[:, :], mc_lo[:, :])))).then_inc(m.work_ready, 1)
                    elif what == "gate":
                        q = slice(k * P, (k + 1) * P)
                        pe.wait_ge(m.work_free, slot0 + (slot + 1))
                        terms = []
                        for c in range(C):
                            terms += three(((xh[n.parity][:, c, q], xl[n.parity][:, c, q]), (g_hi[:, c, :], g_lo[:, c, :])))
                        product(dst[:, 0:H], terms).then_inc(m.work_ready, 1)

            def before_attend(parts):
                return RING4 if parts == (1, 1, 0) else RING4 - 4

            iterations4(pe, one)


def build(nc, io):
    with ExitStack() as ctx:
        sb, _ = allocator(nc, ctx)
        shared = namedtuple("Shared", "const x tok tok_next vm nvm minus_half eps zero one")
        g = shared(
            const=sb("const", [P, NCONST]),
            x=sb("x", [P, B * T, H]),
            tok=sb("tok", [P, B * T], I32),
            tok_next=sb("tok_next", [P, B * T], I32),
            vm=sb("vm", [P, B * T]),
            nvm=sb("nvm", [P, B * T]),
            minus_half=sb("minus_half", [P, T]),
            eps=sb("eps", [P, T]),
            zero=sb("zero", [P, 1]),
            one=sb("one", [P, 1]),
        )
        self_attention(nc, g, io)
        cross_attention(nc, g, io)
        mlp(nc, g, io)
        fusion(nc, g, io)


_INS = ["x", "ctx_1024", "pos_1xS", "mask_BxS_ik0", "L0_xattn_ln_in_w", "L0_xattn_ln_post_attn_w",
        "L0_xattn_ln_post_cross_w", "L0_xattn_v_qkv", "L0_xattn_l_qkv", "L0_xattn_v_dense", "L0_xattn_l_dense",
        "L0_xattn_cq_w", "L0_xattn_ckv_w", "L0_xattn_cdense_w", "L0_xattn_v_gate", "L0_xattn_v_up", "L0_xattn_v_down",
        "L0_xattn_l_gate", "L0_xattn_l_up", "L0_xattn_l_down", "L1_xattn_W_mem", "L1_xattn_W_gate",
        "L1_xattn_b_gate", "L1_xattn_norm_w"]


def kernel(**inputs):
    import concourse.bacc as _bacc
    from concourse.bass_utils import run_bass_kernel_spmd as _run

    nc = _bacc.Bacc("TRN2", target_bir_lowering=False, num_devices=1)
    arrays, io = {}, {}
    for name in _INS:
        a = np.ascontiguousarray(inputs[name])
        arrays[f"in_{name}"] = a
        io[name] = nc.dram_tensor(f"in_{name}", a.shape, mybir.dt.from_np(a.dtype), kind="ExternalInput").ap()
    arrays["in_constants"] = constants()
    io["const"] = nc.dram_tensor("in_constants", (P, NCONST), F32, kind="ExternalInput").ap()
    io["out"] = nc.dram_tensor("out_0", (B, L, H), F32, kind="ExternalOutput").ap()
    build(nc, io)
    r = _run(nc, [arrays], core_ids=[0])
    return r.results[0]["out_0"]
```

```python
from collections import namedtuple
from contextlib import ExitStack

import numpy as np

import concourse.bass as bass
from concourse import mybir

ALU = mybir.AluOpType
ACT = mybir.ActivationFunctionType
F32 = mybir.dt.float32
F32R = mybir.dt.float32r
BF16 = mybir.dt.bfloat16
I32 = mybir.dt.int32
AX_X = mybir.AxisListType.X

P = 128
B, L, H = 8, 256, 256
LE, CH = 1601, 128
NH = 16
HD, CHD = H // NH, CH // NH
FF = 688
EPS = 1e-6
T = L // P
C = H // P
KT = (LE + P - 1) // P
LAST = LE - (KT - 1) * P
NJ = (KT + 3) // 4
EVEN = LAST + LAST % 2
MASKED = -(2.0 ** 120)

ID0 = 0
MS0 = ID0 + P
CS0 = MS0 + NH
PO0 = CS0 + T * 2 * HD
EC0 = PO0 + T
MC0 = EC0 + 4 * 32
CM0 = MC0 + 4
NCONST = CM0 + 2 * P


def chunk_tiles(j):
    return range(4 * j, min(4 * j + 4, KT))


def tile_rows(kt):
    return P if kt < KT - 1 else LAST


def chunk_cols(j):
    return sum(tile_rows(kt) for kt in chunk_tiles(j))


def constants():
    c = np.zeros((P, NCONST), np.float32)
    c[:, ID0:ID0 + P] = np.eye(P, dtype=np.float32)
    for h in range(NH):
        c[96 + h, MS0 + h] = c[112 + h, MS0 + h] = 1.0
    inv = np.float32(1.0) / np.power(np.float32(10000.0), np.arange(0, HD, 2, dtype=np.float32) / np.float32(HD))
    ang = np.arange(L, dtype=np.float32)[:, None] * inv.astype(np.float32)[None, :]
    cos, sin = np.cos(ang).astype(np.float32), np.sin(ang).astype(np.float32)
    tab = np.concatenate([cos, cos, -sin, sin], axis=1)
    for t in range(T):
        c[:, CS0 + t * 32:CS0 + t * 32 + 32] = tab[t * P:(t + 1) * P]
        c[:, PO0 + t] = np.arange(t * P, (t + 1) * P)
    for parity in range(2):
        for kg in range(4):
            for e in range(2):
                for d in range(CHD):
                    col = 16 * parity + CHD * e + d
                    c[32 * kg + 9 * e + d, EC0 + 32 * parity + col] = 1.0
                    c[32 * kg + 9 * e + 8, EC0 + 64 + 32 * parity + col] = 1.0
    for j in range(4):
        c[:, MC0 + j] = (np.arange(P) % 32) // CHD == j
    k = np.arange(P)
    c[:, CM0:CM0 + P] = np.where(k[None, :] > k[:, None], MASKED, 0.0)
    c[:, CM0 + P:CM0 + 2 * P] = np.where(k[:, None] > k[None, :], MASKED, 0.0)
    return c


def allocator(nc, ctx):
    def sb(name, shape, dt=F32):
        return ctx.enter_context(nc.sbuf_tensor(name, shape, dt))

    def ps(name, shape, dt=F32):
        return ctx.enter_context(nc.psum_tensor(name, shape, dt))

    return sb, ps


def semaphores(nc, ctx, *names):
    return namedtuple("Semaphores", names)(*[ctx.enter_context(nc.semaphore(name)) for name in names])


def split_hi(nc, hi, src):
    return nc.vector.tensor_copy(hi, src)


def split_lo(nc, lo, src, hi):
    return nc.vector.tensor_tensor(lo, src, hi.bitcast(F32), ALU.subtract)


def three(hi_lo_pairs):
    (sh, sl), (mh, ml) = hi_lo_pairs
    return [(sh, mh), (sh, ml), (sl, mh)]



RING1 = 3
MAXIMA = [(0, 4 * i, 4) for i in range(4)] + [(1, 2 * i, 2) for i in range(8)]


def plan1(ahead, front, attend):
    out, slots = [], 0

    def put(what, k=0, slot=True):
        nonlocal slots
        out.append((what, k, slots if slot else None))
        slots += slot

    for t in range(T):
        if front:
            put("queries_keys", t)
        if attend:
            for k in range(len(MAXIMA) // T):
                put("max", len(MAXIMA) // T * t + k)
    if attend:
        put("minus", 0, False)
    if front:
        put("values", 0)
    if attend:
        for k in range(2):
            put("max_rows", k)
    if front:
        put("turn", 0)
    for k in range(NH // 2):
        if attend:
            put("scores", k, False)
        if k == 1:
            if front:
                put("turn", 1)
            if ahead:
                put("norm", 0, False)
        if attend and k == NH // 4:
            put("context", 0, False)
    if attend:
        put("context", 1, False)
    if front:
        put("values", 1)
    if ahead:
        for e in range(2):
            put("inputs", e)
    if attend:
        for t in range(T):
            put("out", t)
    return out, slots


PLAN1 = {k: plan1(*k) for k in ((1, 0, 0), (1, 1, 0), (1, 1, 1), (0, 1, 1), (0, 0, 1))}
Numbered = namedtuple("Numbered", "number parity")


def iterations1(eng, one):
    first = 0
    per = PLAN1[1, 1, 1][1]
    assert per % RING1 == 0

    def run(pair, s, parts, slot0, bank0):
        one(Numbered(2 * pair + (s + 2), s), Numbered(2 * pair + (s + 1), 1 - s), Numbered(2 * pair + s, s), parts, slot0, bank0)

    for s, parts in enumerate(((1, 0, 0), (1, 1, 0))):
        run(-1, s, parts, first, first % RING1)
        first += PLAN1[parts][1]
    with eng.Fori(0, B // 2 - 1) as pair:
        for s in range(2):
            run(pair, s, (1, 1, 1), (2 * per) * pair + (first + per * s), first % RING1)
    first += per * (B - 2)
    for s, parts in enumerate(((0, 1, 1), (0, 0, 1))):
        run(B // 2 - 1, s, parts, first, first % RING1)
        first += PLAN1[parts][1]


def self_attention(nc, g, io):
    with ExitStack() as ctx:
        sb, ps = allocator(nc, ctx)
        ident16 = sb("ident16", [P, P], BF16)
        causal = sb("causal", [P, 2 * P], BF16)
        work = ps("work1", [P, RING1, 512])
        st = ps("st1", [P, 2, 2, 512])
        nd = ps("nd1", [P, 2, 256])
        wq_hi = sb("wqkv_hi", [P, 2, C, 3 * H], F32R)
        wq_lo = sb("wqkv_lo", [P, 2, C, 3 * H], F32R)
        wd_hi = sb("wdense_hi", [P, C, 2 * H], F32R)
        wd_lo = sb("wdense_lo", [P, C, 2 * H], F32R)
        lnw = sb("ln_in_w", [P, C])
        posr = sb("positions", [P, L], I32)
        posf = sb("positions_f", [P, L])
        pick = sb("position_picks", [P, T, L])
        cs = sb("cos_sin", [P, T, 2 * HD])
        vones = sb("ones_by_parity", [P, 2, 32])
        sq = sb("squares1", [P, T, H])
        ssq = sb("mean_squares1", [P, T])
        var = sb("variance1", [P, T])
        rstd = sb("rstd1", [P, T])
        rex = sb("rstd_by_expert1", [P, 2, T])
        xe = sb("x_by_expert1", [P, 2, T, H])
        xh = sb("xt_hi1", [P, 2, C, L], F32R)
        xl = sb("xt_lo1", [P, 2, C, L], F32R)
        rc = sb("rot_cos", [P, 2 * H])
        rs = sb("rot_sin", [P, 2 * H])
        qk = sb("qk_rotated", [P, T, 2 * H])
        qkh = sb("qkt_hi", [P, 4, L], F32R)
        qkl = sb("qkt_lo", [P, 4, L], F32R)
        vs = [sb(f"v_self_{s}", [P, T, NH // 2, 64]) for s in range(2)]
        qm = [sb(f"q_rows1_{s}", [P, NH, L], F32R) for s in range(2)]
        ks = [sb(f"k_rows1_{s}", [P, NH // 2, L], F32R) for s in range(2)]
        mx = sb("max1", [P, T, NH])
        mn = sb("neg_max1", [P, T, P], F32R)
        pr = sb("probs1", [P, 2, 8, 384])
        rden = sb("rden1", [P, 256])
        cx = sb("ctx1", [P, C, L])
        cxh = sb("ctx_hi1", [P, C, L], F32R)
        cxl = sb("ctx_lo1", [P, C, L], F32R)
        stage = pr[:, :, :, :].rearrange("p a b n -> p (a b n)")
        staged = [stage[:, i * C * 3 * H:(i + 1) * C * 3 * H].rearrange("p (c n) -> p c n", c=C) for i in range(2)]
        staged_d = [stage[:, (6 + i) * C * H:(7 + i) * C * H].rearrange("p (c n) -> p c n", c=C) for i in range(2)]
        m = semaphores(nc, ctx, "wq_loaded", "wd_loaded", "w1_hi", "w1_lo", "in_loaded", "table_ready", "pos_f",
                       "picks", "cs_psum", "v_zero", "v_ones", "rows_init", "x_loaded", "work_ready", "work_free",
                       "ssq_ready", "var_ready", "rstd_ready", "rex_ready", "xe_ready", "xh_ready", "xl_ready",
                       "rot_parts", "rot_ready", "qkh_ready", "qkl_ready", "v_ready", "q_rows_ready", "k_rows_ready",
                       "k_rows_begun", "mh_ready", "ml_ready", "max_rows_part", "st_ready", "exp_done", "nd_ready",
                       "rden_ready", "ctx_ready", "cxh_ready", "cxl_ready", "res_v", "const_ready", "vm_ready")
        ident = g.const[:, ID0:ID0 + P]
        Q_ROWS, K_ROWS = 24 * 16, 12 * 16
        block = ctx.enter_context(nc.Block())

        @block.sync
        def _(sp):
            sp.dma_start(g.const[:, :], io["const"]).then_inc(m.in_loaded, 16)
            sp.dma_start(lnw[:, :], io["L0_xattn_ln_in_w"].rearrange("(c p) -> p c", p=P),
                         allow_slow_non_contiguous=True).then_inc(m.in_loaded, 16)
            for i, name in enumerate(("L0_xattn_v_qkv", "L0_xattn_l_qkv")):
                sp.dma_start(staged[i], io[name].rearrange("(c p) n -> p c n", p=P)).then_inc(m.wq_loaded, 16)
            sp.dma_start(posr[:, :], io["pos_1xS"].broadcast_to([P, L])).then_inc(m.in_loaded, 16)
            tt = io["mask_BxS_ik0"].rearrange("b (t p) -> p b t", p=P)
            sp.dma_start(g.tok[:, :].rearrange("p (b t) -> p b t", t=T), tt, allow_slow_non_contiguous=True).then_inc(m.in_loaded, 16)
            sp.wait_ge(m.const_ready, 1)
            nxt = io["mask_BxS_ik0"][:, 1:L]
            dst = g.tok_next[:, :].rearrange("p (b t) -> p b t", t=T)
            sp.dma_start(dst[:, :, 0], nxt[:, 0:P].rearrange("b p -> p b"), allow_slow_non_contiguous=True).then_inc(m.in_loaded, 16)
            sp.dma_start(dst[0:P - 1, :, 1], nxt[:, P:L - 1].rearrange("b p -> p b"), allow_slow_non_contiguous=True).then_inc(m.in_loaded, 16)
            for i, name in enumerate(("L0_xattn_v_dense", "L0_xattn_l_dense")):
                sp.dma_start(staged_d[i], io[name].rearrange("(c p) n -> p c n", p=P)).then_inc(m.wd_loaded, 16)

            def one(g2, f, b, parts, slot0, bank0):
                if not parts[1]:
                    return
                sp.wait_ge(m.qkl_ready, 2 * f.number + 1)
                qv = qm[f.parity][:, :, :].rearrange("p (a r e) n -> p a r e n", a=2, e=2).bitcast(F32)
                for blk, part in enumerate((qkh, qkh, qkl)):
                    for r in range(4):
                        for e in range(2):
                            to, src = 32 * blk + 16 * e, 32 * r + 16 * e
                            sp.dma_start(qv[to:to + 16, :, r, e, :],
                                         part[src:src + 16, 0:2, :].bitcast(F32)).then_inc(m.q_rows_ready, 16)

            iterations1(sp, one)

        @block.gpsimd
        def _(pool):
            pool.dma_start(g.x[:, 0:T, :], io["x"][0].rearrange("(t p) n -> p t n", p=P)).then_inc(m.x_loaded, 16)
            pool.dma_start(g.x[:, T:B * T, :], io["x"][1:B].rearrange("b (t p) n -> p (b t) n", p=P)).then_inc(m.x_loaded, 16)
            for s in range(2):
                nc.gpsimd.memset(vs[s][:, :, :, :], 0.0).then_inc(m.v_zero, 1)
            nc.gpsimd.memset(vones[:, :, :], 0.0).then_inc(m.v_zero, 1)
            pool.wait_ge(m.v_zero, 3)
            nc.gpsimd.memset(vones[:, 0, 0:16], 1.0).then_inc(m.v_ones, 1)
            nc.gpsimd.memset(vones[:, 1, 16:32], 1.0).then_inc(m.v_ones, 1)
            pool.wait_ge(m.const_ready, 5)

            def one(g2, f, b, parts, slot0, bank0):
                for what, k, slot in PLAN1[parts][0]:
                    if what == "norm":
                        pool.wait_ge(m.ssq_ready, 2 * g2.number + 2)
                        nc.gpsimd.tensor_tensor(var[:, :], ssq[:, :], g.eps[:, :], ALU.add).then_inc(m.var_ready, 1)
                        pool.wait_ge(m.var_ready, g2.number + 1)
                        nc.gpsimd.tensor_tensor(rstd[:, :], var[:, :], g.minus_half[:, :], ALU.pow).then_inc(m.rstd_ready, 1)
                if parts[1]:
                    pool.wait_ge(m.qkl_ready, 2 * f.number + 2)
                    pool.sem_inc(m.k_rows_begun, 1)
                    kv = ks[f.parity][:, :, :].rearrange("p (a r) n -> p a r n", a=2).bitcast(F32)
                    for blk, part in enumerate((qkh, qkl, qkh)):
                        for r in range(4):
                            pool.dma_start(kv[32 * blk:32 * blk + 32, :, r, :],
                                           part[32 * r:32 * r + 32, 2:4, :].bitcast(F32)).then_inc(m.k_rows_ready, 16)

            iterations1(pool, one)

        @block.scalar
        def _(act):
            act.wait_ge(m.x_loaded, 32)
            act.wait_ge(m.in_loaded, 96)

            def one(g2, f, b, parts, slot0, bank0):
                for what, k, slot in PLAN1[parts][0]:
                    if slot is not None:
                        src = work[:, (bank0 + slot) % RING1, :]
                    if what == "norm":
                        for t in range(T):
                            nc.scalar.activation(sq[:, t, :], g.x[:, 2 * g2.number + t, :], ACT.Square, scale=H ** -0.5,
                                                 accum_out=ssq[:, t:t + 1]).then_inc(m.ssq_ready, 1)
                    elif what == "inputs":
                        act.wait_ge(m.work_ready, slot0 + (slot + 1))
                        for c in range(C):
                            nc.scalar.activation(xh[:, k, c, :], src[:, c * L:(c + 1) * L], ACT.Copy,
                                                 scale=lnw[:, c:c + 1]).then_inc(m.xh_ready, 1)
                    elif what == "turn":
                        act.wait_ge(m.work_ready, slot0 + (slot + 1))
                        nc.scalar.activation(qkh[:, 2 * k:2 * k + 2, :], src.rearrange("p (c n) -> p c n", c=2),
                                             ACT.Copy).then_inc(m.qkh_ready, 1)
                    elif what == "scores":
                        act.wait_ge(m.st_ready, 8 * b.number + (k + 1))
                        if k % 4 == 0:
                            act.wait_ge(m.nd_ready, 2 * b.number + (k // 4 + 1))
                        nc.scalar.activation(pr[:, k // 4, 2 * (k % 4):2 * (k % 4) + 2, :], st[:, k % 2, :, 0:384],
                                             ACT.Exp, scale=HD ** -0.5).then_inc(m.exp_done, 1)
                        if k == 6:
                            act.wait_ge(m.ctx_ready, 2 * b.number + 1)
                            nc.scalar.activation(cxh[:, 0, :], cx[:, 0, :], ACT.Copy).then_inc(m.cxh_ready, 1)
                    elif what == "context" and k == 1:
                        act.wait_ge(m.ctx_ready, 2 * b.number + 2)
                        nc.scalar.activation(cxh[:, 1, :], cx[:, 1, :], ACT.Copy).then_inc(m.cxh_ready, 1)

            iterations1(act, one)

        @block.vector
        def _(dve):
            nc.vector.memset(g.tok_next[:, :], 0).then_inc(m.const_ready, 1)
            nc.vector.memset(g.minus_half[:, :], -0.5).then_inc(m.const_ready, 1)
            nc.vector.memset(g.eps[:, :], EPS).then_inc(m.const_ready, 1)
            nc.vector.memset(g.zero[:, :], 0.0).then_inc(m.const_ready, 1)
            nc.vector.memset(g.one[:, :], 1.0).then_inc(m.const_ready, 1)
            dve.wait_ge(m.const_ready, 5)
            nc.vector.tensor_copy(mn[:, :, :], g.zero[:, 0:1].unsqueeze(2).broadcast_to([P, T, P])).then_inc(m.rows_init, 1)
            for s in range(2):
                nc.vector.tensor_copy(qm[s][:, :, :], g.zero[:, 0:1].unsqueeze(2).broadcast_to([P, NH, L])).then_inc(m.rows_init, 1)
                nc.vector.tensor_copy(ks[s][96:128, :, :], g.one[96:128, 0:1].unsqueeze(2).broadcast_to([32, NH // 2, L])).then_inc(m.rows_init, 1)
            dve.wait_ge(m.in_loaded, 96)
            nc.vector.tensor_copy(causal[:, :], g.const[:, CM0:CM0 + 2 * P]).then_inc(m.table_ready, 1)
            nc.vector.tensor_copy(ident16[:, :], ident).then_inc(m.table_ready, 1)
            nc.vector.tensor_scalar(g.nvm[:, :], g.tok[:, :], 1.0, None, ALU.is_equal).then_inc(m.vm_ready, 1)
            dve.wait_ge(m.vm_ready, 1)
            nc.vector.scalar_tensor_tensor(g.vm[:, :], g.tok_next[:, :], 1.0, g.nvm[:, :], ALU.is_equal,
                                           ALU.mult).then_inc(m.vm_ready, 1)
            dve.wait_ge(m.vm_ready, 2)
            nc.vector.tensor_scalar(g.nvm[:, :], g.vm[:, :], -1.0, 1.0, ALU.mult, ALU.add).then_inc(m.vm_ready, 1)
            nc.vector.tensor_copy(posf[:, :], posr[:, :]).then_inc(m.pos_f, 1)
            dve.wait_ge(m.pos_f, 1)
            for t in range(T):
                nc.vector.tensor_scalar(pick[:, t, :], posf[:, :], g.const[:, PO0 + t:PO0 + t + 1], None,
                                        ALU.is_equal).then_inc(m.picks, 1)
            dve.wait_ge(m.cs_psum, 1)
            nc.vector.tensor_copy(cs[:, :, :], nd[:, 0, 0:64].rearrange("p (t n) -> p t n", t=T)).then_inc(m.table_ready, 1)
            for i in range(2):
                dve.wait_ge(m.wq_loaded, 32)
                split_hi(nc, wq_hi[:, i, :, :], staged[i]).then_inc(m.w1_hi, 1)
                dve.wait_ge(m.w1_hi, i + 1)
                split_lo(nc, wq_lo[:, i, :, :], staged[i], wq_hi[:, i, :, :]).then_inc(m.w1_lo, 1)
            dve.wait_ge(m.wd_loaded, 32)
            for i in range(2):
                split_hi(nc, wd_hi[:, :, i * H:(i + 1) * H], staged_d[i]).then_inc(m.w1_hi, 1)
            dve.wait_ge(m.w1_hi, 4)
            for i in range(2):
                split_lo(nc, wd_lo[:, :, i * H:(i + 1) * H], staged_d[i], wd_hi[:, :, i * H:(i + 1) * H]).then_inc(m.w1_lo, 1)
            dve.wait_ge(m.table_ready, 3)
            dve.wait_ge(m.vm_ready, 3)
            dve.wait_ge(m.v_zero, 3)
            dve.wait_ge(m.rows_init, 5)
            dve.sem_inc(m.work_free, RING1)

            def one(g2, f, b, parts, slot0, bank0):
                for what, k, slot in PLAN1[parts][0]:
                    if slot is not None:
                        src = work[:, (bank0 + slot) % RING1, :]
                    if what == "norm":
                        dve.wait_ge(m.rstd_ready, g2.number + 1)
                        for e, chosen in enumerate((g.vm, g.nvm)):
                            nc.vector.tensor_tensor(rex[:, e, :], rstd[:, :], chosen[:, bass.ds(2 * g2.number, 2)],
                                                    ALU.mult).then_inc(m.rex_ready, 1)
                        dve.wait_ge(m.rex_ready, 2 * g2.number + 2)
                        for e in range(2):
                            for t in range(T):
                                nc.vector.tensor_scalar(xe[:, e, t, :], g.x[:, 2 * g2.number + t, :], rex[:, e, t:t + 1], None,
                                                        ALU.mult).then_inc(m.xe_ready, 1)
                    elif what == "inputs":
                        dve.wait_ge(m.xh_ready, 4 * g2.number + (2 * k + 2))
                        for c in range(C):
                            nc.vector.scalar_tensor_tensor(xl[:, k, c, :], src[:, c * L:(c + 1) * L], lnw[:, c:c + 1],
                                                           xh[:, k, c, :].bitcast(F32), ALU.mult,
                                                           ALU.subtract).then_inc(m.xl_ready, 1)
                        dve.wait_ge(m.xl_ready, 4 * g2.number + (2 * k + 2))
                        dve.sem_inc(m.work_free, 1)
                    elif what == "queries_keys":
                        rotate(f, k, src.rearrange("p (h d) -> p h d", d=HD), slot0 + (slot + 1))
                    elif what == "values":
                        dve.wait_ge(m.work_ready, slot0 + (slot + 1))
                        for e in range(2):
                            ins = nc.vector.tensor_copy(vs[f.parity][:, k, :, 48 * e:48 * e + HD],
                                                        src[:, 0:H].rearrange("p (q e d) -> p q e d", e=2, d=HD)[:, :, e, :])
                            ins.then_inc(m.v_ready if e == 0 else m.work_free, 1)
                    elif what == "turn":
                        dve.wait_ge(m.qkh_ready, 2 * f.number + (k + 1))
                        nc.vector.tensor_tensor(qkl[:, 2 * k:2 * k + 2, :], src.rearrange("p (c n) -> p c n", c=2),
                                                qkh[:, 2 * k:2 * k + 2, :].bitcast(F32), ALU.subtract).then_inc(m.qkl_ready, 1)
                        dve.wait_ge(m.qkl_ready, 2 * f.number + (k + 1))
                        dve.sem_inc(m.work_free, 1)
                    elif what == "max":
                        t, h0, n = MAXIMA[k]
                        dve.wait_ge(m.work_ready, slot0 + (slot + 1))
                        nc.vector.reduce_max(mx[:, t, h0:h0 + n], src.rearrange("p (h k) -> p h k", h=n),
                                             AX_X).then_inc(m.work_free, 1)
                        maxima_slot = slot
                    elif what == "minus":
                        dve.wait_ge(m.work_free, slot0 + (maxima_slot + 1 + RING1))
                        nc.vector.tensor_scalar(mn[:, :, 96:112], mx[:, :, :], -1.0, None, ALU.mult).then_inc(m.mh_ready, 1)
                        dve.wait_ge(m.mh_ready, b.number + 1)
                        nc.vector.scalar_tensor_tensor(mn[:, :, 112:128], mx[:, :, :], -1.0, mn[:, :, 96:112].bitcast(F32),
                                                       ALU.mult, ALU.subtract).then_inc(m.ml_ready, 1)
                    elif what == "max_rows":
                        dve.wait_ge(m.work_ready, slot0 + (slot + 1))
                        for i in range(2):
                            hs = slice((2 * k + i) * NH // 4, (2 * k + i + 1) * NH // 4)
                            ins = nc.vector.tensor_tensor(
                                qm[b.parity][96:128, hs, :], src[96:128, 0:L].unsqueeze(1).broadcast_to([32, NH // 4, L]),
                                g.const[96:128, MS0 + hs.start:MS0 + hs.stop].unsqueeze(2).broadcast_to([32, NH // 4, L]),
                                ALU.mult)
                            ins.then_inc(m.max_rows_part if i == 0 else m.work_free, 1)
                    elif what == "context":
                        dve.wait_ge(m.nd_ready, 2 * b.number + (k + 1 + 2))
                        nc.vector.reciprocal(rden[:, :], nd[:, 1, :]).then_inc(m.rden_ready, 1)
                        dve.wait_ge(m.rden_ready, 2 * b.number + (k + 1))
                        nc.vector.tensor_tensor(cx[:, k, :], nd[:, 0, :], rden[:, :], ALU.mult).then_inc(m.ctx_ready, 1)
                        if k == 1:
                            for c in range(C):
                                dve.wait_ge(m.cxh_ready, 2 * b.number + (c + 1))
                                split_lo(nc, cxl[:, c, :], cx[:, c, :], cxh[:, c, :]).then_inc(m.cxl_ready, 1)
                    elif what == "out":
                        dve.wait_ge(m.work_ready, slot0 + (slot + 1))
                        xt = g.x[:, 2 * b.number + k, :]
                        nc.vector.scalar_tensor_tensor(xt, src[:, 0:H], g.vm[:, bass.ds(2 * b.number + k, 1)], xt, ALU.mult,
                                                       ALU.add).then_inc(m.res_v, 1)
                        dve.wait_ge(m.res_v, 2 * b.number + (k + 1))
                        nc.vector.scalar_tensor_tensor(xt, src[:, H:2 * H], g.nvm[:, bass.ds(2 * b.number + k, 1)], xt,
                                                       ALU.mult, ALU.add).then_inc(m.work_free, 1)

            def rotate(f, t, src, ready):
                dve.wait_ge(m.work_ready, ready)
                if t:
                    dve.wait_ge(m.rot_ready, 2 * f.number + t)
                half = HD // 2
                rcv = rc[:, :].rearrange("p (h d) -> p h d", d=HD)
                rsv = rs[:, :].rearrange("p (h d) -> p h d", d=HD)
                cosb = cs[:, t:t + 1, 0:HD].broadcast_to([P, 2 * NH, HD])
                sina = cs[:, t:t + 1, HD:HD + half].broadcast_to([P, 2 * NH, half])
                sinb = cs[:, t:t + 1, HD + half:2 * HD].broadcast_to([P, 2 * NH, half])
                nc.vector.tensor_tensor(rcv, src, cosb, ALU.mult).then_inc(m.rot_parts, 1)
                nc.vector.tensor_tensor(rsv[:, :, 0:half], src[:, :, half:HD], sina, ALU.mult).then_inc(m.rot_parts, 1)
                nc.vector.tensor_tensor(rsv[:, :, half:HD], src[:, :, 0:half], sinb, ALU.mult).then_inc(m.work_free, 1)
                dve.wait_ge(m.rot_parts, 4 * f.number + (2 * t + 2))
                dve.wait_ge(m.work_free, ready + RING1)
                nc.vector.tensor_tensor(qk[:, t, :], rc[:, :], rs[:, :], ALU.add).then_inc(m.rot_ready, 1)

            iterations1(dve, one)

        @block.tensor
        def _(pe):
            pe.sem_inc(m.nd_ready, 2)
            pe.wait_ge(m.picks, 2)
            for t in range(T):
                for u in range(T):
                    last = nc.tensor.matmul(nd[:, 0, 32 * t:32 * t + 32], pick[:, u, t * P:(t + 1) * P],
                                            g.const[:, CS0 + 32 * u:CS0 + 32 * u + 32], start=(u == 0), stop=(u == T - 1))
            last.then_inc(m.cs_psum, 1)
            pe.wait_ge(m.w1_lo, 4)
            pe.wait_ge(m.table_ready, 3)
            pe.wait_ge(m.v_ones, 2)
            pe.wait_ge(m.rows_init, 5)

            def product(dst, terms):
                for i, (stat, mv) in enumerate(terms):
                    last = nc.tensor.matmul(dst, stat, mv, start=(i == 0), stop=(i == len(terms) - 1))
                return last

            def project(dst, t, a, w):
                terms = []
                for e in range(2):
                    for c in range(C):
                        terms += three(((xh[:, e, c, t * P:(t + 1) * P], xl[:, e, c, t * P:(t + 1) * P]),
                                        (wq_hi[:, e, c, a:a + w], wq_lo[:, e, c, a:a + w])))
                return product(dst[:, 0:w], terms)

            def one(g2, f, b, parts, slot0, bank0):
                for what, k, slot in PLAN1[parts][0]:
                    if slot is not None:
                        dst = work[:, (bank0 + slot) % RING1, :]
                    if what == "inputs":
                        pe.wait_ge(m.xe_ready, 4 * g2.number + (2 * k + 2))
                        pe.wait_ge(m.work_free, slot0 + (slot + 1))
                        for t in range(T):
                            for c in range(C):
                                last = nc.tensor.transpose(dst[:, c * L + t * P:c * L + t * P + P],
                                                           xe[:, k, t, c * P:(c + 1) * P], ident)
                        last.then_inc(m.work_ready, 1)
                    elif what == "queries_keys":
                        if k == 0:
                            pe.wait_ge(m.xl_ready, 4 * f.number + 4)
                        pe.wait_ge(m.work_free, slot0 + (slot + 1))
                        project(dst, k, 0, 2 * H).then_inc(m.work_ready, 1)
                    elif what == "values":
                        pe.wait_ge(m.work_free, slot0 + (slot + 1))
                        project(dst, k, 2 * H, H).then_inc(m.work_ready, 1)
                    elif what == "turn":
                        pe.wait_ge(m.rot_ready, 2 * f.number + 2)
                        pe.wait_ge(m.work_free, slot0 + (slot + 1))
                        for t in range(T):
                            for c in range(2):
                                last = nc.tensor.transpose(dst[:, c * L + t * P:c * L + t * P + P],
                                                           qk[:, t, (2 * k + c) * P:(2 * k + c + 1) * P], ident)
                        last.then_inc(m.work_ready, 1)
                    elif what == "max":
                        if k == 0:
                            pe.wait_ge(m.q_rows_ready, Q_ROWS * b.number + Q_ROWS)
                            pe.wait_ge(m.k_rows_ready, K_ROWS * b.number + K_ROWS)
                        pe.wait_ge(m.work_free, slot0 + (slot + 1))
                        t, h0, n = MAXIMA[k]
                        w = (t + 1) * P
                        for j in range(n):
                            h = h0 + j
                            nc.tensor.matmul(dst[:, j * w:(j + 1) * w], qm[b.parity][0:96, h, t * P:(t + 1) * P],
                                             ks[b.parity][0:96, h // 2, 0:w], start=True, stop=False, skip_group_check=True)
                            last = nc.tensor.matmul(dst[:, (j + 1) * w - P:(j + 1) * w], ident16[:, :], causal[:, 0:P],
                                                    start=False, stop=True, skip_group_check=True)
                        last.then_inc(m.work_ready, 1)
                    elif what == "max_rows":
                        if k == 0:
                            pe.wait_ge(m.ml_ready, b.number + 1)
                            rows_slot = slot
                        pe.wait_ge(m.work_free, slot0 + (slot + 1))
                        for t in range(T):
                            last = nc.tensor.transpose(dst[:, t * P:(t + 1) * P], mn[:, t, :].bitcast(F32), ident)
                        last.then_inc(m.work_ready, 1)
                    elif what == "scores":
                        if k in (0, 4):
                            pe.wait_ge(m.max_rows_part, 2 * b.number + (k // 4 + 1))
                        if k in (2, 6):
                            pe.wait_ge(m.work_free, slot0 + (rows_slot + k // 4 + 1 + RING1))
                        if k >= 2:
                            pe.wait_ge(m.exp_done, 8 * b.number + (k - 1))
                        scores(b, k)
                    elif what == "context":
                        if k == 0:
                            pe.wait_ge(m.v_ready, 2 * b.number + 2)
                        pe.wait_ge(m.exp_done, 8 * b.number + (4 * k + 4))
                        if k:
                            pe.wait_ge(m.ctx_ready, 2 * b.number + k)
                        context(b, k)
                    elif what == "out":
                        if k == 0:
                            pe.wait_ge(m.cxl_ready, 2 * b.number + 2)
                        pe.wait_ge(m.work_free, slot0 + (slot + 1))
                        terms = []
                        for c in range(C):
                            terms += three(((cxh[:, c, k * P:(k + 1) * P], cxl[:, c, k * P:(k + 1) * P]),
                                            (wd_hi[:, c, :], wd_lo[:, c, :])))
                        product(dst, terms).then_inc(m.work_ready, 1)

            def scores(b, i):
                for k in range(2):
                    h = 2 * i + k
                    for kt in range(2):
                        a = 256 * kt
                        nc.tensor.matmul(st[:, i % 2, k, a:a + 256 - 128 * kt], ks[b.parity][:, h // 2, kt * P:(kt + 1) * P],
                                         qm[b.parity][:, h, kt * P:L], start=True, stop=False, skip_group_check=True)
                        last = nc.tensor.matmul(st[:, i % 2, k, a:a + P], ident16[:, :], causal[:, P:2 * P],
                                                start=False, stop=True, skip_group_check=True)
                last.then_inc(m.st_ready, 1)

            def context(b, c):
                for what in range(2):
                    for kt in range(2):
                        for e in range(2):
                            for q in range(4):
                                lhs = vs[b.parity][:, kt, 4 * c + q, 32 * e:32 * e + 32] if what == 0 else vones[:, e, :]
                                rhs = pr[:, c, 2 * q + e, 256 * kt:384 if kt else 256]
                                last = nc.tensor.matmul(nd[32 * q:32 * q + 32, what, kt * P:L], lhs, rhs,
                                                        start=(kt == 0 and e == 0), stop=(kt == 1 and e == 1),
                                                        tile_position=(0, 32 * q), skip_group_check=True)
                last.then_inc(m.nd_ready, 1)

            iterations1(pe, one)



QUADS = NH // 4
ITEMS = 26
CHUNKS = 13
FRONT = 14
QC = NJ - 1


HOLD, LATE = 4, 2


def plan(front, maxima, probs):
    out, slots = [], 0

    def put(what, k, slot=True):
        nonlocal slots
        out.append((what, k, slots if slot else None))
        slots += slot

    steps = QUADS * CHUNKS
    items = QUADS * ITEMS
    hold = HOLD if probs else 0
    done = fronts = 0
    for s in range(steps):
        if probs:
            put("scores", s, False)
            if s == LATE:
                put("lastcol", QUADS - 1)
        if maxima:
            while done < (s + 1) * (items - hold) // steps:
                put("max", done)
                done += 1
                if done % ITEMS == 0 and done < items:
                    put("maxrow", done // ITEMS - 1, False)
                if done % ITEMS == 6 and done > ITEMS:
                    put("maxcol", done // ITEMS - 1)
        if front and s == 2:
            put("norm", 0, False)
        if front:
            while fronts < FRONT and s >= 3 * fronts + 4:
                put("front", fronts)
                fronts += 1
        if probs and s >= 2:
            put("values", s - 2, False)
    if probs:
        put("values", steps - 2, False)
        put("values", steps - 1, False)
    rest = items - done if maxima else 0

    def some(n):
        nonlocal done, rest
        for _ in range(min(n, rest)):
            put("max", done)
            done += 1
            rest -= 1

    some(2)
    if probs:
        put("sums", 0)
        put("sums", 1)
    some(3)
    if probs:
        put("out", 0)
        put("out", 1)
    some(rest)
    if maxima:
        put("maxrow", QUADS - 1, False)
    return out, slots


PLAN = {k: plan(*k) for k in ((1, 0, 0), (1, 1, 0), (1, 1, 1), (0, 1, 1), (0, 0, 1))}


Batch = namedtuple("Batch", "number parity before")


def iterations(eng, one):
    first = 0
    per = PLAN[1, 1, 1][1]
    assert per % 3 == 0

    def run(pair, s, parts, slot0, bank0):
        one(Batch(2 * pair + (s + 2), s, pair + 1), Batch(2 * pair + (s + 1), 1 - s, pair + s), Batch(2 * pair + s, s, pair),
            parts, slot0, bank0)

    for s, parts in enumerate(((1, 0, 0), (1, 1, 0))):
        run(-1, s, parts, first, first % 3)
        first += PLAN[parts][1]
    with eng.Fori(0, B // 2 - 1) as pair:
        for s in range(2):
            run(pair, s, (1, 1, 1), (2 * per) * pair + (first + per * s), first % 3)
    first += per * (B - 2)
    for s, parts in enumerate(((0, 1, 1), (0, 0, 1))):
        run(B // 2 - 1, s, parts, first, first % 3)
        first += PLAN[parts][1]


def cross_attention(nc, g, io):
    with ExitStack() as ctx:
        sb, ps = allocator(nc, ctx)
        work = ps("work2", [P, 3, 512])
        st = ps("st2", [P, 2, 4, 256])
        acc = ps("acc2", [P, 2, 256])
        wq_hi = sb("wcq_hi", [P, C, CH], F32R)
        wq_lo = sb("wcq_lo", [P, C, CH], F32R)
        wkv_hi = sb("wckv_hi", [P, 2 * CH], F32R)
        wkv_lo = sb("wckv_lo", [P, 2 * CH], F32R)
        wd_hi = sb("wcdense_hi", [P, H], F32R)
        wd_lo = sb("wcdense_lo", [P, H], F32R)
        lnw = sb("ln_cross_w", [P, C])
        ssq = sb("mean_squares2", [P, T])
        var = sb("variance2", [P, T])
        rstd = sb("rstd2", [P, T])
        xs = sb("x_scaled2", [P, T, H])
        xh = sb("xt_hi2", [P, C, L], F32R)
        xl = sb("xt_lo2", [P, C, L], F32R)
        qh = sb("cqt_hi", [P, L], F32R)
        ql = sb("cqt_lo", [P, L], F32R)
        qb = sb("q_quads", [96, QUADS, L], F32R)
        qm = [sb(f"q_rows2_{s}", [P, NH, L], F32R) for s in range(2)]
        ks = [sb(f"k_rows2_{s}", [P, QUADS, LE], F32R) for s in range(2)]
        enc = sb("enc2", [P, KT, CH])
        eh = sb("enct_hi2", [P, 2, 512], F32R)
        el = sb("enct_lo2", [P, 2, 512], F32R)
        kh = sb("ckt_hi", [P, LE], F32R)
        kl = sb("ckt_lo", [P, LE], F32R)
        vraw = enc
        va = [sb(f"v_cross_{s}", [P, KT, NH // 2, 2, 18]) for s in range(2)]
        mp = sb("max_parts2", [P, T, NH, NJ])
        mx = sb("max2", [P, T, NH])
        mn = sb("neg_max2", [P, T, P], F32R)
        mt = sb("neg_max_rows2", [P, L])
        pr = sb("probs2", [P, 4, 4, 256])
        stage = pr[:, 0:2, 0, :]
        accs = sb("acc_sb2", [P, QUADS, 2, 256])
        rden = sb("rden2", [P, L])
        cx = sb("ctx2", [P, L])
        cxh = sb("ctx_hi2", [P, L], F32R)
        cxl = sb("ctx_lo2", [P, L], F32R)
        m = semaphores(nc, ctx, "w2_loaded", "w2_hi", "w2_lo", "v_zeroed", "v_one", "mn_zero", "key_ones",
                       "acc_zero", "work_ready", "work_free", "ssq_ready", "eps_added", "rstd_ready", "xs_ready",
                       "xh_ready", "xl_ready", "qh_ready", "qb_ready", "qm_ready", "enc_loaded", "eh_ready",
                       "kh_ready", "ks_ready00", "ks_ready01", "ks_ready02", "ks_ready03", "ks_ready10",
                       "ks_ready11", "ks_ready12", "ks_ready13", "va_ready", "mx_ready", "mh_ready", "ml_ready",
                       "mrow_ready", "st_ready", "exp_done", "pv_done", "acc_copied", "acc_used", "cxh_ready",
                       "cxl_ready")
        ks_ready = [[m.ks_ready00, m.ks_ready01, m.ks_ready02, m.ks_ready03],
                    [m.ks_ready10, m.ks_ready11, m.ks_ready12, m.ks_ready13]]
        ident = g.const[:, ID0:ID0 + P]
        NS = QUADS * CHUNKS
        DMA = 16

        def chunk(k):
            quad, r = divmod(k, CHUNKS)
            return quad, (4 * quad + r // QC if r < CHUNKS - 1 else None), r % QC

        def item(k):
            pair, r = divmod(k, ITEMS // 2)
            if r == ITEMS // 2 - 1:
                return pair // 2, 2 * pair, None, NJ - 1
            return pair // 2, 2 * pair + r // (T * QC), (r // QC) % T, r % QC

        def front_part(k):
            return ("x", 0) if k == 0 else ("q", 0) if k == 1 else (("t", "k", "v")[(k - 2) % 3], (k - 2) // 3)

        def slot_of(parts, what, k):
            return next(s for w, n, s in PLAN[parts][0] if (w, n) == (what, k))

        block = ctx.enter_context(nc.Block())

        @block.sync
        def _(sp):
            sp.dma_start(lnw[:, :], io["L0_xattn_ln_post_cross_w"].rearrange("(c p) -> p c", p=P),
                         allow_slow_non_contiguous=True).then_inc(m.w2_loaded, DMA)
            sp.dma_start(stage[:, :, 0:CH], io["L0_xattn_cq_w"].rearrange("(c p) n -> p c n", p=P)).then_inc(m.w2_loaded, DMA)
            sp.dma_start(stage[:, 0, CH:2 * CH], io["L0_xattn_ckv_w"][:, 0:CH]).then_inc(m.w2_loaded, DMA)
            sp.dma_start(stage[:, 1, CH:2 * CH], io["L0_xattn_ckv_w"][:, CH:2 * CH]).then_inc(m.w2_loaded, DMA)
            sp.dma_start(cx[:, :], io["L0_xattn_cdense_w"]).then_inc(m.w2_loaded, DMA)

            def one(f, n, b, parts, slot0, bank0):
                if not parts[0]:
                    return
                i, s = f.number, f.parity
                if parts != (1, 0, 0):
                    sp.wait_ge(m.va_ready, 4 * i)
                load_encoder(i)
                sp.wait_ge(m.work_free, slot0 + (slot_of(parts, "front", 1) + 4))
                if parts != (1, 0, 0):
                    sp.wait_ge(m.qm_ready, 4 * i)
                for blk, part in enumerate((qh, qh, ql)):
                    for quad in range(QUADS):
                        sp.dma_start(qb[32 * blk:32 * blk + 32, quad, :].bitcast(F32),
                                     part[32 * quad:32 * quad + 32, :].bitcast(F32)).then_inc(m.qb_ready, DMA)
                sp.wait_ge(m.work_free, slot0 + (slot_of(parts, "front", FRONT - 2) + 4))
                for quad in range(QUADS):
                    if parts[2]:
                        sp.wait_ge(m.exp_done, NS * b.number + (CHUNKS * (quad + 1) + 2))
                    for blk, part in enumerate((kh, kl, kh)):
                        sp.dma_start(ks[s][32 * blk:32 * blk + 32, quad, :].bitcast(F32),
                                     part[32 * quad:32 * quad + 32, :].bitcast(F32)).then_inc(ks_ready[s][quad], DMA)

            def load_encoder(i):
                src = io["ctx_1024"]
                if isinstance(i, int):
                    rows = src[i]
                else:
                    rows = src[bass.ds(i, 1)].rearrange("a l c -> (a l) c")
                sp.dma_start(enc[:, 0:KT - 1, :], rows[0:(KT - 1) * P, :].rearrange("(k p) c -> p k c", p=P)).then_inc(m.enc_loaded, DMA)
                sp.dma_start(enc[0:LAST, KT - 1, :], rows[(KT - 1) * P:LE, :]).then_inc(m.enc_loaded, DMA)

            iterations(sp, one)

        @block.gpsimd
        def _(pool):
            for s in range(2):
                nc.gpsimd.memset(va[s][:, :, :, :, :], 0.0).then_inc(m.v_zeroed, 1)
            pool.wait_ge(m.v_zeroed, 2)
            for s in range(2):
                for e in range(2):
                    nc.gpsimd.memset(va[s][:, :, :, e, 9 * e + 8], 1.0).then_inc(m.v_one, 1)
            pool.wait_ge(m.v_one, 4)

            def one(f, n, b, parts, slot0, bank0):
                if parts[0]:
                    pool.wait_ge(m.ssq_ready, 2 * f.number + 2)
                    nc.gpsimd.tensor_tensor(var[:, :], ssq[:, :], g.eps[:, :], ALU.add).then_inc(m.eps_added, 1)
                    pool.wait_ge(m.eps_added, f.number + 1)
                    nc.gpsimd.tensor_tensor(rstd[:, :], var[:, :], g.minus_half[:, :], ALU.pow).then_inc(m.rstd_ready, 1)
                masked = 0
                for what, k, slot in PLAN[parts][0]:
                    if what == "max" and k == 0:
                        pool.wait_ge(m.work_ready, slot0 + (slot + 1))
                        pool.wait_ge(m.work_free, slot0 + (slot + 3))
                        for e in range(2):
                            for k0, k1, rows in ((0, KT - 1, P), (KT - 1, KT, LAST)):
                                src = vraw[0:rows, k0:k1, :].rearrange("p k (q e d) -> p k q e d", e=2, d=CHD)[:, :, :, e, :]
                                nc.gpsimd.tensor_tensor(
                                    va[n.parity][0:rows, k0:k1, :, e, 9 * e:9 * e + CHD], src,
                                    g.zero[0:rows, 0:1].unsqueeze(2).unsqueeze(3).broadcast_to([rows, k1 - k0, NH // 2, CHD]),
                                    ALU.add).then_inc(m.va_ready, 1)
                    elif what in ("maxcol", "lastcol"):
                        of = n if what == "maxcol" else b
                        if what == "maxcol" or parts[1]:
                            pool.wait_ge(m.va_ready, 4 * n.number + 4)
                        pool.wait_ge(m.rstd_ready, f.number + 1 if parts[0] else B)
                        pool.wait_ge(m.qm_ready, 4 * f.number + masked if parts[0] else 4 * B)
                        pool.wait_ge(m.work_free, slot0 + (slot + 4))
                        nc.gpsimd.tensor_tensor(qm[of.parity][96:128, 4 * k:4 * k + 4, :],
                                                mt[96:128, :].unsqueeze(1).broadcast_to([32, 4, L]),
                                                g.const[96:128, MS0 + 4 * k:MS0 + 4 * k + 4].unsqueeze(2).broadcast_to([32, 4, L]),
                                                ALU.mult).then_inc(m.mrow_ready, 1)
                        pool.wait_ge(m.mrow_ready, 4 * of.number + (k + 1))
                    elif what == "front" and k == FRONT - 1 and not parts[2]:
                        for quad in range(QUADS):
                            mask_quad(f, b, parts, quad)
                        masked = QUADS
                    elif what == "scores" and parts[0] and k >= CHUNKS and k % CHUNKS == 2:
                        mask_quad(f, b, parts, k // CHUNKS - 1)
                        masked += 1
                if parts[0] and parts[2]:
                    mask_quad(f, b, parts, QUADS - 1)

            def mask_quad(f, b, parts, quad):
                pool.wait_ge(m.qb_ready, 12 * DMA * f.number + 12 * DMA)
                if parts[2]:
                    pool.wait_ge(m.exp_done, NS * b.number + (CHUNKS * (quad + 1) + 2))
                nc.gpsimd.tensor_tensor(qm[f.parity][0:96, 4 * quad:4 * quad + 4, :],
                                        qb[:, quad:quad + 1, :].bitcast(F32).broadcast_to([96, 4, L]),
                                        g.const[0:96, MC0:MC0 + 4].unsqueeze(2).broadcast_to([96, 4, L]),
                                        ALU.mult).then_inc(m.qm_ready, 1)

            iterations(pool, one)

        @block.scalar
        def _(act):
            act.wait_ge(m.w2_loaded, 5 * DMA)
            act.sem_inc(m.acc_copied, 1)
            act.sem_inc(m.exp_done, 2)

            def one(f, n, b, parts, slot0, bank0):
                if parts[0]:
                    for t in range(T):
                        nc.scalar.activation(xs[:, t, :], g.x[:, 2 * f.number + t, :], ACT.Square, scale=H ** -0.5,
                                             accum_out=ssq[:, t:t + 1]).then_inc(m.ssq_ready, 1)
                for what, k, slot in PLAN[parts][0]:
                    if what == "scores":
                        act.wait_ge(m.st_ready, NS * b.number + (k + 1))
                        act.wait_ge(m.pv_done, NS * b.number + (k + 1))
                        rows = P if chunk(k)[1] is not None else LAST
                        nc.scalar.activation(pr[0:rows, k % 4], st[0:rows, k % 2], ACT.Exp,
                                             scale=CHD ** -0.5).then_inc(m.exp_done, 1)
                    elif what == "values" and k % CHUNKS == CHUNKS - 1:
                        if k == CHUNKS - 1:
                            act.wait_ge(m.acc_used, b.number + 1)
                        act.wait_ge(m.pv_done, NS * b.number + (k + 5))
                        nc.scalar.activation(accs[:, k // CHUNKS, :, :], acc[:, :, :], ACT.Copy).then_inc(m.acc_copied, 1)
                    elif what == "front":
                        front(f, parts, *front_part(k), work[:, (bank0 + slot) % 3, :], slot0 + (slot + 1))
                    elif what == "sums" and k == 1:
                        act.wait_ge(m.work_free, slot0 + (slot + 4))
                        nc.scalar.activation(cxh[:, :], cx[:, :], ACT.Copy).then_inc(m.cxh_ready, 1)

            def front(f, parts, kind, j, src, ready):
                if kind == "v":
                    return
                act.wait_ge(m.work_ready, ready)
                w = chunk_cols(j)
                if kind == "x":
                    for c in range(C):
                        nc.scalar.activation(xh[:, c, :], src[:, c * L:(c + 1) * L], ACT.Copy,
                                             scale=lnw[:, c:c + 1]).then_inc(m.xh_ready, 1)
                elif kind == "q":
                    nc.scalar.activation(qh[:, :], src[:, 0:L], ACT.Copy).then_inc(m.qh_ready, 2)
                elif kind == "t":
                    nc.scalar.activation(eh[:, j % 2, 0:w], src[:, 0:w], ACT.Copy).then_inc(m.eh_ready, 1)
                else:
                    if j == 0 and parts != (1, 0, 0):
                        for quad in range(QUADS):
                            before = f.before if f.parity else f.before - 1
                            act.wait_ge(ks_ready[1 - f.parity][quad], 3 * DMA * (before + 1))
                    nc.scalar.activation(kh[:, 512 * j:512 * j + w], src[:, 0:w], ACT.Copy).then_inc(m.kh_ready, 1)

            iterations(act, one)

        @block.vector
        def _(dve):
            nc.vector.tensor_copy(mn[:, :, :], g.zero[:, 0:1].unsqueeze(2).broadcast_to([P, T, P])).then_inc(m.mn_zero, 1)
            nc.vector.memset(acc[:, :, :], 0.0).then_inc(m.acc_zero, 1)
            dve.wait_ge(m.w2_loaded, 5 * DMA)
            pieces = ((wq_hi[:, :, :], wq_lo[:, :, :], stage[:, :, 0:CH]), (wkv_hi[:, 0:CH], wkv_lo[:, 0:CH], stage[:, 0, CH:2 * CH]),
                      (wkv_hi[:, CH:2 * CH], wkv_lo[:, CH:2 * CH], stage[:, 1, CH:2 * CH]), (wd_hi[:, :], wd_lo[:, :], cx[:, :]))
            for hi, lo, src in pieces:
                split_hi(nc, hi, src).then_inc(m.w2_hi, 1)
            dve.wait_ge(m.w2_hi, 4)
            for hi, lo, src in pieces:
                split_lo(nc, lo, src, hi).then_inc(m.w2_lo, 1)
            dve.wait_ge(m.mn_zero, 1)
            dve.wait_ge(m.w2_lo, 4)
            dve.sem_inc(m.work_free, 3)

            def one(f, n, b, parts, slot0, bank0):
                for what, k, slot in PLAN[parts][0]:
                    if what == "norm":
                        dve.wait_ge(m.rstd_ready, f.number + 1)
                        for t in range(T):
                            nc.vector.tensor_scalar(xs[:, t, :], g.x[:, 2 * f.number + t, :], rstd[:, t:t + 1], None,
                                                    ALU.mult).then_inc(m.xs_ready, 1)
                    if slot is not None:
                        src = work[:, (bank0 + slot) % 3, :]
                    if what == "max":
                        quad, h, t, j = item(k)
                        dve.wait_ge(m.work_ready, slot0 + (slot + 1))
                        if t is None:
                            nc.vector.reduce_max(mp[:, :, h:h + 2, j].rearrange("p t h -> p h t"),
                                                 src[:, 0:2 * T * EVEN].rearrange("p (h t k) -> p h t k", h=2, t=T),
                                                 AX_X).then_inc(m.work_free, 1)
                        else:
                            nc.vector.reduce_max(mp[:, t, h, j:j + 1], src[:, :], AX_X).then_inc(m.work_free, 1)
                    elif what == "maxrow":
                        row_maxima(n, k, slot0, last_slot)
                    elif what in ("maxcol", "lastcol"):
                        of = n if what == "maxcol" else b
                        dve.wait_ge(m.work_ready, slot0 + (slot + 1))
                        if not (parts == (1, 1, 0) and k == 0):
                            dve.wait_ge(m.mrow_ready, 4 * of.number + k)
                        nc.vector.tensor_copy(mt[96:128, :], src[96:128, 0:L]).then_inc(m.work_free, 1)
                    elif what == "front":
                        front(f, n, parts, *front_part(k), src, slot0 + (slot + 1))
                    elif what == "sums" and k == 0:
                        dve.wait_ge(m.work_ready, slot0 + (slot + 1))
                        nc.vector.reciprocal(rden[:, :], src[:, 0:L]).then_inc(m.work_free, 1)
                    elif what == "sums":
                        dve.wait_ge(m.work_ready, slot0 + (slot + 1))
                        dve.wait_ge(m.work_free, slot0 + (slot + 3))
                        nc.vector.tensor_tensor(cx[:, :], src[:, 0:L], rden[:, :], ALU.mult).then_inc(m.work_free, 1)
                    elif what == "out":
                        if k == 0:
                            dve.wait_ge(m.cxh_ready, b.number + 1)
                            split_lo(nc, cxl[:, :], cx[:, :], cxh[:, :]).then_inc(m.cxl_ready, 1)
                        dve.wait_ge(m.work_ready, slot0 + (slot + 1))
                        xt = g.x[:, 2 * b.number + k, :]
                        nc.vector.tensor_tensor(xt, src[:, 0:H], xt, ALU.add).then_inc(m.work_free, 1)
                    if slot is not None:
                        last_slot = slot
                if parts == (1, 0, 0):
                    for rows in ks:
                        nc.vector.tensor_copy(rows[96:128, :, :],
                                              g.one[96:128, 0:1].unsqueeze(2).broadcast_to([32, QUADS, LE])).then_inc(m.key_ones, 1)

            def row_maxima(n, quad, slot0, last_slot):
                hs = slice(4 * quad, 4 * quad + 4)
                dve.wait_ge(m.work_free, slot0 + (last_slot + 4))
                nc.vector.reduce_max(mx[:, :, hs], mp[:, :, hs, :], AX_X).then_inc(m.mx_ready, 1)
                dve.wait_ge(m.mx_ready, 4 * n.number + (quad + 1))
                nc.vector.tensor_scalar(mn[:, :, 96 + 4 * quad:100 + 4 * quad], mx[:, :, hs], -1.0, None,
                                        ALU.mult).then_inc(m.mh_ready, 1)
                dve.wait_ge(m.mh_ready, 4 * n.number + (quad + 1))
                nc.vector.scalar_tensor_tensor(mn[:, :, 112 + 4 * quad:116 + 4 * quad], mx[:, :, hs], -1.0,
                                               mn[:, :, 96 + 4 * quad:100 + 4 * quad].bitcast(F32), ALU.mult,
                                               ALU.subtract).then_inc(m.ml_ready, 1)

            def front(f, n, parts, kind, j, src, ready):
                w = chunk_cols(j)
                if kind == "x":
                    dve.wait_ge(m.xh_ready, 2 * f.number + 2)
                    for c in range(C):
                        ins = nc.vector.scalar_tensor_tensor(xl[:, c, :], src[:, c * L:(c + 1) * L], lnw[:, c:c + 1],
                                                             xh[:, c, :].bitcast(F32), ALU.mult, ALU.subtract)
                        ins.then_inc(m.xl_ready if c == 0 else m.work_free, 1)
                elif kind == "q":
                    dve.wait_ge(m.qh_ready, 2 * f.number + 2)
                    nc.vector.tensor_tensor(ql[:, :], src[:, 0:L], qh[:, :].bitcast(F32), ALU.subtract).then_inc(m.work_free, 1)
                elif kind == "t":
                    dve.wait_ge(m.eh_ready, 4 * f.number + (j + 1))
                    nc.vector.tensor_tensor(el[:, j % 2, 0:w], src[:, 0:w], eh[:, j % 2, 0:w].bitcast(F32),
                                            ALU.subtract).then_inc(m.work_free, 1)
                elif kind == "k":
                    dve.wait_ge(m.kh_ready, 4 * f.number + (j + 1))
                    nc.vector.tensor_tensor(kl[:, 512 * j:512 * j + w], src[:, 0:w], kh[:, 512 * j:512 * j + w].bitcast(F32),
                                            ALU.subtract).then_inc(m.work_free, 1)
                else:
                    dve.wait_ge(m.work_ready, ready)
                    tiles = chunk_tiles(j)
                    rows = tile_rows(tiles[-1])
                    nc.vector.tensor_copy(vraw[0:rows, tiles[0]:tiles[-1] + 1, :],
                                          src[0:rows, 0:len(tiles) * CH].rearrange("p (k c) -> p k c", c=CH)).then_inc(m.work_free, 1)

            iterations(dve, one)

        @block.tensor
        def _(pe):
            pe.sem_inc(m.pv_done, 4)
            pe.sem_inc(m.acc_used, 1)
            pe.wait_ge(m.w2_lo, 4)
            pe.wait_ge(m.mn_zero, 1)
            pe.wait_ge(m.acc_zero, 1)
            pe.wait_ge(m.v_one, 4)

            def one(f, n, b, parts, slot0, bank0):
                for what, k, slot in PLAN[parts][0]:
                    if slot is not None:
                        dst = work[:, (bank0 + slot) % 3, :]
                        if what not in ("sums", "out", "maxcol", "lastcol") and what != "front":
                            pe.wait_ge(m.work_free, slot0 + (slot + 1))
                    if what == "max":
                        maxima(n, k, dst)
                    elif what in ("maxcol", "lastcol"):
                        pe.wait_ge(m.ml_ready, 4 * (n if what == "maxcol" else b).number + (k + 1))
                        pe.wait_ge(m.work_free, slot0 + (slot + 1))
                        for t in range(T):
                            last = nc.tensor.transpose(dst[:, t * P:(t + 1) * P], mn[:, t, :].bitcast(F32), ident)
                        last.then_inc(m.work_ready, 1)
                    elif what == "front":
                        before = slot_of(parts, "front", k - 1) if k else 0
                        front(f, *front_part(k), dst, slot0 + (slot + 1), slot0 + max(slot + 1, before + 4))
                    elif what == "scores":
                        scores(b, k)
                    elif what == "values":
                        values(b, k)
                    elif what == "sums":
                        if k == 0:
                            pe.wait_ge(m.acc_copied, 4 * b.number + 5)
                        pe.wait_ge(m.work_free, slot0 + (slot + 1))
                        for par in range(2):
                            for quad in range(QUADS):
                                e0 = EC0 + 64 * (1 - k) + 32 * par
                                last = nc.tensor.matmul(dst[32 * quad:32 * quad + 32, 0:L], g.const[:, e0:e0 + 32],
                                                        accs[:, quad, par, :], start=(par == 0), stop=(par == 1),
                                                        tile_position=(0, 32 * quad), skip_group_check=True)
                        last.then_inc(m.work_ready, 1)
                        if k == 1:
                            pe.wait_ge(m.work_ready, slot0 + (slot + 1))
                            pe.sem_inc(m.acc_used, 1)
                    elif what == "out":
                        if k == 0:
                            pe.wait_ge(m.cxl_ready, b.number + 1)
                        pe.wait_ge(m.work_free, slot0 + (slot + 1))
                        terms = three(((cxh[:, k * P:(k + 1) * P], cxl[:, k * P:(k + 1) * P]), (wd_hi[:, :], wd_lo[:, :])))
                        for i, (stat, mv) in enumerate(terms):
                            last = nc.tensor.matmul(dst[:, 0:H], stat, mv, start=(i == 0), stop=(i == 2))
                        last.then_inc(m.work_ready, 1)

            def maxima(n, k, dst):
                quad, h, t, j = item(k)
                if k % ITEMS == 0:
                    pe.wait_ge(m.qm_ready, 4 * n.number + (quad + 1))
                    pe.wait_ge(ks_ready[n.parity][quad], 3 * DMA * n.before + 3 * DMA)
                if t is None:
                    for i in range(2):
                        for t in range(T):
                            a = (i * T + t) * EVEN
                            last = nc.tensor.matmul(dst[:, a:a + EVEN], qm[n.parity][0:96, h + i, t * P:(t + 1) * P],
                                                    ks[n.parity][0:96, quad, LE - EVEN:LE], start=True, stop=True)
                else:
                    last = nc.tensor.matmul(dst[:, :], qm[n.parity][0:96, h, t * P:(t + 1) * P],
                                            ks[n.parity][0:96, quad, 512 * j:512 * j + 512], start=True, stop=True)
                last.then_inc(m.work_ready, 1)

            def scores(b, k):
                quad, h, j = chunk(k)
                if k == 0:
                    pe.wait_ge(m.key_ones, 2)
                if k % CHUNKS == 0:
                    pe.wait_ge(m.mrow_ready, 4 * b.number + (quad + 1))
                pe.wait_ge(m.exp_done, NS * b.number + (k + 1))
                for i in range(4):
                    kt, head, rows = (4 * j + i, h, P) if h is not None else (KT - 1, 4 * quad + i, LAST)
                    last = nc.tensor.matmul(st[0:rows, k % 2, i, :], ks[b.parity][:, quad, kt * P:kt * P + rows],
                                            qm[b.parity][:, head, :], start=True, stop=True)
                last.then_inc(m.st_ready, 1)

            def values(b, k):
                quad, h, j = chunk(k)
                if k == 0:
                    pe.wait_ge(m.va_ready, 4 * b.number + 4)
                if k % CHUNKS == 0:
                    pe.wait_ge(m.acc_copied, 4 * b.number + (quad + 1))
                pe.wait_ge(m.exp_done, NS * b.number + (k + 3))
                for i in range(4):
                    kt, head, rows = (4 * j + i, h, P) if h is not None else (KT - 1, 4 * quad + i, LAST)
                    local = head - 4 * quad
                    last = nc.tensor.matmul(acc[32 * i:32 * i + 18, local // 2, :],
                                            va[b.parity][0:rows, kt, head // 2, local % 2, :], pr[0:rows, k % 4, i, :],
                                            start=(k % CHUNKS == 0), stop=(h is None), tile_position=(0, 32 * i),
                                            skip_group_check=True)
                last.then_inc(m.pv_done, 1)

            def front(f, kind, j, dst, free, lo_ready):
                i = f.number
                tiles = chunk_tiles(j)
                w = chunk_cols(j)
                if kind == "x":
                    pe.wait_ge(m.xs_ready, 2 * i + 2)
                    pe.wait_ge(m.work_free, free)
                    for t in range(T):
                        for c in range(C):
                            last = nc.tensor.transpose(dst[:, c * L + t * P:c * L + t * P + P], xs[:, t, c * P:(c + 1) * P], ident)
                elif kind == "t":
                    if j == 0:
                        pe.wait_ge(m.enc_loaded, 2 * DMA * i + 2 * DMA)
                    pe.wait_ge(m.work_free, free)
                    for a, kt in enumerate(tiles):
                        rows = tile_rows(kt)
                        last = nc.tensor.transpose(dst[:, a * P:a * P + rows], enc[0:rows, kt, :], ident[0:rows, 0:rows])
                elif kind == "q":
                    pe.wait_ge(m.work_free, lo_ready)
                    terms = []
                    for c in range(C):
                        terms += three(((wq_hi[:, c, :], wq_lo[:, c, :]), (xh[:, c, :], xl[:, c, :])))
                    for a, (stat, mv) in enumerate(terms):
                        last = nc.tensor.matmul(dst[:, 0:L], stat, mv, start=(a == 0), stop=(a == len(terms) - 1))
                elif kind == "k":
                    pe.wait_ge(m.work_free, lo_ready)
                    w += w % 2
                    terms = three(((wkv_hi[:, 0:CH], wkv_lo[:, 0:CH]), (eh[:, j % 2, 0:w], el[:, j % 2, 0:w])))
                    for a, (stat, mv) in enumerate(terms):
                        last = nc.tensor.matmul(dst[:, 0:w], stat, mv, start=(a == 0), stop=(a == 2))
                else:
                    pe.wait_ge(m.work_free, free)
                    for a, kt in enumerate(tiles):
                        rows = tile_rows(kt)
                        terms = three(((eh[:, j % 2, a * P:a * P + rows], el[:, j % 2, a * P:a * P + rows]),
                                       (wkv_hi[:, CH:2 * CH], wkv_lo[:, CH:2 * CH])))
                        for c, (stat, mv) in enumerate(terms):
                            last = nc.tensor.matmul(dst[0:rows, a * CH:(a + 1) * CH], stat, mv, start=(c == 0), stop=(c == 2))
                last.then_inc(m.work_ready, 1)

            iterations(pe, one)



FT = 6
FW = (FF + FT - 1) // FT
RING3 = 5
SLOTS3 = FT + 2 + T


def ff_width(i):
    return min(FW, FF - FW * i)


def mlp(nc, g, io, loads, fw):
    with ExitStack() as ctx:
        sb, ps = allocator(nc, ctx)
        work = ps("work3", [P, RING3, 512])
        raw_gu = sb("w_gate_up", [P, 2, 2, C, FF])
        raw_d = sb("w_down", [P, FT, 2 * H])
        gu_hi = sb("w_gate_up_hi", [P, 2, 2, C, FF], F32R)
        gu_lo = sb("w_gate_up_lo", [P, 2, 2, C, FF], F32R)
        d_hi = sb("w_down_hi", [P, FT, 2 * H], F32R)
        d_lo = sb("w_down_lo", [P, FT, 2 * H], F32R)
        lnw = sb("ln_mlp_w", [P, C])
        sq = sb("squares3", [P, T, H])
        ssq = sb("mean_squares3", [P, T])
        var = sb("variance3", [P, T])
        rstd = sb("rstd3", [P, T])
        rex = sb("rstd_by_expert3", [P, 2, T])
        xe = sb("x_by_expert3", [P, 2, T, H])
        xh = sb("xt_hi3", [P, 2, C, L], F32R)
        xl = sb("xt_lo3", [P, 2, C, L], F32R)
        th = sb("tanh3", [P, 2, L])
        sg = sb("gated3", [P, 2, L])
        pa = sb("act3", [P, FT, L])
        ah = sb("act_hi3", [P, FT, L], F32R)
        al = sb("act_lo3", [P, FT, L], F32R)
        m = semaphores(nc, ctx, "ln_loaded", "gu_loaded", "d_loaded", "gu_hi_ready", "gu_hi_act", "gu_lo_ready",
                       "d_hi_ready", "d_lo_ready", "ssq_ready", "eps_added", "rstd_ready", "rex_ready", "xe_ready",
                       "xh_ready", "xl_ready", "work_ready", "work_free", "th_ready", "sg_ready", "ah_ready",
                       "al_ready", "res_v")
        ident = g.const[:, ID0:ID0 + P]
        FIRST = 2
        PIECES = [(slice(0, FW), slice(0, FT - 1)), (slice(0, ff_width(FT - 1)), slice(FT - 1, FT))]
        block = ctx.enter_context(nc.Block())

        width = ff_width

        def iterations(eng, one):
            with eng.Fori(0, B - 1) as b:
                one(b, True)
            one(B - 1, False)

        def slot(b, n):
            return SLOTS3 * b + (FIRST + n)

        def out_slot(t, ahead):
            return FT + (2 if ahead else 0) + t

        @block.sync
        def _(sp):
            sp.dma_start(lnw[:, :], io["L0_xattn_ln_post_attn_w"].rearrange("(c p) -> p c", p=P),
                         allow_slow_non_contiguous=True).then_inc(m.ln_loaded, 16)
            for e, x in enumerate("vl"):
                for u, name in enumerate(("gate", "up")):
                    sp.dma_start(raw_gu[:, e, u], io[f"L0_xattn_{x}_{name}"].rearrange("(c p) n -> p c n", p=P)).then_inc(m.gu_loaded, 16)
            for e, x in enumerate("vl"):
                wd = io[f"L0_xattn_{x}_down"]
                sp.dma_start(raw_d[0:FW, 0:FT - 1, e * H:(e + 1) * H],
                             wd[0:FW * (FT - 1), :].rearrange("(k p) n -> p k n", p=FW)).then_inc(m.d_loaded, 16)
                sp.dma_start(raw_d[0:width(FT - 1), FT - 1, e * H:(e + 1) * H], wd[FW * (FT - 1):FF, :]).then_inc(m.d_loaded, 16)
            sp.dma_start(fw.w_gate[:, :, :], io["L1_xattn_W_gate"].rearrange("(c p) n -> p c n", p=P)).then_inc(loads.w4, 16)
            sp.dma_start(fw.w_mem[:, :, :], io["L1_xattn_W_mem"].rearrange("(c p) n -> p c n", p=P)).then_inc(loads.w4, 16)
            sp.dma_start(fw.b_gate[:, :], io["L1_xattn_b_gate"].rearrange("(a n) -> a n", a=1).broadcast_to([P, H])).then_inc(loads.w4, 16)
            sp.dma_start(fw.norm_w[:, :], io["L1_xattn_norm_w"].rearrange("(a n) -> a n", a=1).broadcast_to([P, H])).then_inc(loads.w4, 16)
            rows = io["ctx_1024"][0]
            sp.dma_start(fw.enc0[:, 0:KT - 1, :], rows[0:(KT - 1) * P, :].rearrange("(k p) c -> p k c", p=P)).then_inc(loads.enc0, 16)
            sp.dma_start(fw.enc0[0:LAST, KT - 1, :], rows[(KT - 1) * P:LE, :]).then_inc(loads.enc0, 16)

        @block.gpsimd
        def _(pool):
            def norm(b):
                pool.wait_ge(m.ssq_ready, 2 * b + 2)
                nc.gpsimd.tensor_tensor(var[:, :], ssq[:, :], g.eps[:, :], ALU.add).then_inc(m.eps_added, 1)
                pool.wait_ge(m.eps_added, b + 1)
                nc.gpsimd.tensor_tensor(rstd[:, :], var[:, :], g.minus_half[:, :], ALU.pow).then_inc(m.rstd_ready, 1)

            norm(0)
            with pool.Fori(1, B) as b:
                norm(b)

        @block.scalar
        def _(act):
            def norm(b):
                for t in range(T):
                    nc.scalar.activation(sq[:, t, :], g.x[:, 2 * b + t, :], ACT.Square, scale=H ** -0.5,
                                         accum_out=ssq[:, t:t + 1]).then_inc(m.ssq_ready, 1)

            def inputs(b, slot0, bank0):
                for e in range(2):
                    act.wait_ge(m.work_ready, slot0 + (e + 1))
                    for c in range(C):
                        nc.scalar.activation(xh[:, e, c, :], work[:, (bank0 + e) % RING3, c * L:(c + 1) * L], ACT.Copy,
                                             scale=lnw[:, c:c + 1]).then_inc(m.xh_ready, 1)

            def hi(b, i):
                act.wait_ge(m.work_free, slot(b, i) + (1 + RING3))
                w = width(i)
                nc.scalar.activation(ah[0:w, i, :], pa[0:w, i, :], ACT.Copy, scale=0.5).then_inc(m.ah_ready, 1)

            def one(b, ahead):
                if ahead:
                    norm(b + 1)
                for i in range(FT):
                    w = width(i)
                    act.wait_ge(m.work_ready, slot(b, i) + 1)
                    if i >= 2:
                        act.wait_ge(m.sg_ready, FT * b + (i - 1))
                    nc.scalar.activation(th[0:w, i % 2, :], work[0:w, (FIRST + i) % RING3, 0:L], ACT.Tanh,
                                         scale=0.5).then_inc(m.th_ready, 1)
                    if i:
                        hi(b, i - 1)
                hi(b, FT - 1)
                if ahead:
                    inputs(b + 1, slot(b, FT), FIRST + FT)

            act.wait_ge(m.ln_loaded, 16)
            norm(0)
            act.wait_ge(m.gu_loaded, 64)
            nc.scalar.activation(gu_hi[:, 1], raw_gu[:, 1], ACT.Copy).then_inc(m.gu_hi_act, 1)
            inputs(0, 0, 0)
            act.wait_ge(m.d_loaded, 64)
            for r, k in PIECES:
                nc.scalar.activation(d_hi[r, k], raw_d[r, k], ACT.Copy).then_inc(m.d_hi_ready, 1)
            iterations(act, one)

        @block.vector
        def _(dve):
            def scaled(b):
                dve.wait_ge(m.rstd_ready, b + 1)
                nc.vector.tensor_tensor(rex[:, 0, :], rstd[:, :], g.vm[:, bass.ds(2 * b, 2)], ALU.mult).then_inc(m.rex_ready, 1)
                nc.vector.tensor_tensor(rex[:, 1, :], rstd[:, :], g.nvm[:, bass.ds(2 * b, 2)], ALU.mult).then_inc(m.rex_ready, 1)
                dve.wait_ge(m.rex_ready, 2 * b + 2)
                for e in range(2):
                    for t in range(T):
                        nc.vector.tensor_scalar(xe[:, e, t, :], g.x[:, 2 * b + t, :], rex[:, e, t:t + 1], None,
                                                ALU.mult).then_inc(m.xe_ready, 1)

            def inputs(b, bank0):
                for e in range(2):
                    dve.wait_ge(m.xh_ready, 4 * b + (2 * e + 2))
                    for c in range(C):
                        ins = nc.vector.scalar_tensor_tensor(xl[:, e, c, :], work[:, (bank0 + e) % RING3, c * L:(c + 1) * L],
                                                             lnw[:, c:c + 1], xh[:, e, c, :].bitcast(F32), ALU.mult, ALU.subtract)
                        ins.then_inc(m.xl_ready if c == 0 else m.work_free, 1)

            def lo(b, i):
                dve.wait_ge(m.ah_ready, FT * b + (i + 1))
                w = width(i)
                nc.vector.scalar_tensor_tensor(al[0:w, i, :], pa[0:w, i, :], 0.5, ah[0:w, i, :].bitcast(F32), ALU.mult,
                                               ALU.subtract).then_inc(m.al_ready, 1)

            def one(b, ahead):
                if ahead:
                    scaled(b + 1)
                for i in range(FT):
                    w = width(i)
                    src = work[0:w, (FIRST + i) % RING3, :]
                    dve.wait_ge(m.th_ready, FT * b + (i + 1))
                    nc.vector.scalar_tensor_tensor(sg[0:w, i % 2, :], th[0:w, i % 2, :], 1.0, src[:, 0:L], ALU.add,
                                                   ALU.mult).then_inc(m.sg_ready, 1)
                    dve.wait_ge(m.sg_ready, FT * b + (i + 1))
                    nc.vector.tensor_tensor(pa[0:w, i, :], src[:, L:2 * L], sg[0:w, i % 2, :], ALU.mult).then_inc(m.work_free, 1)
                    if i:
                        lo(b, i - 1)
                lo(b, FT - 1)
                if ahead:
                    inputs(b + 1, FIRST + FT)
                for t in range(T):
                    n = out_slot(t, ahead)
                    src = work[:, (FIRST + n) % RING3, :]
                    xt = g.x[:, 2 * b + t, :]
                    dve.wait_ge(m.work_ready, slot(b, n) + 1)
                    nc.vector.scalar_tensor_tensor(xt, src[:, 0:H], g.vm[:, bass.ds(2 * b + t, 1)], xt, ALU.mult,
                                                   ALU.add).then_inc(m.res_v, 1)
                    dve.wait_ge(m.res_v, 2 * b + (t + 1))
                    nc.vector.scalar_tensor_tensor(xt, src[:, H:2 * H], g.nvm[:, bass.ds(2 * b + t, 1)], xt, ALU.mult,
                                                   ALU.add).then_inc(m.work_free, 1)

            dve.sem_inc(m.work_free, RING3)
            dve.wait_ge(m.ln_loaded, 16)
            scaled(0)
            dve.wait_ge(m.gu_loaded, 64)
            split_hi(nc, gu_hi[:, 0], raw_gu[:, 0]).then_inc(m.gu_hi_ready, 1)
            for e, hi_ready in enumerate((m.gu_hi_ready, m.gu_hi_act)):
                dve.wait_ge(hi_ready, 1)
                split_lo(nc, gu_lo[:, e], raw_gu[:, e], gu_hi[:, e]).then_inc(m.gu_lo_ready, 1)
            inputs(0, 0)
            dve.wait_ge(m.d_hi_ready, 2)
            for r, k in PIECES:
                split_lo(nc, d_lo[r, k], raw_d[r, k], d_hi[r, k]).then_inc(m.d_lo_ready, 1)
            iterations(dve, one)

        @block.tensor
        def _(pe):
            def inputs(b, slot0, bank0):
                for e in range(2):
                    pe.wait_ge(m.xe_ready, 4 * b + (2 * e + 2))
                    pe.wait_ge(m.work_free, slot0 + (e + 1))
                    for t in range(T):
                        for c in range(C):
                            a = c * L + t * P
                            last = nc.tensor.transpose(work[:, (bank0 + e) % RING3, a:a + P], xe[:, e, t, c * P:(c + 1) * P], ident)
                    last.then_inc(m.work_ready, 1)

            def one(b, ahead):
                pe.wait_ge(m.xl_ready, 2 * b + 2)
                for i in range(FT):
                    w = width(i)
                    pe.wait_ge(m.work_free, slot(b, i) + 1)
                    if i == 0:
                        pe.wait_ge(m.work_free, SLOTS3 * b + RING3)
                    for u in range(2):
                        terms = []
                        for e in range(2):
                            for c in range(C):
                                terms += three(((gu_hi[:, e, u, c, FW * i:FW * i + w], gu_lo[:, e, u, c, FW * i:FW * i + w]),
                                                (xh[:, e, c, :], xl[:, e, c, :])))
                        for k, (stat, mv) in enumerate(terms):
                            last = nc.tensor.matmul(work[0:w, (FIRST + i) % RING3, u * L:(u + 1) * L], stat, mv,
                                                    start=(k == 0), stop=(k == len(terms) - 1))
                    last.then_inc(m.work_ready, 1)
                if ahead:
                    inputs(b + 1, slot(b, FT), FIRST + FT)
                pe.wait_ge(m.d_lo_ready, 2)
                pe.wait_ge(m.al_ready, FT * b + FT)
                for t in range(T):
                    n = out_slot(t, ahead)
                    pe.wait_ge(m.work_free, slot(b, n) + 1)
                    terms = []
                    for i in range(FT):
                        w = width(i)
                        for stat, mv in three(((ah[0:w, i, t * P:(t + 1) * P], al[0:w, i, t * P:(t + 1) * P]),
                                               (d_hi[0:w, i, :], d_lo[0:w, i, :]))):
                            terms.append((stat, mv))
                    for k, (stat, mv) in enumerate(terms):
                        last = nc.tensor.matmul(work[:, (FIRST + n) % RING3, :], stat, mv, start=(k == 0), stop=(k == len(terms) - 1))
                    last.then_inc(m.work_ready, 1)

            pe.wait_ge(m.xe_ready, 4)
            inputs(0, 0, 0)
            pe.wait_ge(m.gu_lo_ready, 2)
            pe.wait_ge(m.work_free, 2 + RING3)
            iterations(pe, one)



RING4 = 4


def plan4(front, attend, close):
    out, slots = [], 0

    def put(what, k=0, slot=True):
        nonlocal slots
        out.append((what, k, slots if slot else None))
        slots += slot

    if front:
        for c in range(C):
            put("x", c)
    if attend:
        put("gate", 0)
    if front:
        put("query", 0)
    if attend:
        put("scores", 0, False)
        put("gate", 1)
        put("scores", 1, False)
        for j in range(NJ):
            put("turn", j)
    if close:
        put("fuse", 0, False)
    if front:
        for j in range(NJ - 2):
            put("memory", j)
    if attend:
        for j in range(NJ, 2 * NJ):
            put("turn", j)
    if close:
        put("finish", 0, False)
    if attend:
        put("context", 0)
    if front:
        for j in range(NJ - 2, NJ):
            put("memory", j)
    if attend:
        for t in range(T):
            put("out", t)
    return out, slots


PLAN4 = {k: plan4(*k) for k in ((1, 0, 0), (1, 1, 0), (1, 1, 1), (0, 1, 1), (0, 0, 1))}


def iterations4(eng, one):
    first = 0

    def run(i, s, before, parts, slot0, bank0):
        one(Batch(i + 1, 1 - s, before + s), Batch(i, s, before), Batch(i - 1, 1 - s, before + s - 1), parts, slot0, bank0)

    run(-1, 1, -1, (1, 0, 0), 0, 0)
    first += PLAN4[1, 0, 0][1]
    run(0, 0, 0, (1, 1, 0), first, first % RING4)
    first += PLAN4[1, 1, 0][1]
    per = PLAN4[1, 1, 1][1]
    assert per % RING4 == 0
    with eng.Fori(0, B // 2 - 1) as pair:
        for s in range(2):
            run(2 * pair + (1 + s), 1 - s, pair + s, (1, 1, 1), (2 * per) * pair + (first + per * s), first % RING4)
    first += per * (B - 2)
    run(B - 1, 1, B // 2 - 1, (0, 1, 1), first, first % RING4)
    first += PLAN4[0, 1, 1][1]
    run(B, 0, B // 2, (0, 0, 1), first, first % RING4)


def fusion(nc, g, io, loads, fw):
    with ExitStack() as ctx:
        sb, ps = allocator(nc, ctx)
        work = ps("work4", [P, RING4, 512])
        st = ps("scores4", [P, NJ * 512])
        raw_m, raw_g, bg, nw = fw.w_mem, fw.w_gate, fw.b_gate, fw.norm_w
        m_hi = sb("w_mem_hi", [P, C, CH], F32R)
        m_lo = sb("w_mem_lo", [P, C, CH], F32R)
        gt = sb("w_gate_t", [P, 4, H])
        g_hi = sb("w_gate_t_hi", [P, C, H], F32R)
        g_lo = sb("w_gate_t_lo", [P, C, H], F32R)
        mc = sb("w_context", [P, 2 * H])
        mc_hi = sb("w_context_hi", [P, 2 * H], F32R)
        mc_lo = sb("w_context_lo", [P, 2 * H], F32R)
        xc = sb("x_of_batch", [P, T, H])
        enc = [fw.enc0, sb("memory_1", [P, KT, CH])]
        xh = [sb(f"xt_hi4_{s}", [P, C, L], F32R) for s in range(2)]
        xl = [sb(f"xt_lo4_{s}", [P, C, L], F32R) for s in range(2)]
        qh = [sb(f"queries_hi_{s}", [P, L], F32R) for s in range(2)]
        ql = [sb(f"queries_lo_{s}", [P, L], F32R) for s in range(2)]
        eh = sb("memory_t_hi", [P, LE + 1], F32R)
        el = sb("memory_t_lo", [P, LE + 1], F32R)
        mp = sb("max_parts4", [P, T, NJ])
        mx = sb("max4", [P, T])
        nm = sb("neg_max4", [P, T])
        pr = sb("probs4", [P, T, LE])
        sums = sb("prob_sum_parts4", [P, T, NJ])
        total = sb("prob_sums4", [P, T])
        rt = sb("reciprocal_sums4", [P, T])
        pt = sb("probs_t4", [P, KT, L])
        tth = sb("memory_mix_hi", [P, L], F32R)
        ttl = sb("memory_mix_lo", [P, L], F32R)
        cv = [sb(f"context_{s}", [P, T, H]) for s in range(2)]
        gp = sb("gate_part", [P, T, H])
        gs = [sb(f"gate_in_{s}", [P, T, H]) for s in range(2)]
        th = sb("tanh4", [P, T, H])
        fz = sb("gated_context", [P, T, H])
        fu = sb("fused", [P, T, H])
        sq = sb("squares4", [P, T, H])
        ssq = sb("mean_squares4", [P, T])
        var = sb("variance4", [P, T])
        rstd = sb("rstd4", [P, T])
        y = [sb(f"y_{s}", [P, T, H]) for s in range(2)]
        m = semaphores(nc, ctx, "pad_ready", "xc_ready", "gt_psum", "gt_ready", "m_psum", "mt_ready", "w4_hi",
                       "w4_lo", "enc_free", "xh_ready", "qh_ready", "eh_ready", "work_ready", "work_free",
                       "st_ready", "mp_ready", "mx_ready", "nm_ready", "exp_done", "total_ready", "rt_ready",
                       "tth_ready", "cv_ready", "th_ready", "fz_ready", "fu_ready", "ssq_ready", "eps_added",
                       "rstd_ready", "y_ready", "y_free", "stored")
        enc_loaded = [loads.enc0, loads.enc1]
        ident = g.const[:, ID0:ID0 + P]
        block = ctx.enter_context(nc.Block())

        def slot_of(parts, what, k):
            return next(s for w, n, s in PLAN4[parts][0] if (w, n) == (what, k))

        @block.sync
        def _(sp):
            def one(f, n, b, parts, slot0, bank0):
                if parts[0] and parts != (1, 0, 0):
                    if parts[2]:
                        sp.wait_ge(m.enc_free, 2 * f.number - 2)
                    src = io["ctx_1024"]
                    rows = src[f.number] if isinstance(f.number, int) else src[bass.ds(f.number, 1)].rearrange("a l c -> (a l) c")
                    dst, sem = enc[f.parity], enc_loaded[f.parity]
                    sp.dma_start(dst[:, 0:KT - 1, :], rows[0:(KT - 1) * P, :].rearrange("(k p) c -> p k c", p=P)).then_inc(sem, 16)
                    sp.dma_start(dst[0:LAST, KT - 1, :], rows[(KT - 1) * P:LE, :]).then_inc(sem, 16)
                if parts[2]:
                    sp.wait_ge(m.y_ready, 2 * b.number + 2)
                    out = io["out"]
                    dst = out[b.number] if isinstance(b.number, int) else out[bass.ds(b.number, 1)].rearrange("a l c -> (a l) c")
                    sp.dma_start(dst.rearrange("(t p) n -> p t n", p=P), y[b.parity][:, :, :]).then_inc(m.stored, 16)
                    sp.wait_ge(m.stored, 16 * b.number + 16)
                    sp.sem_inc(m.y_free, 1)

            sp.sem_inc(m.y_free, 2)
            iterations4(sp, one)

        @block.gpsimd
        def _(pool):
            def one(f, n, b, parts, slot0, bank0):
                for what, k, slot in PLAN4[parts][0]:
                    if what == "x" and k == 0:
                        if parts[1]:
                            pool.wait_ge(m.xh_ready, 2 * f.number)
                        nc.gpsimd.tensor_copy(xc[:, :, :], g.x[:, bass.ds(2 * f.number, 2), :]).then_inc(m.xc_ready, 1)
                    elif what == "finish":
                        pool.wait_ge(m.ssq_ready, 2 * b.number + 2)
                        nc.gpsimd.tensor_tensor(var[:, :], ssq[:, :], g.eps[:, :], ALU.add).then_inc(m.eps_added, 1)
                        pool.wait_ge(m.eps_added, b.number + 1)
                        nc.gpsimd.tensor_tensor(rstd[:, :], var[:, :], g.minus_half[:, :], ALU.pow).then_inc(m.rstd_ready, 1)

            iterations4(pool, one)

        @block.scalar
        def _(act):
            def one(f, n, b, parts, slot0, bank0):
                for what, k, slot in PLAN4[parts][0]:
                    if slot is not None:
                        src = work[:, (bank0 + slot) % RING4, :]
                    if what == "scores":
                        act.wait_ge(m.nm_ready, 2 * n.number + (k + 1))
                        for j in range(NJ):
                            js = slice(512 * j, 512 * j + chunk_cols(j))
                            nc.scalar.activation(pr[:, k, js], st[:, js], ACT.Exp, bias=nm[:, k:k + 1], scale=H ** -0.5,
                                                 accum_out=sums[:, k, j:j + 1]).then_inc(m.exp_done, 1)
                    elif what == "x":
                        act.wait_ge(m.work_ready, slot0 + (slot + 1))
                        nc.scalar.activation(xh[f.parity][:, k, :], src[:, 0:L], ACT.Copy).then_inc(m.xh_ready, 1)
                    elif what == "query":
                        act.wait_ge(m.work_ready, slot0 + (slot + 1))
                        nc.scalar.activation(qh[f.parity][:, :], src[:, 0:L], ACT.Copy).then_inc(m.qh_ready, 1)
                    elif what == "memory":
                        act.wait_ge(m.work_ready, slot0 + (slot + 1))
                        w = chunk_cols(k)
                        nc.scalar.activation(eh[:, 512 * k:512 * k + w], src[:, 0:w], ACT.Copy).then_inc(m.eh_ready, 1)
                    elif what == "context":
                        act.wait_ge(m.work_ready, slot0 + (slot + 1))
                        nc.scalar.activation(tth[:, :], src[:, 0:L], ACT.Copy).then_inc(m.tth_ready, 1)
                    elif what == "fuse":
                        act.wait_ge(m.work_free, slot0 + RING4)
                        for t in range(T):
                            nc.scalar.activation(th[:, t, :], gs[b.parity][:, t, :], ACT.Tanh, scale=0.5).then_inc(m.th_ready, 1)
                    elif what == "finish":
                        act.wait_ge(m.fu_ready, 2 * b.number + 2)
                        for t in range(T):
                            nc.scalar.activation(sq[:, t, :], fu[:, t, :], ACT.Square, scale=H ** -0.5,
                                                 accum_out=ssq[:, t:t + 1]).then_inc(m.ssq_ready, 1)

            iterations4(act, one)

        @block.vector
        def _(dve):
            dve.sem_inc(m.work_free, RING4)
            for x in (eh, el):
                nc.vector.tensor_copy(x[:, LE:LE + 1], g.zero[:, :]).then_inc(m.pad_ready, 1)
            dve.wait_ge(m.gt_psum, 4)
            nc.vector.tensor_copy(gt[:, :, :], st[:, 0:4 * H].rearrange("p (k n) -> p k n", k=4)).then_inc(m.gt_ready, 1)
            dve.wait_ge(m.m_psum, 1)
            nc.vector.tensor_copy(mc[:, 0:H], st[:, 2 * 512:2 * 512 + H]).then_inc(m.mt_ready, 1)
            dve.wait_ge(m.m_psum, 2)
            nc.vector.tensor_copy(mc[:, H:2 * H], st[:, 3 * 512:3 * 512 + H]).then_inc(m.mt_ready, 1)
            dve.wait_ge(m.mt_ready, 2)
            pieces = ((m_hi[:, :, :], m_lo[:, :, :], raw_m[:, :, :]), (g_hi[:, :, :], g_lo[:, :, :], gt[:, 0:C, :]),
                      (mc_hi[:, :], mc_lo[:, :], mc[:, :]))
            for hi, lo, src in pieces:
                split_hi(nc, hi, src).then_inc(m.w4_hi, 1)
            dve.wait_ge(m.w4_hi, 3)
            for hi, lo, src in pieces:
                split_lo(nc, lo, src, hi).then_inc(m.w4_lo, 1)

            def one(f, n, b, parts, slot0, bank0):
                for what, k, slot in PLAN4[parts][0]:
                    if slot is not None:
                        src = work[:, (bank0 + slot) % RING4, :]
                        if what not in ("x", "query", "memory", "context"):
                            dve.wait_ge(m.work_ready, slot0 + (slot + 1))
                    if what == "scores":
                        for j in range(NJ):
                            dve.wait_ge(m.st_ready, 2 * NJ * n.number + (NJ * k + j + 1))
                            nc.vector.reduce_max(mp[:, k, j:j + 1], st[:, 512 * j:512 * j + chunk_cols(j)],
                                                 AX_X).then_inc(m.mp_ready, 1)
                        dve.wait_ge(m.mp_ready, 2 * NJ * n.number + NJ * (k + 1))
                        nc.vector.reduce_max(mx[:, k:k + 1], mp[:, k, :], AX_X).then_inc(m.mx_ready, 1)
                        dve.wait_ge(m.mx_ready, 2 * n.number + (k + 1))
                        nc.vector.tensor_scalar(nm[:, k:k + 1], mx[:, k:k + 1], -(H ** -0.5), None, ALU.mult).then_inc(m.nm_ready, 1)
                    elif what == "x":
                        dve.wait_ge(m.xh_ready, 2 * f.number + (k + 1))
                        nc.vector.tensor_tensor(xl[f.parity][:, k, :], src[:, 0:L], xh[f.parity][:, k, :].bitcast(F32),
                                                ALU.subtract).then_inc(m.work_free, 1)
                    elif what == "query":
                        dve.wait_ge(m.qh_ready, f.number + 1)
                        nc.vector.tensor_tensor(ql[f.parity][:, :], src[:, 0:L], qh[f.parity][:, :].bitcast(F32),
                                                ALU.subtract).then_inc(m.work_free, 1)
                    elif what == "memory":
                        w = chunk_cols(k)
                        dve.wait_ge(m.eh_ready, NJ * f.number + (k + 1))
                        nc.vector.tensor_tensor(el[:, 512 * k:512 * k + w], src[:, 0:w], eh[:, 512 * k:512 * k + w].bitcast(F32),
                                                ALU.subtract).then_inc(m.work_free, 1)
                    elif what == "turn":
                        t, j = divmod(k, NJ)
                        tiles = chunk_tiles(j)
                        rows = tile_rows(tiles[-1])
                        nc.vector.tensor_copy(pt[0:rows, tiles[0]:tiles[-1] + 1, t * P:(t + 1) * P],
                                              src[0:rows, 0:len(tiles) * P].rearrange("p (k q) -> p k q", q=P)).then_inc(m.work_free, 1)
                    elif what == "context":
                        dve.wait_ge(m.exp_done, 2 * NJ * n.number + 2 * NJ)
                        nc.vector.reduce_sum(total[:, :], sums[:, :, :], AX_X).then_inc(m.total_ready, 1)
                        dve.wait_ge(m.total_ready, n.number + 1)
                        nc.vector.reciprocal(rt[:, :], total[:, :]).then_inc(m.rt_ready, 1)
                        dve.wait_ge(m.tth_ready, n.number + 1)
                        nc.vector.tensor_tensor(ttl[:, :], src[:, 0:L], tth[:, :].bitcast(F32), ALU.subtract).then_inc(m.work_free, 1)
                    elif what == "out":
                        dve.wait_ge(m.rt_ready, n.number + 1)
                        nc.vector.tensor_scalar(cv[n.parity][:, k, :], src[:, 0:H], rt[:, k:k + 1], None, ALU.mult).then_inc(m.cv_ready, 1)
                        dve.wait_ge(m.work_free, slot0 + (slot_of(parts, "gate", k) + 1 + RING4))
                        nc.vector.scalar_tensor_tensor(gs[n.parity][:, k, :], src[:, H:2 * H], rt[:, k:k + 1], gp[:, k, :],
                                                       ALU.mult, ALU.add).then_inc(m.work_free, 1)
                    elif what == "gate":
                        if k == 0:
                            dve.wait_ge(m.work_free, slot0 + RING4)
                        nc.vector.tensor_tensor(gp[:, k, :], src[:, 0:H], bg[:, :], ALU.add).then_inc(m.work_free, 1)
                    elif what == "fuse":
                        dve.wait_ge(m.th_ready, 2 * b.number + 2)
                        for t in range(T):
                            nc.vector.scalar_tensor_tensor(fz[:, t, :], th[:, t, :], 1.0, cv[b.parity][:, t, :], ALU.add,
                                                           ALU.mult).then_inc(m.fz_ready, 1)
                        dve.wait_ge(m.fz_ready, 2 * b.number + 2)
                        for t in range(T):
                            nc.vector.scalar_tensor_tensor(fu[:, t, :], fz[:, t, :], 0.5, g.x[:, 2 * b.number + t, :], ALU.mult,
                                                           ALU.add).then_inc(m.fu_ready, 1)
                    elif what == "finish":
                        dve.wait_ge(m.rstd_ready, b.number + 1)
                        dve.wait_ge(m.y_free, b.number + 1)
                        for t in range(T):
                            nc.vector.scalar_tensor_tensor(y[b.parity][:, t, :], fu[:, t, :], rstd[:, t:t + 1], nw[:, :], ALU.mult,
                                                           ALU.mult).then_inc(m.y_ready, 1)

            iterations4(dve, one)

        @block.tensor
        def _(pe):
            pe.wait_ge(loads.w4, 64)
            for f in range(4):
                for o in range(C):
                    last = nc.tensor.transpose(st[:, f * H + o * P:f * H + o * P + P], raw_g[:, o, f * P:(f + 1) * P], ident)
                last.then_inc(m.gt_psum, 1)
            for c in range(C):
                last = nc.tensor.transpose(st[:, 2 * 512 + c * P:2 * 512 + c * P + P], raw_m[:, c, :], ident)
            last.then_inc(m.m_psum, 1)
            pe.wait_ge(m.gt_ready, 1)
            for c in range(C):
                last = nc.tensor.matmul(st[:, 3 * 512:3 * 512 + H], raw_m[:, c, :], gt[:, C + c, :], start=(c == 0), stop=(c == C - 1))
            last.then_inc(m.m_psum, 1)
            pe.wait_ge(m.w4_lo, 3)
            pe.wait_ge(m.pad_ready, 2)

            def product(dst, terms):
                for i, (stat, mv) in enumerate(terms):
                    last = nc.tensor.matmul(dst, stat, mv, start=(i == 0), stop=(i == len(terms) - 1))
                return last

            def one(f, n, b, parts, slot0, bank0):
                for what, k, slot in PLAN4[parts][0]:
                    if slot is not None:
                        dst = work[:, (bank0 + slot) % RING4, :]
                    if what == "scores":
                        if k == 0:
                            pe.wait_ge(m.work_free, slot0 + before_attend(parts))
                            if parts != (1, 1, 0):
                                pe.wait_ge(m.exp_done, 2 * NJ * n.number)
                        q = slice(k * P, (k + 1) * P)
                        for j in range(NJ):
                            if k:
                                pe.wait_ge(m.exp_done, 2 * NJ * n.number + (j + 1))
                            w = chunk_cols(j) + chunk_cols(j) % 2
                            product(st[:, 512 * j:512 * j + w],
                                           three(((qh[n.parity][:, q], ql[n.parity][:, q]),
                                                  (eh[:, 512 * j:512 * j + w], el[:, 512 * j:512 * j + w])))).then_inc(m.st_ready, 1)
                    elif what == "x":
                        pe.wait_ge(m.xc_ready, f.number + 1)
                        pe.wait_ge(m.work_free, slot0 + (slot + 1))
                        for t in range(T):
                            last = nc.tensor.transpose(dst[:, t * P:(t + 1) * P], xc[:, t, k * P:(k + 1) * P], ident)
                        last.then_inc(m.work_ready, 1)
                    elif what == "query":
                        pe.wait_ge(m.work_free, slot0 + max(slot + 1, slot_of(parts, "x", 1) + 1 + RING4))
                        terms = []
                        for c in range(C):
                            terms += three(((m_hi[:, c, :], m_lo[:, c, :]), (xh[f.parity][:, c, :], xl[f.parity][:, c, :])))
                        product(dst[:, 0:L], terms).then_inc(m.work_ready, 1)
                    elif what == "memory":
                        if k == 0:
                            pe.wait_ge(enc_loaded[f.parity], 32 * f.before + 32)
                        pe.wait_ge(m.work_free, slot0 + (slot + 1))
                        for a, kt in enumerate(chunk_tiles(k)):
                            rows = tile_rows(kt)
                            last = nc.tensor.transpose(dst[:, a * P:a * P + rows], enc[f.parity][0:rows, kt, :], ident[0:rows, 0:rows])
                        last.then_inc(m.work_ready, 1)
                    elif what == "turn":
                        t, j = divmod(k, NJ)
                        pe.wait_ge(m.exp_done, 2 * NJ * n.number + (k + 1))
                        pe.wait_ge(m.work_free, slot0 + (slot + 1))
                        for a, kt in enumerate(chunk_tiles(j)):
                            rows = tile_rows(kt)
                            last = nc.tensor.transpose(dst[0:rows, a * P:(a + 1) * P], pr[:, t, kt * P:kt * P + rows], ident)
                        last.then_inc(m.work_ready, 1)
                    elif what == "context":
                        pe.wait_ge(m.work_free, slot0 + (slot + RING4))
                        for kt in range(KT):
                            rows = tile_rows(kt)
                            last = nc.tensor.matmul(dst[:, 0:L], enc[n.parity][0:rows, kt, :], pt[0:rows, kt, :],
                                                    start=(kt == 0), stop=(kt == KT - 1))
                        last.then_inc(m.work_ready, 1)
                        pe.wait_ge(m.work_ready, slot0 + (slot + 1))
                        pe.sem_inc(m.enc_free, 2)
                    elif what == "out":
                        q = slice(k * P, (k + 1) * P)
                        pe.wait_ge(m.work_free, slot0 + max(slot + 1, slot_of(parts, "context", 0) + 1 + RING4))
                        product(dst, three(((tth[:, q], ttl[:, q]), (mc_hi[:, :], mc_lo[:, :])))).then_inc(m.work_ready, 1)
                    elif what == "gate":
                        q = slice(k * P, (k + 1) * P)
                        pe.wait_ge(m.work_free, slot0 + (slot + 1))
                        terms = []
                        for c in range(C):
                            terms += three(((xh[n.parity][:, c, q], xl[n.parity][:, c, q]), (g_hi[:, c, :], g_lo[:, c, :])))
                        product(dst[:, 0:H], terms).then_inc(m.work_ready, 1)

            def before_attend(parts):
                return RING4 if parts == (1, 1, 0) else RING4 - T

            iterations4(pe, one)


def build(nc, io):
    with ExitStack() as ctx:
        sb, _ = allocator(nc, ctx)
        shared = namedtuple("Shared", "const x tok tok_next vm nvm minus_half eps zero one")
        g = shared(
            const=sb("const", [P, NCONST]),
            x=sb("x", [P, B * T, H]),
            tok=sb("tok", [P, B * T], I32),
            tok_next=sb("tok_next", [P, B * T], I32),
            vm=sb("vm", [P, B * T]),
            nvm=sb("nvm", [P, B * T]),
            minus_half=sb("minus_half", [P, T]),
            eps=sb("eps", [P, T]),
            zero=sb("zero", [P, 1]),
            one=sb("one", [P, 1]),
        )
        self_attention(nc, g, io)
        cross_attention(nc, g, io)
        with ExitStack() as rest:
            sb, _ = allocator(nc, rest)
            loads = semaphores(nc, rest, "w4", "enc0", "enc1")
            fw = namedtuple("FusionWeights", "w_mem w_gate b_gate norm_w enc0")(
                w_mem=sb("w_mem", [P, C, CH]), w_gate=sb("w_gate", [P, C, 2 * H]), b_gate=sb("b_gate", [P, H]),
                norm_w=sb("norm_w", [P, H]), enc0=sb("memory_0", [P, KT, CH]))
            mlp(nc, g, io, loads, fw)
            fusion(nc, g, io, loads, fw)


_INS = ["x", "ctx_1024", "pos_1xS", "mask_BxS_ik0", "L0_xattn_ln_in_w", "L0_xattn_ln_post_attn_w",
        "L0_xattn_ln_post_cross_w", "L0_xattn_v_qkv", "L0_xattn_l_qkv", "L0_xattn_v_dense", "L0_xattn_l_dense",
        "L0_xattn_cq_w", "L0_xattn_ckv_w", "L0_xattn_cdense_w", "L0_xattn_v_gate", "L0_xattn_v_up", "L0_xattn_v_down",
        "L0_xattn_l_gate", "L0_xattn_l_up", "L0_xattn_l_down", "L1_xattn_W_mem", "L1_xattn_W_gate",
        "L1_xattn_b_gate", "L1_xattn_norm_w"]


def kernel(**inputs):
    import concourse.bacc as _bacc
    from concourse.bass_utils import run_bass_kernel_spmd as _run

    nc = _bacc.Bacc("TRN2", target_bir_lowering=False, num_devices=1)
    arrays, io = {}, {}
    for name in _INS:
        a = np.ascontiguousarray(inputs[name])
        arrays[f"in_{name}"] = a
        io[name] = nc.dram_tensor(f"in_{name}", a.shape, mybir.dt.from_np(a.dtype), kind="ExternalInput").ap()
    arrays["in_constants"] = constants()
    io["const"] = nc.dram_tensor("in_constants", (P, NCONST), F32, kind="ExternalInput").ap()
    io["out"] = nc.dram_tensor("out_0", (B, L, H), F32, kind="ExternalOutput").ap()
    build(nc, io)
    r = _run(nc, [arrays], core_ids=[0])
    return r.results[0]["out_0"]
```
